# Optimizing a Trainium2 kernel written in Bass

```python
import numpy as np
import jax
import jax.numpy as jnp

def _softmax(x, axis=-1):
    return jax.nn.softmax(x, axis=axis)

def _gelu(x):
    return jax.nn.gelu(x, approximate=True)

def _silu(x):
    return jax.nn.silu(x)

def _sigmoid(x):
    return jax.nn.sigmoid(x)

def _layernorm(x, axis=-1, eps=1e-05):
    m = jnp.mean(x, axis=axis, keepdims=True)
    v = jnp.var(x, axis=axis, keepdims=True)
    return (x - m) / jnp.sqrt(v + eps)

def _scatter_add(tgt, idx, src, axis=0):
    return tgt.at[idx].add(src)

def _segment_sum(src, seg, n):
    return jax.ops.segment_sum(src, seg, n)
kernel_name = 'mk_seq_postln_d2_jaxref_r8_d93e1b'

def setup_inputs(seed: int=0):
    np.random.seed(seed)
    _w = jnp.asarray

    def _L0_attn_setup():
        import jax, jax.numpy as jnp
        import numpy as np
        H = 16
        D_NOPE = 128
        D_ROPE = 64
        D_QK = 192
        D_V = 128
        THETA = 10000.0
        EPS = 1e-06

        def rmsnorm(x, w):
            x32 = x.astype(jnp.float32)
            x32 = x32 * jax.lax.rsqrt(jnp.mean(x32 * x32, axis=-1, keepdims=True) + EPS)
            return (x32 * w).astype(x.dtype)

        def rope_cos_sin(seq_len, dim, dtype):
            inv_freq = 1.0 / THETA ** (jnp.arange(0, dim, 2, dtype=jnp.float32) / dim)
            t = jnp.arange(seq_len, dtype=jnp.float32)
            freqs = jnp.outer(t, inv_freq)
            return (jnp.cos(freqs).astype(dtype), jnp.sin(freqs).astype(dtype))

        def apply_rope(x, cos, sin):
            d2 = x.shape[-1] // 2
            x1, x2 = (x[..., :d2], x[..., d2:])
            c = cos[None, :, None, :]
            s = sin[None, :, None, :]
            return jnp.concatenate([x1 * c - x2 * s, x2 * c + x1 * s], axis=-1)
        key = jax.random.key(seed)
        ks = jax.random.split(key, 8)
        B, T, D = (2, 256, 256)
        q_lora, kv_lora = (192, 64)

        def w(k, fan_in, fan_out):
            return jax.random.normal(k, (fan_in, fan_out), dtype=jnp.float32) * (1.0 / np.sqrt(fan_in))
        return {'hidden_states': jax.random.normal(ks[0], (B, T, D), dtype=jnp.float32), 'Wq_a': w(ks[1], D, q_lora), 'q_norm_w': jnp.ones((q_lora,), dtype=jnp.float32), 'Wq_b': w(ks[2], q_lora, H * D_QK), 'Wk_rope': w(ks[3], D, D_ROPE), 'Wkv_a': w(ks[4], D, kv_lora), 'kv_norm_w': jnp.ones((kv_lora,), dtype=jnp.float32), 'Wkv_b': w(ks[5], kv_lora, H * (D_NOPE + D_V)), 'Wo': w(ks[6], H * D_V, D)}
    _L0_attn_in = _L0_attn_setup()

    def _L0_ffn_setup():
        import jax, jax.numpy as jnp
        import numpy as np
        B, S, H, E, I, TOPK = (1, 128, 256, 16, 128, 2)
        SCALE = 1.0
        key = jax.random.key(seed)
        k0, k1, k2, k3 = jax.random.split(key, 4)
        hidden_states = jax.random.normal(k0, (B, S, H), dtype=jnp.float32)
        gate_w = jax.random.normal(k1, (E, H), dtype=jnp.float32) * 0.02
        gate_up_proj = jax.random.normal(k2, (E, H, 2 * I), dtype=jnp.float32) / np.sqrt(H)
        down_proj = jax.random.normal(k3, (E, I, H), dtype=jnp.float32) / np.sqrt(I)
        return {'hidden_states': hidden_states, 'gate_w': gate_w, 'gate_up_proj': gate_up_proj, 'down_proj': down_proj}
    _L0_ffn_in = _L0_ffn_setup()

    def _L1_attn_setup():
        import jax, jax.numpy as jnp
        import numpy as np
        import math
        B, T, D = (2, 256, 256)
        H, G, DQ, DV = (16, 4, 128, 128)
        REP = H // G
        ROPE_THETA = 10000.0

        def _rope(x):
            t = x.shape[2]
            inv_freq = 1.0 / ROPE_THETA ** (jnp.arange(0, DQ, 2, dtype=jnp.float32) / DQ)
            freqs = jnp.arange(t, dtype=jnp.float32)[:, None] * inv_freq[None, :]
            freqs = jnp.repeat(freqs, 2, axis=-1)
            cos, sin = (jnp.cos(freqs), jnp.sin(freqs))
            x2 = x.reshape(*x.shape[:-1], DQ // 2, 2)
            rot = jnp.stack([-x2[..., 1], x2[..., 0]], axis=-1).reshape(x.shape)
            return x * cos + rot * sin

        def _alibi(t):
            slopes = 2.0 ** (-jnp.arange(1, H + 1, dtype=jnp.float32) * 8.0 / H)
            pos = jnp.arange(t, dtype=jnp.float32)
            diff = jnp.abs(pos[:, None] - pos[None, :])
            return -diff[None, :, :] * slopes[:, None, None]
        key = jax.random.key(seed)
        ks = jax.random.split(key, 5)
        s = 0.02
        return {'hidden_states': jax.random.normal(ks[0], (B, T, D), jnp.float32), 'Wq': jax.random.normal(ks[1], (D, H * DQ), jnp.float32) * s, 'Wk': jax.random.normal(ks[2], (D, G * DQ), jnp.float32) * s, 'Wv': jax.random.normal(ks[3], (D, G * DV), jnp.float32) * s, 'Wo': jax.random.normal(ks[4], (H * DV, D), jnp.float32) * s, 'bo': jnp.zeros((D,), jnp.float32)}
    _L1_attn_in = _L1_attn_setup()

    def _L1_ffn_setup():
        import jax, jax.numpy as jnp
        import numpy as np

        def binarize_weight(w):
            alpha = jnp.mean(jnp.abs(w), axis=tuple(range(1, w.ndim)), keepdims=True)
            bw = jnp.where(w >= 0, 1.0, -1.0) * alpha
            return jax.lax.stop_gradient(bw - w) + w
        key = jax.random.key(seed)
        k1, k2, k3 = jax.random.split(key, 3)
        in_features, out_features = (256, 256)
        x = jax.random.normal(k1, (8, 256, in_features), dtype=jnp.float32)
        std = np.sqrt(2.0 / out_features).astype(np.float32)
        weight = jax.random.normal(k2, (out_features, in_features), dtype=jnp.float32) * std
        bias = jax.random.normal(k3, (out_features,), dtype=jnp.float32) * 0.01
        return {'x': x, 'weight': weight, 'bias': bias}
    _L1_ffn_in = _L1_ffn_setup()
    _d = {'L0_attn_hidden_states': _L0_attn_in['hidden_states'], 'L0_attn_Wq_a': _L0_attn_in['Wq_a'], 'L0_attn_q_norm_w': _L0_attn_in['q_norm_w'], 'L0_attn_Wq_b': _L0_attn_in['Wq_b'], 'L0_attn_Wk_rope': _L0_attn_in['Wk_rope'], 'L0_attn_Wkv_a': _L0_attn_in['Wkv_a'], 'L0_attn_kv_norm_w': _L0_attn_in['kv_norm_w'], 'L0_attn_Wkv_b': _L0_attn_in['Wkv_b'], 'L0_attn_Wo': _L0_attn_in['Wo'], 'L0_ffn_gate_w': _L0_ffn_in['gate_w'], 'L0_ffn_gate_up_proj': _L0_ffn_in['gate_up_proj'], 'L0_ffn_down_proj': _L0_ffn_in['down_proj'], 'L1_attn_Wq': _L1_attn_in['Wq'], 'L1_attn_Wk': _L1_attn_in['Wk'], 'L1_attn_Wv': _L1_attn_in['Wv'], 'L1_attn_Wo': _L1_attn_in['Wo'], 'L1_attn_bo': _L1_attn_in['bo'], 'L1_ffn_weight': _L1_ffn_in['weight'], 'L1_ffn_bias': _L1_ffn_in['bias']}
    _x0 = _d['L0_attn_hidden_states']
    _d['L0_attn_hidden_states'] = jax.random.normal(jax.random.fold_in(jax.random.key(seed), 1), (4, 256, 256), dtype=_x0.dtype)
    del _x0
    return _d

def reference(L0_attn_hidden_states, L0_attn_Wq_a, L0_attn_q_norm_w, L0_attn_Wq_b, L0_attn_Wk_rope, L0_attn_Wkv_a, L0_attn_kv_norm_w, L0_attn_Wkv_b, L0_attn_Wo, L0_ffn_gate_w, L0_ffn_gate_up_proj, L0_ffn_down_proj, L1_attn_Wq, L1_attn_Wk, L1_attn_Wv, L1_attn_Wo, L1_attn_bo, L1_ffn_weight, L1_ffn_bias):

    def _L0_attn_ref(hidden_states, Wq_a, q_norm_w, Wq_b, Wk_rope, Wkv_a, kv_norm_w, Wkv_b, Wo):
        import jax, jax.numpy as jnp
        import numpy as np
        H = 16
        D_NOPE = 128
        D_ROPE = 64
        D_QK = 192
        D_V = 128
        THETA = 10000.0
        EPS = 1e-06

        def rmsnorm(x, w):
            x32 = x.astype(jnp.float32)
            x32 = x32 * jax.lax.rsqrt(jnp.mean(x32 * x32, axis=-1, keepdims=True) + EPS)
            return (x32 * w).astype(x.dtype)

        def rope_cos_sin(seq_len, dim, dtype):
            inv_freq = 1.0 / THETA ** (jnp.arange(0, dim, 2, dtype=jnp.float32) / dim)
            t = jnp.arange(seq_len, dtype=jnp.float32)
            freqs = jnp.outer(t, inv_freq)
            return (jnp.cos(freqs).astype(dtype), jnp.sin(freqs).astype(dtype))

        def apply_rope(x, cos, sin):
            d2 = x.shape[-1] // 2
            x1, x2 = (x[..., :d2], x[..., d2:])
            c = cos[None, :, None, :]
            s = sin[None, :, None, :]
            return jnp.concatenate([x1 * c - x2 * s, x2 * c + x1 * s], axis=-1)
        B, T, D = hidden_states.shape
        q = rmsnorm(hidden_states @ Wq_a, q_norm_w) @ Wq_b
        q = q.reshape(B, T, H, D_QK)
        q_pass, q_rot = (q[..., :D_NOPE], q[..., D_NOPE:])
        kv = rmsnorm(hidden_states @ Wkv_a, kv_norm_w) @ Wkv_b
        kv = kv.reshape(B, T, H, D_NOPE + D_V)
        k_pass, v = (kv[..., :D_NOPE], kv[..., D_NOPE:])
        k_rot = (hidden_states @ Wk_rope)[:, :, None, :]
        cos, sin = rope_cos_sin(T, D_ROPE, hidden_states.dtype)
        q_rot = apply_rope(q_rot, cos, sin)
        k_rot = apply_rope(k_rot, cos, sin)
        k_rot = jnp.broadcast_to(k_rot, (B, T, H, D_ROPE))
        qf = jnp.concatenate([q_pass, q_rot], axis=-1)
        kf = jnp.concatenate([k_pass, k_rot], axis=-1)
        scale = 1.0 / np.sqrt(D_QK)
        scores = jnp.einsum('bqhd,bkhd->bhqk', qf, kf) * scale
        mask = jnp.tril(jnp.ones((T, T), dtype=bool))
        scores = jnp.where(mask[None, None], scores, jnp.finfo(scores.dtype).min)
        p = jax.nn.softmax(scores, axis=-1)
        o = jnp.einsum('bhqk,bkhd->bqhd', p, v)
        o = o.reshape(B, T, H * D_V) @ Wo
        return o

    def _L0_ffn_ref(hidden_states, gate_w, gate_up_proj, down_proj):
        import jax, jax.numpy as jnp
        import numpy as np
        B, S, H, E, I, TOPK = (1, 128, 256, 16, 128, 2)
        SCALE = 1.0
        b, s, h = hidden_states.shape
        e = gate_w.shape[0]
        x = hidden_states.reshape(-1, h)
        logits = jnp.matmul(x.astype(jnp.float32), gate_w.T.astype(jnp.float32))
        p = jax.nn.sigmoid(logits)
        p = p / jnp.sum(p, axis=-1, keepdims=True)
        w, idx = jax.lax.top_k(p, TOPK)
        w = w / jnp.sum(w, axis=-1, keepdims=True)
        w = w * SCALE
        combine = jnp.sum(jax.nn.one_hot(idx, e, dtype=w.dtype) * w[..., None], axis=1)
        gu = jnp.einsum('th,ehf->etf', x, gate_up_proj)
        gate, up = jnp.split(gu, 2, axis=-1)
        inter = jax.nn.silu(gate) * up
        y = jnp.einsum('eti,eih->eth', inter, down_proj)
        out = jnp.einsum('eth,te->th', y, combine.astype(y.dtype))
        return out.reshape(b, s, h)

    def _L1_attn_ref(hidden_states, Wq, Wk, Wv, Wo, bo):
        import jax, jax.numpy as jnp
        import numpy as np
        import math
        B, T, D = (2, 256, 256)
        H, G, DQ, DV = (16, 4, 128, 128)
        REP = H // G
        ROPE_THETA = 10000.0

        def _rope(x):
            t = x.shape[2]
            inv_freq = 1.0 / ROPE_THETA ** (jnp.arange(0, DQ, 2, dtype=jnp.float32) / DQ)
            freqs = jnp.arange(t, dtype=jnp.float32)[:, None] * inv_freq[None, :]
            freqs = jnp.repeat(freqs, 2, axis=-1)
            cos, sin = (jnp.cos(freqs), jnp.sin(freqs))
            x2 = x.reshape(*x.shape[:-1], DQ // 2, 2)
            rot = jnp.stack([-x2[..., 1], x2[..., 0]], axis=-1).reshape(x.shape)
            return x * cos + rot * sin

        def _alibi(t):
            slopes = 2.0 ** (-jnp.arange(1, H + 1, dtype=jnp.float32) * 8.0 / H)
            pos = jnp.arange(t, dtype=jnp.float32)
            diff = jnp.abs(pos[:, None] - pos[None, :])
            return -diff[None, :, :] * slopes[:, None, None]
        N, t, _ = hidden_states.shape
        q = (hidden_states @ Wq).reshape(N, t, H, DQ).transpose(0, 2, 1, 3)
        k = (hidden_states @ Wk).reshape(N, t, G, DQ).transpose(0, 2, 1, 3)
        v = (hidden_states @ Wv).reshape(N, t, G, DV).transpose(0, 2, 1, 3)
        q = _rope(q)
        k = _rope(k)
        k = jnp.repeat(k, REP, axis=1)
        v = jnp.repeat(v, REP, axis=1)
        scores = jnp.einsum('bhtd,bhsd->bhts', q, k)
        scores = scores + _alibi(t)[None]
        scores = scores / math.sqrt(DQ)
        scores = 30.0 * jnp.tanh(scores / 30.0)
        causal = jnp.tril(jnp.ones((t, t), bool))
        scores = jnp.where(causal[None, None], scores, -jnp.inf)
        probs = jax.nn.softmax(scores, axis=-1)
        ctx = jnp.einsum('bhts,bhsd->bhtd', probs, v)
        ctx = ctx.transpose(0, 2, 1, 3).reshape(N, t, H * DV)
        return ctx @ Wo + bo

    def _L1_ffn_ref(x, weight, bias):
        import jax, jax.numpy as jnp
        import numpy as np

        def binarize_weight(w):
            alpha = jnp.mean(jnp.abs(w), axis=tuple(range(1, w.ndim)), keepdims=True)
            bw = jnp.where(w >= 0, 1.0, -1.0) * alpha
            return jax.lax.stop_gradient(bw - w) + w
        bw = binarize_weight(weight)
        return jnp.einsum('bsi,oi->bso', x, bw) + bias
    x = L0_attn_hidden_states
    x = _layernorm(x + _L0_attn_ref(x, L0_attn_Wq_a, L0_attn_q_norm_w, L0_attn_Wq_b, L0_attn_Wk_rope, L0_attn_Wkv_a, L0_attn_kv_norm_w, L0_attn_Wkv_b, L0_attn_Wo), axis=-1)
    x = _layernorm(x + _L0_ffn_ref(x, L0_ffn_gate_w, L0_ffn_gate_up_proj, L0_ffn_down_proj), axis=-1)
    x = _layernorm(x + _L1_attn_ref(x, L1_attn_Wq, L1_attn_Wk, L1_attn_Wv, L1_attn_Wo, L1_attn_bo), axis=-1)
    x = _layernorm(x + _L1_ffn_ref(x, L1_ffn_weight, L1_ffn_bias), axis=-1)
    return x

_drawn_inputs = setup_inputs


def setup_inputs(seed=0):
    import zlib

    import numpy as np

    out = dict(_drawn_inputs(seed))
    spreads = {'L0_attn_q_norm_w': (1.0, 0.2), 'L0_attn_kv_norm_w': (1.0, 0.2), 'L1_attn_bo': (0.0, 0.1)}
    factors = {'L1_attn_Wq': 8.0, 'L1_attn_Wk': 8.0, 'L1_ffn_bias': 8.0}
    for name, (base, spread) in spreads.items():
        noise = np.random.default_rng([zlib.crc32(name.encode()), seed]).standard_normal(out[name].shape)
        drawn = base * np.exp(spread * noise) if base else spread * noise
        out[name] = jnp.asarray(drawn.astype(out[name].dtype))
    for name, factor in factors.items():
        out[name] = (out[name] * factor).astype(out[name].dtype)
    return out
```

```python
from contextlib import ExitStack

import numpy as np

import concourse.bass as bass
from concourse import mybir

F32 = mybir.dt.float32
F32R = mybir.dt.float32r
BF16 = mybir.dt.bfloat16
ALU = mybir.AluOpType
ACT = mybir.ActivationFunctionType
AX_X = mybir.AxisListType.X

P = 128
B, T, D = 4, 256, 256
NT = B * T // P
KD = D // P
H = 16
PAIRS = H // 2
NOPE, ROPE, DV = 128, 64, 128
QL, KVL = 192, 64
KQ = QL // 2
DQ = 128
G = 4
E, FF = 16, 128
LN_EPS, RMS_EPS = 1e-5, 1e-6
NEG = -1e30
ROUTE_STEPS, FFN_STEPS, N_CONSTS = 21, 6, 9
Y_BEFORE = {0: 0, 2: NT, 3: 2 * NT}
PROJ = QL + KVL + ROPE


def shape_constants():
    pos = np.arange(T, dtype=np.float32)

    def angles(dim):
        inv = (np.float32(1.0) / np.float32(10000.0) ** (np.arange(0, dim, 2, dtype=np.float32) / np.float32(dim)))
        return (pos[:, None] * inv.astype(np.float32)[None, :]).astype(np.float32)

    a0, a1 = angles(ROPE), angles(DQ)
    c0, s0, c1, s1 = (f(a).astype(np.float32) for a in (a0, a1) for f in (np.cos, np.sin))
    one, zero = np.ones((T, KVL), np.float32), np.zeros((T, KVL), np.float32)
    rope_cos = np.stack([np.concatenate([one, c0, c0], 1).T, np.concatenate([c1, c1], 1).T], 1)
    rope_sin = np.stack([np.concatenate([zero, -s0, s0], 1).T, np.concatenate([-s1, s1], 1).T], 1)
    key_cos = np.concatenate([c0, c0], 1).reshape(T // P, P, ROPE).transpose(1, 0, 2)
    key_sin = np.concatenate([-s0, s0], 1).reshape(T // P, P, ROPE).transpose(1, 0, 2)
    later = np.where(np.arange(P)[None, :] > np.arange(P)[:, None], np.float32(NEG), np.float32(0))
    mask = np.concatenate([later, later], 1)

    def parts(x):
        out, rest = [], x.astype(np.float32)
        for _ in range(3):
            hi = ((rest.view(np.uint32) + np.uint32(0x8000)) & np.uint32(0xFFFF0000)).view(np.float32)
            out.append(hi)
            rest = (rest - hi).astype(np.float32)
        return out

    slopes = np.float32(2.0) ** (-np.arange(1, H + 1, dtype=np.float32) * np.float32(8.0) / np.float32(H))
    slopes = slopes.astype(np.float32)
    key_rows = parts((slopes[:, None] * pos[None, :]).astype(np.float32))
    key_rows += parts(np.ascontiguousarray(np.broadcast_to(-slopes[:, None], (H, T))))
    alibi_keys = np.stack(key_rows, 0)
    alibi_queries = np.stack([np.ones(T, np.float32)] * 3 + [pos] * 3, 0)
    rank = np.broadcast_to(np.float32(E) - np.arange(E, dtype=np.float32), (P, E))
    out = dict(c_ident=np.eye(P, dtype=np.float32), c_mask=mask, c_rope_cos=rope_cos, c_rope_sin=rope_sin,
               c_key_cos=key_cos, c_key_sin=key_sin, c_alibi_keys=alibi_keys, c_alibi_queries=alibi_queries,
               c_rank=rank)
    return {k: np.ascontiguousarray(v, dtype=np.float32) for k, v in out.items()}


def raw(ap):
    return ap.bitcast(F32)


def program(nc, a, out):
    with ExitStack() as ctx:
        build(nc, a, out, ctx)


def build(nc, a, out, ctx):
    def sb(name, shape, dt=F32, stack=ctx):
        return stack.enter_context(nc.sbuf_tensor(name, shape, dt))

    def sem(name):
        return ctx.enter_context(nc.semaphore(name))

    def sems(prefix, names):
        return dict(**{n: sem(f"{prefix}_{n}") for n in names.split()})

    x_tok = sb("x_tok", [P, NT, D])
    ident = sb("ident", [P, P])
    ident_bf = sb("ident_bf", [P, P], BF16)
    mask = sb("mask", [P, 2 * P])
    mask_bf = sb("mask_bf", [P, 2 * P], BF16)
    rope_cos = sb("rope_cos", [P, 2, T])
    rope_sin = sb("rope_sin", [P, 2, T])
    bo_rows = sb("bo_rows", [P, D])
    bias_rows = sb("bias_rows", [P, D])
    alibi_keys = sb("alibi_keys", [6, H, T], BF16)
    alibi_queries = sb("alibi_queries", [6, T], BF16)
    moments = sb("moments", [P, NT, 2])
    bn_out = sb("bn_out", [P, NT, 6])
    square_sum = sb("square_sum", [P, 2, NT])
    var_eps = sb("var_eps", [P, 2, NT])
    deviation = sb("deviation", [P, 2, NT])
    inv_dev = sb("inv_dev", [P, 2, NT])
    xT_hi = sb("xT_hi", [P, KD, B * T], F32R)
    xT_lo = sb("xT_lo", [P, KD, B * T], F32R)
    w_hi = sb("w_hi", [P, 2, 512], F32R)
    w_lo = sb("w_lo", [P, 2, 512], F32R)
    wq_full = sb("wq_full", [P, KD, H * P])
    wo_full = sb("wo_full", [P, H, D])
    keysT = sb("keysT", [P, G, B * T])
    v_head = sb("v_head", [P, 2, 2, DV])
    qT = sb("qT", [P, 2, B * T])
    swapped = sb("swapped", [P, 2, 2 * T])
    probs = sb("probs", [P, 2, 2, 3 * P])
    probsT = sb("probsT", [P, 2, 2, 3 * P])
    row_max = sb("row_max", [P, 2, 4])
    neg_max = sb("neg_max", [P, 2, 4])
    row_sum = sb("row_sum", [P, 2, 4])
    inv_sum = sb("inv_sum", [P, 2, 4])
    bank = ctx.enter_context(nc.psum_tensor("bank", [P, 8, 512], F32))

    with ExitStack() as early:
        latT_hi = sb("latT_hi", [P, 2, B * T], F32R, early)
        latT_lo = sb("latT_lo", [P, 2, B * T], F32R, early)
    v_tok = sb("v_tok", [P, NT, G * DV])
    with ExitStack() as setup:
        wqb_raw = sb("wqb_raw", [KQ, 2, H * (NOPE + ROPE)], F32, setup)
        wkvb_raw = sb("wkvb_raw", [KVL, H * (NOPE + DV)], F32, setup)
        wo_raw = sb("wo_raw", [P, H, D], F32, setup)
        qn_rows = sb("qn_rows", [P, QL], F32, setup)
        kvn_rows = sb("kvn_rows", [P, KVL], F32, setup)
        key_cos = sb("key_cos", [P, 2, ROPE], F32, setup)
        key_sin = sb("key_sin", [P, 2, ROPE], F32, setup)
        wa_raw = sb("wa_raw", [P, KD, PROJ], F32, setup)
    with ExitStack() as layer0:
        ctxT0 = sb("ctxT0", [P, PAIRS, B * T], F32, layer0)
    with ExitStack() as moe:
        gate_raw = sb("gate_raw", [E, D], F32, moe)
        gate_hi = sb("gate_hi", [P, KD, P], F32R, moe)
        gate_lo = sb("gate_lo", [P, KD, P], F32R, moe)
        p_rows = sb("p_rows", [E, B * T], F32, moe)
        p_tok = sb("p_tok", [P, NT, E], F32, moe)
        rank = sb("rank", [P, E], F32, moe)
        chosen = sb("chosen", [P, 2, NT, E], F32, moe)
        scratch = sb("scratch", [P, NT, E], F32, moe)
        best = sb("best", [P, 6, NT], F32, moe)
        wgu_raw = sb("wgu_raw", [P, 2, KD * 2 * FF], F32, moe)
        wdn_raw = sb("wdn_raw", [P, 2, D], F32, moe)
        wdn_hi = sb("wdn_hi", [P, 2, D], F32R, moe)
        wdn_lo = sb("wdn_lo", [P, 2, D], F32R, moe)
        comb_rows = sb("comb_rows", [P, 2, B * T], F32, moe)
        silu = sb("silu", [P, 2, 512], F32, moe)
        weighted = sb("weighted", [P, 2, 512], F32, moe)
        zeros_bf = sb("zeros_bf", [P, 512], BF16, moe)
        wk_raw = sb("wk_raw", [P, KD, G * DQ], F32, moe)
        wv_raw = sb("wv_raw", [P, KD, G * DV], F32, moe)
        wq1_raw = sb("wq1_raw", [P, KD, H * DQ], F32, moe)
    ctxT1 = sb("ctxT1", [P, H, B * T])
    qlat_tok = qT[:].rearrange("p h t -> p (h t)")[:, 0:NT * QL].rearrange("p (t f) -> p t f", f=QL)
    key_tok = keysT[:, 1, :].rearrange("p (t f) -> p t f", f=P)
    key_part = swapped[:].rearrange("p a b -> p (a b)")[:, 0:NT * ROPE].rearrange("p (t f) -> p t f", f=ROPE)
    headT = probs[:].rearrange("p a h n -> p (a h n)")[:, 0:2 * 320].rearrange("p (a n) -> p a n", a=2)
    squares = probsT[:].rearrange("p a h n -> p (a h n)")[:, 0:NT * QL].rearrange("p (t n) -> p t n", n=QL)
    key_sq = v_head[:].rearrange("p a t n -> p (a t n)").rearrange("p (t n) -> p t n", n=KVL)
    ffn_w = probs[:].rearrange("p a h n -> p (a h n)")[:, 0:2 * D].rearrange("p (a n) -> p a n", a=2)
    ffn_bw = probsT[:].rearrange("p a h n -> p (a h n)")[:, 0:2 * D].rearrange("p (a n) -> p a n", a=2)
    comb_dram = nc.dram_tensor("comb_dram", (E, B * T), F32, kind="Internal").ap()
    x_dram = a["x"].rearrange("b (j p) d -> p (b j) d", p=P)
    out_dram = out.rearrange("b (j p) d -> p (b j) d", p=P)

    x_in = [sem(f"x_in{b}") for b in range(B)]
    expert_in = [sem("expert_in0"), sem("expert_in1")]
    comb_in = [sem("comb_in0"), sem("comb_in1")]
    ld = sems("load", "ident_in consts_in bf_in alibi_in wa_in wqb_in wkvb_in wo0_in gate_in wkv1_in wq1_in wo1_in ffn_in "
              "comb_out stored")
    su = sems("setup", "wa_hi wa_lo proj_done sq_done rms_var rms_sqrt rms_inv latents key_steps latT_done latT_hi_done "
              "latT_lo_done keysT_copied headT_done headT_copied fold_done fold_q_copied fold_o_copied rope_cols")
    ln = sems("norm", "xT_done xT_hi_done xT_lo_done y_done rows_added y_read stats var_ready moments_ready sqrt_done "
              "inv_ready x_new")
    mo = sems("moe", "gateT_done gate_zero gate_hi gate_lo logits_done sigmoid_done p_done step combT_done combT_copied "
              "zeros gu_hi gu_lo dn_hi dn_lo up_done silu_done weighted act act_hi act_lo down_done")
    kv = sems("kv1", "wk_hi wk_lo k_done cos_done swap_done sin_done k_ready wv_hi wv_lo v_done v_copied wq_perm")
    ff = sems("ffn", "abs_done step bwT_done bw_hi bw_lo")

    def attention(name, layer):
        names = ("w_hi_done w_lo_done q_done cos_done swap_done sin_done q_ready scores_done max_step max_ready "
                 "capped masked exp_done inv_ready probs_ready probsT_done probsT_copied v_copied ctx_done "
                 "ctx_copied").split()
        return dict(layer=layer, **{n: sem(f"{name}_{n}") for n in names})

    at0, at1 = attention("a0", 0), attention("a1", 1)

    def scores_of(par):
        return bank[:, 2 * par:2 * par + 2, 0:3 * P]

    probsT_bank = bank[:, 4:6, 0:3 * P]
    CTX, QRY = 6, 7

    def perm_in(x, k, heads):
        return x[:, k, :].rearrange("p (h j e) -> p h e j", h=heads, e=2)

    def perm_out(x, k):
        return x[:, k, :].rearrange("p (h e j) -> p h e j", e=2, j=DQ // 2)

    def steps(eng, body):
        def pair(p, first, more):
            for b in range(B):
                body(p, b, 4 * p + b, (lambda k, b=b: not first or b >= k), True, more)

        pair(0, True, True)
        with eng.Fori(1, PAIRS - 1) as p:
            pair(p, False, True)
        pair(PAIRS - 1, False, False)
        for b in range(3):
            body(PAIRS, b, 4 * PAIRS + b, (lambda k, b=b: k > b), False, False)

    def back(p, b, k):
        return (p, b - k) if b >= k else (p - 1, b - k + B)

    def three_pass(eng, dst, s_hi, s_lo, m_hi, m_lo, start, stop):
        eng.matmul(dst, s_hi, m_hi, start=start, stop=False, skip_group_check=True)
        eng.matmul(dst, s_hi, m_lo, start=False, stop=False, skip_group_check=True)
        return eng.matmul(dst, s_lo, m_hi, start=False, stop=stop, skip_group_check=True)

    def pe_transpose_x(eng, turn):
        for b in range(B):
            if turn == 0:
                eng.wait_ge(x_in[b], 16)
                if b == 0:
                    eng.wait_ge(ld["ident_in"], 16)
            else:
                eng.wait_ge(ln["x_new"], NT * (turn - 1) + 2 * b + 2)
                if b == 0:
                    eng.wait_ge(ln["y_read"], NT * turn)
            for k in range(KD):
                for j in range(2):
                    mm = eng.transpose(bank[:, b, k * T + j * P:k * T + j * P + P],
                                       x_tok[:, 2 * b + j, k * P:k * P + P], ident[:])
            mm.then_inc(ln["xT_done"], 1)

    def pe_queries(eng, at, p, b):
        m = 4 * p + b
        rows = KQ if at["layer"] == 0 else P
        xh, xl = (latT_hi, latT_lo) if at["layer"] == 0 else (xT_hi, xT_lo)
        if b == 0:
            eng.wait_ge(at["w_hi_done"], p + 1)
            eng.wait_ge(at["w_lo_done"], p + 1)
        if not (isinstance(p, int) and m == 0):
            eng.wait_ge(at["cos_done"], m)
            eng.wait_ge(at["swap_done"], m)
        for h in range(2):
            for k in range(2):
                mm = three_pass(eng, bank[:, QRY, h * T:h * T + T],
                                w_hi[0:rows, k, h * P:h * P + P], w_lo[0:rows, k, h * P:h * P + P],
                                xh[0:rows, k, T * b:T * b + T], xl[0:rows, k, T * b:T * b + T],
                                k == 0, k == 1)
        mm.then_inc(at["q_done"], 1)

    def pe_attention(eng, at):
        def body(p, b, n, lag, own, more):
            if own:
                eng.wait_ge(at["q_ready"], n + 1)
                if lag(2):
                    eng.wait_ge(at["exp_done"] if at["layer"] == 0 else at["capped"], n - 1)
                group = 0 if at["layer"] == 0 else p // 2
                for h in range(2):
                    dst = bank[:, 2 * (b % 2) + h, :]
                    q = qT[:, h, T * b:T * b + T]
                    eng.matmul(dst[:, 0:T], q[:, P:T], keysT[:, group, T * b:T * b + T],
                               start=True, stop=False, skip_group_check=True)
                    eng.matmul(dst[:, T:T + P], q[:, 0:P], keysT[:, group, T * b:T * b + P],
                               start=False, stop=False, skip_group_check=True)
                    if at["layer"] == 0:
                        mm = eng.matmul(dst[:, P:3 * P], ident_bf[:], mask_bf[:],
                                        start=False, stop=True, skip_group_check=True)
                    else:
                        eng.matmul(dst[:, 0:T], alibi_queries[:, P:T], alibi_keys[:, 2 * p + h, :],
                                   start=False, stop=False, skip_group_check=True)
                        mm = eng.matmul(dst[:, T:T + P], alibi_queries[:, 0:P], alibi_keys[:, 2 * p + h, 0:P],
                                        start=False, stop=True, skip_group_check=True)
                mm.then_inc(at["scores_done"], 1)
            if more:
                pe_queries(eng, at, p + 1, b)
            if lag(1):
                eng.wait_ge(at["probs_ready"], n)
                if lag(2):
                    eng.wait_ge(at["probsT_copied"], n - 1)
                for h in range(2):
                    pr = probs[:, (b - 1) % 2, h, :]
                    dst = probsT_bank[:, h, :]
                    eng.transpose(dst[:, 0:P], pr[:, T:T + P], ident[:])
                    eng.transpose(dst[:, P:T], pr[:, 0:P], ident[:])
                    mm = eng.transpose(dst[:, T:T + P], pr[:, P:T], ident[:])
                mm.then_inc(at["probsT_done"], 1)
            if lag(2):
                b2 = (b - 2) % B
                eng.wait_ge(at["probsT_copied"], n - 1)
                if lag(3):
                    eng.wait_ge(at["ctx_copied"], n - 2)
                if at["layer"] == 1:
                    eng.wait_ge(at["v_copied"], n - 1)
                for h in range(2):
                    pt = probsT[:, b % 2, h, :]
                    if at["layer"] == 0:
                        dst = bank[64 * h:64 * h + 64, CTX, 0:T]
                        values = [key_tok[:, (2 * b2 + j + 4) % NT, 0:KVL] for j in range(2)]
                    else:
                        dst = bank[:, CTX, T * h:T * h + T]
                        values = [v_head[:, b % 2, j, :] for j in range(2)]
                    eng.matmul(dst, values[0], pt[:, 0:T], start=True, stop=False, skip_group_check=True)
                    mm = eng.matmul(dst[:, P:T], values[1], pt[:, T:T + P],
                                    start=False, stop=True, skip_group_check=True)
                mm.then_inc(at["ctx_done"], 1)

        for b in range(B):
            pe_queries(eng, at, 0, b)
        steps(eng, body)

    block = ctx.enter_context(nc.Block())

    @block.tensor
    def _(pe):
        pe_transpose_x(pe, 0)
        pe.wait_ge(su["wa_hi"], 1)
        pe.wait_ge(su["wa_lo"], 1)
        for t in range(NT):
            need = max(t // 2 + 1, t - 3)
            pe.wait_ge(ln["xT_hi_done"], need)
            pe.wait_ge(ln["xT_lo_done"], need)
            for k in range(KD):
                mm = three_pass(pe, bank[:, (t + 4) % NT, 0:PROJ],
                                xT_hi[:, k, t * P:t * P + P], xT_lo[:, k, t * P:t * P + P],
                                w_hi[:, k, 0:PROJ], w_lo[:, k, 0:PROJ], k == 0, k == KD - 1)
            mm.then_inc(su["proj_done"], 1)
        pe.wait_ge(su["latents"], 2 * NT)
        pe.wait_ge(su["key_steps"], 4)
        for b in range(B):
            for k in range(2):
                for j in range(2):
                    pe.transpose(bank[0:KQ, b, k * T + j * P:k * T + j * P + P],
                                 qlat_tok[:, 2 * b + j, k * KQ:k * KQ + KQ], ident[:])
            for j in range(2):
                mm = pe.transpose(bank[:, 4 + b, j * P:j * P + P], key_tok[:, (2 * b + j + 4) % NT, :], ident[:])
            mm.then_inc(su["latT_done"], 1)
        pe.wait_ge(su["latT_hi_done"], B)
        pe.wait_ge(su["latT_lo_done"], B)
        pe.wait_ge(su["keysT_copied"], B)
        pe.wait_ge(ld["wqb_in"], 32)
        pe.wait_ge(ld["wkvb_in"], 16)
        for h in range(H + 1):
            if h < H:
                if h >= 2:
                    pe.wait_ge(su["headT_copied"], h - 1)
                dst = bank[:, 6 + h % 2, :]
                for k in range(2):
                    c = h * (NOPE + ROPE)
                    pe.transpose(dst[:, k * KQ:k * KQ + KQ], wqb_raw[:, k, c:c + NOPE], ident[0:KQ, 0:KQ])
                c = h * (NOPE + DV)
                pe.transpose(dst[:, QL:QL + KVL], wkvb_raw[:, c:c + NOPE], ident[0:KVL, 0:KVL])
                pe.transpose(dst[:, QL + KVL:QL + 2 * KVL], wkvb_raw[:, c + NOPE:c + NOPE + DV],
                             ident[0:KVL, 0:KVL]).then_inc(su["headT_done"], 1)
            if h >= 1:
                g = h - 1
                pe.wait_ge(su["headT_copied"], g + 1)
                if g == 0:
                    pe.wait_ge(ld["wo0_in"], 16)
                if g >= 2:
                    pe.wait_ge(su["fold_q_copied"], g - 1)
                if g >= 4 and g % 2 == 0:
                    pe.wait_ge(su["fold_o_copied"], g // 2 - 1)
                ht = headT[:, g % 2, :]
                for k in range(2):
                    pe.matmul(bank[0:KQ, g % 2, k * KVL:k * KVL + KVL], ht[:, k * KQ:k * KQ + KQ],
                              ht[:, QL:QL + KVL], start=True, stop=True)
                r = 64 * (g % 2)
                pe.matmul(bank[r:r + 64, 2 + (g // 2) % 2, 0:D], ht[:, QL + KVL:QL + 2 * KVL], wo_raw[:, g, :],
                          start=True, stop=True).then_inc(su["fold_done"], 1)
        pe.wait_ge(su["fold_q_copied"], H)
        pe.wait_ge(su["fold_o_copied"], PAIRS)
        pe.wait_ge(ld["bf_in"], 32)
        pe_attention(pe, at0)
        pe.wait_ge(at0["ctx_copied"], 4 * PAIRS)
        for t in range(NT):
            if t >= 4:
                pe.wait_ge(ln["y_read"], t - 3)
            for p in range(PAIRS):
                mm = pe.matmul(bank[:, t % 4, 0:D], ctxT0[:, p, t * P:t * P + P], wo_full[:, p, :],
                               start=(p == 0), stop=(p == PAIRS - 1))
            mm.then_inc(ln["y_done"], 1)
        pe.wait_ge(ld["gate_in"], 32)
        for k in range(KD):
            mm = pe.transpose(bank[:, 4, k * E:k * E + E], gate_raw[:, k * P:k * P + P], ident[0:E, 0:E])
        mm.then_inc(mo["gateT_done"], 1)
        pe_transpose_x(pe, 1)
        pe.wait_ge(mo["gate_hi"], 1)
        pe.wait_ge(mo["gate_lo"], 1)
        for j in range(2):
            pe.wait_ge(ln["xT_hi_done"], B + 2 * j + 2)
            pe.wait_ge(ln["xT_lo_done"], B + 2 * j + 2)
            for k in range(KD):
                mm = three_pass(pe, bank[:, 5 + j, :], gate_hi[:, k, :], gate_lo[:, k, :],
                                xT_hi[:, k, 512 * j:512 * j + 512], xT_lo[:, k, 512 * j:512 * j + 512],
                                k == 0, k == KD - 1)
            mm.then_inc(mo["logits_done"], 1)
        pe.wait_ge(mo["zeros"], 1)
        for i in range(4):
            pe.matmul(bank[:, i, :], zeros_bf[:, 0:P], zeros_bf[:], start=True, stop=False, skip_group_check=True)
        pe.wait_ge(mo["sigmoid_done"], 2)
        for t in range(NT):
            mm = pe.transpose(bank[:, 4, t * E:t * E + E], p_rows[:, t * P:t * P + P], ident[0:E, 0:E])
        mm.then_inc(mo["p_done"], 1)
        pe.wait_ge(mo["step"], ROUTE_STEPS)
        for t in range(NT):
            mm = pe.transpose(bank[0:E, 6 + t // 4, (t % 4) * P:(t % 4) * P + P], chosen[:, 0, t, :], ident[:])
        mm.then_inc(mo["combT_done"], 1)
        pe.wait_ge(mo["combT_copied"], 1)

        def up(e, par, first):
            pe.wait_ge(mo["gu_hi"], e + 1)
            pe.wait_ge(mo["gu_lo"], e + 1)
            for j in range(2):
                if not first:
                    pe.wait_ge(mo["silu_done"], 2 * e + j - 1)
                    pe.wait_ge(mo["weighted"], 2 * e + j - 1)
                for half in range(2):
                    for k in range(KD):
                        c = k * 2 * FF + half * FF
                        mm = three_pass(pe, bank[:, 4 + 2 * j + half, :],
                                        w_hi[:, par, c:c + FF], w_lo[:, par, c:c + FF],
                                        xT_hi[:, k, 512 * j:512 * j + 512], xT_lo[:, k, 512 * j:512 * j + 512],
                                        k == 0, k == KD - 1)
                mm.then_inc(mo["up_done"], 1)

        def down(e, par):
            pe.wait_ge(mo["dn_hi"], e + 1)
            pe.wait_ge(mo["dn_lo"], e + 1)
            for j in range(2):
                pe.wait_ge(mo["act_hi"], 2 * e + j + 1)
                pe.wait_ge(mo["act_lo"], 2 * e + j + 1)
                for t in range(4 * j, 4 * j + 4):
                    mm = three_pass(pe, bank[:, t // 2, (t % 2) * D:(t % 2) * D + D],
                                    latT_hi[:, par, t * P:t * P + P], latT_lo[:, par, t * P:t * P + P],
                                    wdn_hi[:, par, :], wdn_lo[:, par, :], False, False)
            mm.then_inc(mo["down_done"], 1)

        up(0, 0, True)
        up(1, 1, False)
        down(0, 0)
        with pe.Fori(1, E // 2) as i:
            for par in range(2):
                up(2 * i + par, par, False)
                down(2 * i + par - 1, 1 - par)
        down(E - 1, 1)

        pe_transpose_x(pe, 2)
        pe.wait_ge(kv["wk_hi"], KD)
        pe.wait_ge(kv["wk_lo"], KD)
        for i in range(2 * G):
            g, j = i // 2, i % 2
            if i < 2:
                pe.wait_ge(ln["xT_hi_done"], 2 * B + 2 * j + 2)
                pe.wait_ge(ln["xT_lo_done"], 2 * B + 2 * j + 2)
            if i >= 4:
                pe.wait_ge(kv["cos_done"], i - 3)
                pe.wait_ge(kv["swap_done"], i - 3)
            for k in range(KD):
                mm = three_pass(pe, bank[:, 4 + i % 4, :],
                                w_hi[:, k, g * DQ:g * DQ + DQ], w_lo[:, k, g * DQ:g * DQ + DQ],
                                xT_hi[:, k, 512 * j:512 * j + 512], xT_lo[:, k, 512 * j:512 * j + 512],
                                k == 0, k == KD - 1)
            mm.then_inc(kv["k_done"], 1)
        pe.wait_ge(kv["wv_hi"], 1)
        pe.wait_ge(kv["wv_lo"], 1)
        for t in range(NT):
            if t >= 4:
                pe.wait_ge(kv["v_copied"], t - 3)
            for k in range(KD):
                mm = three_pass(pe, bank[:, t % 4, :],
                                xT_hi[:, k, t * P:t * P + P], xT_lo[:, k, t * P:t * P + P],
                                w_hi[:, k, :], w_lo[:, k, :], k == 0, k == KD - 1)
            mm.then_inc(kv["v_done"], 1)
        pe.wait_ge(kv["cos_done"], 2 * G)
        pe.wait_ge(kv["swap_done"], 2 * G)
        pe.wait_ge(kv["k_ready"], 2 * G)
        pe.wait_ge(kv["v_copied"], NT)
        pe.wait_ge(ld["alibi_in"], 32)
        pe_attention(pe, at1)
        pe.wait_ge(at1["ctx_copied"], 4 * PAIRS)
        pe.wait_ge(ld["wo1_in"], 16)
        for t in range(NT):
            if t >= 4:
                pe.wait_ge(ln["y_read"], 2 * NT + t - 3)
            for h in range(H):
                mm = pe.matmul(bank[:, t % 4, 0:D], ctxT1[:, h, t * P:t * P + P], wo_full[:, h, :],
                               start=(h == 0), stop=(h == H - 1))
            mm.then_inc(ln["y_done"], 1)
        pe.wait_ge(ff["step"], FFN_STEPS)
        for o in range(2):
            for k in range(KD):
                mm = pe.transpose(bank[:, 4, k * D + o * P:k * D + o * P + P], ffn_bw[:, o, k * P:k * P + P],
                                  ident[:])
        mm.then_inc(ff["bwT_done"], 1)
        pe_transpose_x(pe, 3)
        pe.wait_ge(ff["bw_hi"], 1)
        pe.wait_ge(ff["bw_lo"], 1)
        for t in range(NT):
            pe.wait_ge(ln["xT_hi_done"], 3 * B + t // 2 + 1)
            pe.wait_ge(ln["xT_lo_done"], 3 * B + t // 2 + 1)
            if t >= 4:
                pe.wait_ge(ln["y_read"], 3 * NT + t - 3)
            for k in range(KD):
                mm = three_pass(pe, bank[:, 4 + t % 4, 0:D],
                                xT_hi[:, k, t * P:t * P + P], xT_lo[:, k, t * P:t * P + P],
                                w_hi[:, k, 0:D], w_lo[:, k, 0:D], k == 0, k == KD - 1)
            mm.then_inc(ln["y_done"], 1)

    def act_split_x(act, turn):
        for b in range(B):
            act.wait_ge(ln["xT_done"], B * turn + b + 1)
            act.activation(xT_hi[:, :, T * b:T * b + T], bank[:, b, :].rearrange("p (k t) -> p k t", k=KD),
                           ACT.Copy).then_inc(ln["xT_hi_done"], 1)

    def act_sqrt(act, turn):
        act.wait_ge(ln["var_ready"], turn + 1)
        act.activation(deviation[:, 0, :], var_eps[:, 0, :], ACT.Sqrt).then_inc(ln["sqrt_done"], 1)

    def act_split_w(act, at, p):
        rows = KQ if at["layer"] == 0 else P
        if not (isinstance(p, int) and p == 0):
            act.wait_ge(at["q_done"], 4 * p)
        act.activation(w_hi[0:rows, :, 0:2 * P], wq_full[0:rows, :, bass.ds(2 * P * p, 2 * P)],
                       ACT.Copy).then_inc(at["w_hi_done"], 1)

    def act_swap(act, at, p, b):
        m = 4 * p + b
        act.wait_ge(at["q_done"], m + 1)
        if not (isinstance(p, int) and m < 2):
            act.wait_ge(at["q_ready"], m - 1)
        r0, rn = (64, 32) if at["layer"] == 0 else (0, 64)
        act.activation(swapped[r0:r0 + rn, b % 2, :], bank[r0 + rn:r0 + 2 * rn, QRY, :], ACT.Copy)
        act.activation(swapped[r0 + rn:r0 + 2 * rn, b % 2, :], bank[r0:r0 + rn, QRY, :],
                       ACT.Copy).then_inc(at["swap_done"], 1)

    def act_attention(act, at):
        scale = (NOPE + ROPE) ** -0.5

        def body(p, b, n, lag, own, more):
            par = b % 2
            if more and b == 0:
                act_split_w(act, at, p + 1)
            if own and at["layer"] == 1:
                act.wait_ge(at["scores_done"], n + 1)
                if lag(2):
                    act.wait_ge(at["probsT_done"], n - 1)
                act.activation(probs[:, par, :, :], scores_of(par), ACT.Tanh,
                               scale=DQ ** -0.5 / 30.0).then_inc(at["capped"], 1)
                if more:
                    act_swap(act, at, p + 1, b)
            if own:
                if at["layer"] == 0:
                    act.wait_ge(at["max_ready"], n + 1)
                    if lag(2):
                        act.wait_ge(at["probsT_done"], n - 1)
                else:
                    act.wait_ge(at["masked"], n + 1)
                for h in range(2):
                    for tile, c0, c1 in ((0, 0, T), (1, T, T + P)):
                        i = 2 * tile + h
                        if at["layer"] == 0:
                            ins = act.activation(probs[:, par, h, c0:c1], bank[:, 2 * par + h, c0:c1], ACT.Exp,
                                                 bias=neg_max[:, par, i:i + 1], scale=scale,
                                                 accum_out=row_sum[:, par, i:i + 1])
                        else:
                            ins = act.activation(probs[:, par, h, c0:c1], probs[:, par, h, c0:c1], ACT.Exp,
                                                 scale=30.0, accum_out=row_sum[:, par, i:i + 1])
                ins.then_inc(at["exp_done"], 1)
            if more and at["layer"] == 0:
                act_swap(act, at, p + 1, b)
            if lag(1) and at["layer"] == 0:
                act.wait_ge(at["probsT_done"], n)
                if lag(3):
                    act.wait_ge(at["ctx_done"], n - 2)
                act.activation(probsT[:, (b - 1) % 2, :, :], probsT_bank, ACT.Copy).then_inc(at["probsT_copied"], 1)

        act_split_w(act, at, 0)
        for b in range(B):
            act_swap(act, at, 0, b)
        steps(act, body)

    @block.scalar
    def _(act):
        act.wait_ge(ld["wa_in"], 48)
        act.activation(w_hi[:, :, 0:PROJ], wa_raw[:], ACT.Copy).then_inc(su["wa_hi"], 1)
        act_split_x(act, 0)
        for t in range(NT):
            act.wait_ge(su["proj_done"], t + 1)
            src = bank[:, (t + 4) % NT, :]
            act.activation(squares[:, t, :], src[:, 0:QL], ACT.Square,
                           accum_out=square_sum[:, 0, t:t + 1]).then_inc(su["sq_done"], 1)
            act.activation(key_sq[:, t, :], src[:, QL:QL + KVL], ACT.Square,
                           accum_out=square_sum[:, 1, t:t + 1]).then_inc(su["sq_done"], 1)
        act.wait_ge(su["rms_var"], 2)
        act.activation(deviation[:], var_eps[:], ACT.Sqrt).then_inc(su["rms_sqrt"], 1)
        for b in range(B):
            act.wait_ge(su["latT_done"], b + 1)
            act.activation(latT_hi[0:KQ, :, T * b:T * b + T], bank[0:KQ, b, :].rearrange("p (k t) -> p k t", k=2),
                           ACT.Copy).then_inc(su["latT_hi_done"], 1)
            act.activation(keysT[:, 0, T * b:T * b + T], bank[:, 4 + b, 0:T],
                           ACT.Copy).then_inc(su["keysT_copied"], 1)
        for h in range(H):
            act.wait_ge(su["headT_done"], h + 1)
            if h >= 2:
                act.wait_ge(su["fold_done"], h - 1)
            act.activation(headT[:, h % 2, :], bank[:, 6 + h % 2, 0:QL + 2 * KVL],
                           ACT.Copy).then_inc(su["headT_copied"], 1)
        act.wait_ge(su["rope_cols"], 2)
        act.wait_ge(su["fold_q_copied"], H)
        act_attention(act, at0)
        act_sqrt(act, 0)
        act.wait_ge(mo["gateT_done"], 1)
        act.wait_ge(mo["gate_zero"], 2)
        act.activation(gate_hi[:, :, 0:E], bank[:, 4, 0:KD * E].rearrange("p (k e) -> p k e", k=KD),
                       ACT.Copy).then_inc(mo["gate_hi"], 1)
        act_split_x(act, 1)
        for j in range(2):
            act.wait_ge(mo["logits_done"], j + 1)
            act.activation(p_rows[:, 512 * j:512 * j + 512], bank[0:E, 5 + j, :],
                           ACT.Sigmoid).then_inc(mo["sigmoid_done"], 1)
        act.wait_ge(mo["combT_done"], 1)
        act.activation(p_rows[:].rearrange("e (a n) -> e a n", a=2), bank[0:E, 6:8, :],
                       ACT.Copy).then_inc(mo["combT_copied"], 1)

        def gate_up_hi(e, par, i, first):
            act.wait_ge(expert_in[par], 32 * (i + 1))
            if not first:
                act.wait_ge(mo["up_done"], 2 * e - 2)
            act.activation(w_hi[:, par, :], wgu_raw[:, par, :], ACT.Copy).then_inc(mo["gu_hi"], 1)

        def down_hi(e, par, first):
            if not first:
                act.wait_ge(mo["down_done"], e - 1)
            act.activation(wdn_hi[:, par, :], wdn_raw[:, par, :], ACT.Copy).then_inc(mo["dn_hi"], 1)

        def activations(e, par, first):
            for j in range(2):
                act.wait_ge(mo["up_done"], 2 * e + j + 1)
                if not first:
                    act.wait_ge(mo["act_lo"], 2 * e + j - 1)
                act.activation(silu[:, j, :], bank[:, 4 + 2 * j, :], ACT.Silu).then_inc(mo["silu_done"], 1)
            for j in range(2):
                act.wait_ge(mo["act"], 2 * e + j + 1)
                if j == 0 and not first:
                    act.wait_ge(mo["down_done"], e - 1)
                act.activation(latT_hi[:, par, 512 * j:512 * j + 512], silu[:, j, :],
                               ACT.Copy).then_inc(mo["act_hi"], 1)

        gate_up_hi(0, 0, 0, True)
        down_hi(0, 0, True)
        gate_up_hi(1, 1, 0, True)
        activations(0, 0, True)
        down_hi(1, 1, True)
        with act.Fori(1, E // 2) as i:
            gate_up_hi(2 * i, 0, i, False)
            activations(2 * i - 1, 1, False)
            down_hi(2 * i, 0, False)
            gate_up_hi(2 * i + 1, 1, i, False)
            activations(2 * i, 0, False)
            down_hi(2 * i + 1, 1, False)
        activations(E - 1, 1, False)
        act_sqrt(act, 1)

        act.wait_ge(ld["wkv1_in"], 32)
        act.wait_ge(mo["up_done"], 2 * E)
        for k in range(KD):
            act.activation(perm_out(w_hi, k), perm_in(wk_raw, k, G), ACT.Copy).then_inc(kv["wk_hi"], 1)
        act_split_x(act, 2)
        for i in range(2 * G):
            act.wait_ge(kv["k_done"], i + 1)
            if i >= 2:
                act.wait_ge(kv["k_ready"], i - 1)
            act.activation(swapped[0:64, i % 2, :], bank[64:P, 4 + i % 4, :], ACT.Copy)
            act.activation(swapped[64:P, i % 2, :], bank[0:64, 4 + i % 4, :], ACT.Copy).then_inc(kv["swap_done"], 1)
        act.activation(w_hi[:], wv_raw[:], ACT.Copy).then_inc(kv["wv_hi"], 1)
        for t in range(NT):
            act.wait_ge(kv["v_done"], t + 1)
            act.activation(v_tok[:, t, :], bank[:, t % 4, :], ACT.Copy).then_inc(kv["v_copied"], 1)
        act.wait_ge(kv["wq_perm"], KD)
        act_attention(act, at1)
        act.wait_ge(ld["ffn_in"], 16)
        act.wait_ge(at1["ctx_done"], 4 * PAIRS)
        for o in range(2):
            act.activation(ffn_bw[:, o, :], ffn_w[:, o, :], ACT.Abs,
                           accum_out=square_sum[:, 0, o:o + 1]).then_inc(ff["abs_done"], 1)
        act_sqrt(act, 2)
        act.wait_ge(ff["bwT_done"], 1)
        act.activation(w_hi[:, :, 0:D], bank[:, 4, :].rearrange("p (k o) -> p k o", k=KD),
                       ACT.Copy).then_inc(ff["bw_hi"], 1)
        act_split_x(act, 3)
        act_sqrt(act, 3)

    def dve_split_x(dve, turn):
        for b in range(B):
            dve.wait_ge(ln["xT_hi_done"], B * turn + b + 1)
            sl = (slice(None), slice(None), slice(T * b, T * b + T))
            dve.tensor_tensor(xT_lo[sl], bank[:, b, :].rearrange("p (k t) -> p k t", k=KD), raw(xT_hi[sl]),
                              ALU.subtract).then_inc(ln["xT_lo_done"], 1)

    def dve_layer_norm(dve, turn, y_of):
        for t in range(NT):
            y_of(t)
            dve.wait_ge(ln["y_read"], NT * turn + t + 1)
            dve.bn_stats(bn_out[:, t, :], x_tok[:, t, :]).then_inc(ln["stats"], 1)
            dve.wait_ge(ln["stats"], NT * turn + t + 1)
            dve.bn_aggr(moments[:, t, :], bn_out[:, t, :]).then_inc(ln["moments_ready"], 1)
        dve.wait_ge(ln["moments_ready"], NT * (turn + 1))
        dve.tensor_scalar(var_eps[:, 0, :], moments[:, :, 1], LN_EPS, None, ALU.add).then_inc(ln["var_ready"], 1)
        dve.wait_ge(ln["sqrt_done"], turn + 1)
        dve.reciprocal(inv_dev[:, 0, :], deviation[:, 0, :]).then_inc(ln["inv_ready"], 1)
        dve.wait_ge(ln["inv_ready"], turn + 1)
        for t in range(NT):
            dve.tensor_scalar(x_tok[:, t, :], x_tok[:, t, :], moments[:, t, 0:1], inv_dev[:, 0, t:t + 1],
                              ALU.subtract, ALU.mult).then_inc(ln["x_new"], 1)

    def dve_add_y(dve, turn, banks_from=0):
        def y_of(t):
            dve.wait_ge(ln["y_done"], Y_BEFORE[turn] + t + 1)
            dve.tensor_tensor(x_tok[:, t, :], bank[:, banks_from + t % 4, 0:D], x_tok[:, t, :],
                              ALU.add).then_inc(ln["y_read"], 1)
        return y_of

    def dve_split_w(dve, at, p):
        rows = KQ if at["layer"] == 0 else P
        dve.wait_ge(at["w_hi_done"], p + 1)
        dve.tensor_tensor(w_lo[0:rows, :, 0:2 * P], wq_full[0:rows, :, bass.ds(2 * P * p, 2 * P)],
                          raw(w_hi[0:rows, :, 0:2 * P]), ALU.subtract).then_inc(at["w_lo_done"], 1)

    def cos_rows(layer):
        return rope_cos[:, layer:layer + 1, :].broadcast_to([P, 2, T])

    def sin_rows(layer, r0):
        return rope_sin[r0:P, layer:layer + 1, :].broadcast_to([P - r0, 2, T])

    def pair_view(ap):
        return ap.rearrange("p (h t) -> p h t", h=2)

    def dve_cos(dve, at, p, b):
        m = 4 * p + b
        dve.wait_ge(at["swap_done"], m + 1)
        dve.tensor_tensor(qT[:, :, T * b:T * b + T], pair_view(bank[:, QRY, :]), cos_rows(at["layer"]),
                          ALU.mult).then_inc(at["cos_done"], 1)

    def dve_rope_sum(dve, at, p, b):
        m = 4 * p + b
        dve.wait_ge(at["cos_done"], m + 1)
        dve.wait_ge(at["sin_done"], m + 1)
        dve.tensor_tensor(qT[:, :, T * b:T * b + T], qT[:, :, T * b:T * b + T], pair_view(swapped[:, b % 2, :]),
                          ALU.add).then_inc(at["q_ready"], 1)

    def dve_attention(dve, at):
        scale = (NOPE + ROPE) ** -0.5

        def body(p, b, n, lag, own, more):
            par = b % 2
            if more and b == 0:
                dve_split_w(dve, at, p + 1)
            if lag(3):
                p3, b3 = back(p, b, 3)
                dve.wait_ge(at["ctx_done"], n - 2)
                if at["layer"] == 0:
                    dst = ctxT0[:, p3, T * b3:T * b3 + T]
                    src = bank[:, CTX, 0:T]
                else:
                    dst = ctxT1[:, bass.ds(2 * p3, 2), T * b3:T * b3 + T]
                    src = pair_view(bank[:, CTX, :])
                dve.tensor_copy(dst, src).then_inc(at["ctx_copied"], 1)
            if lag(1):
                p1, b1 = back(p, b, 1)
                q = 1 - par
                dve.wait_ge(at["exp_done"], n)
                dve.reciprocal(inv_sum[:, q, :], row_sum[:, q, :]).then_inc(at["inv_ready"], 1)
                dve.wait_ge(at["inv_ready"], n)
                for h in range(2):
                    for tile, c0, c1 in ((0, 0, T), (1, T, T + P)):
                        i = 2 * tile + h
                        ins = dve.tensor_scalar(probs[:, q, h, c0:c1], probs[:, q, h, c0:c1],
                                                inv_sum[:, q, i:i + 1], None, ALU.mult)
                ins.then_inc(at["probs_ready"], 1)
                if at["layer"] == 1:
                    if lag(3):
                        dve.wait_ge(at["ctx_done"], n - 2)
                    dve.tensor_copy(v_head[:, q, :, :],
                                    v_tok[:, 2 * b1:2 * b1 + 2, bass.ds((p1 // 2) * DV, DV)])\
                       .then_inc(at["v_copied"], 1)
            if own and at["layer"] == 0:
                dve.wait_ge(at["scores_done"], n + 1)
                if lag(2):
                    dve.wait_ge(at["exp_done"], n - 1)
                sc = scores_of(par)
                dve.tensor_reduce(row_max[:, par, 0:2], sc[:, :, 0:T], AX_X, ALU.max).then_inc(at["max_step"], 1)
                dve.tensor_reduce(row_max[:, par, 2:4], sc[:, :, T:T + P], AX_X, ALU.max).then_inc(at["max_step"], 1)
                dve.wait_ge(at["max_step"], 2 * n + 2)
                dve.tensor_scalar(neg_max[:, par, :], row_max[:, par, :], -scale, None,
                                  ALU.mult).then_inc(at["max_ready"], 1)
            if more:
                dve_cos(dve, at, p + 1, b)
            if lag(1) and at["layer"] == 1:
                dve.wait_ge(at["probsT_done"], n)
                dve.tensor_copy(probsT[:, (b - 1) % 2, :, :], probsT_bank).then_inc(at["probsT_copied"], 1)
            if more and at["layer"] == 1:
                dve_rope_sum(dve, at, p + 1, b)

        dve_split_w(dve, at, 0)
        for b in range(B):
            dve_cos(dve, at, 0, b)
            if at["layer"] == 1:
                dve_rope_sum(dve, at, 0, b)
        steps(dve, body)

    @block.vector
    def _(dve):
        dve.wait_ge(su["wa_hi"], 1)
        dve.tensor_tensor(w_lo[:, :, 0:PROJ], wa_raw[:], raw(w_hi[:, :, 0:PROJ]),
                          ALU.subtract).then_inc(su["wa_lo"], 1)
        dve_split_x(dve, 0)
        dve.wait_ge(ld["consts_in"], 16 * N_CONSTS)
        dve.wait_ge(su["sq_done"], 2 * NT)
        kr = bank[:, :, QL + KVL:PROJ].rearrange("p (b j) f -> p b j f", j=2)
        kp = key_part.rearrange("p (b j) f -> p b j f", j=2)
        kt = key_tok[:, :, KVL:P].rearrange("p (b j) f -> p b j f", j=2)

        def table(x, c0, c1):
            return x[:, :, c0:c1].unsqueeze(1).broadcast_to([P, B, 2, c1 - c0])

        half = ROPE // 2
        dve.tensor_tensor(kt, kr, table(key_cos, 0, ROPE), ALU.mult).then_inc(su["key_steps"], 1)
        dve.tensor_tensor(kp[:, :, :, 0:half], kr[:, :, :, half:ROPE], table(key_sin, 0, half),
                          ALU.mult).then_inc(su["key_steps"], 1)
        dve.tensor_tensor(kp[:, :, :, half:ROPE], kr[:, :, :, 0:half], table(key_sin, half, ROPE),
                          ALU.mult).then_inc(su["key_steps"], 1)
        dve.wait_ge(su["key_steps"], 3)
        dve.tensor_tensor(kt, kt, kp, ALU.add).then_inc(su["key_steps"], 1)
        dve.tensor_scalar(var_eps[:, 0, :], square_sum[:, 0, :], 1.0 / QL, RMS_EPS, ALU.mult,
                          ALU.add).then_inc(su["rms_var"], 1)
        dve.tensor_scalar(var_eps[:, 1, :], square_sum[:, 1, :], 1.0 / KVL, RMS_EPS, ALU.mult,
                          ALU.add).then_inc(su["rms_var"], 1)
        dve.wait_ge(su["rms_sqrt"], 1)
        dve.reciprocal(inv_dev[:], deviation[:]).then_inc(su["rms_inv"], 1)
        dve.wait_ge(su["rms_inv"], 1)
        for t in range(NT):
            src = bank[:, (t + 4) % NT, :]
            dve.scalar_tensor_tensor(out=qlat_tok[:, t, :], in0=src[:, 0:QL], scalar=inv_dev[:, 0, t:t + 1],
                                     in1=qn_rows[:], op0=ALU.mult, op1=ALU.mult).then_inc(su["latents"], 1)
            dve.scalar_tensor_tensor(out=key_tok[:, (t + 4) % NT, 0:KVL], in0=src[:, QL:QL + KVL],
                                     scalar=inv_dev[:, 1, t:t + 1], in1=kvn_rows[:], op0=ALU.mult,
                                     op1=ALU.mult).then_inc(su["latents"], 1)
        for b in range(B):
            dve.wait_ge(su["latT_hi_done"], b + 1)
            sl = (slice(0, KQ), slice(None), slice(T * b, T * b + T))
            dve.tensor_tensor(latT_lo[sl], bank[0:KQ, b, :].rearrange("p (k t) -> p k t", k=2),
                              raw(latT_hi[sl]), ALU.subtract).then_inc(su["latT_lo_done"], 1)
        for h in range(H):
            dve.wait_ge(su["fold_done"], h + 1)
            dve.tensor_copy(wq_full[0:KQ, :, h * P:h * P + KVL],
                            bank[0:KQ, h % 2, 0:2 * KVL].rearrange("p (k f) -> p k f", k=2))\
               .then_inc(su["fold_q_copied"], 1)
            if h % 2:
                dve.tensor_copy(wo_full[:, h // 2, :], bank[:, 2 + (h // 2) % 2, 0:D])\
                   .then_inc(su["fold_o_copied"], 1)
        dve.wait_ge(su["rope_cols"], 2)
        dve.wait_ge(su["fold_q_copied"], H)
        dve_attention(dve, at0)
        dve_layer_norm(dve, 0, dve_add_y(dve, 0))
        dve.wait_ge(mo["gate_hi"], 1)
        dve.tensor_tensor(gate_lo[:, :, 0:E], bank[:, 4, 0:KD * E].rearrange("p (k e) -> p k e", k=KD),
                          raw(gate_hi[:, :, 0:E]), ALU.subtract).then_inc(mo["gate_lo"], 1)
        dve_split_x(dve, 1)
        n_step = [0]

        def step(ins):
            n_step[0] += 1
            ins.then_inc(mo["step"], 1)
            dve.wait_ge(mo["step"], n_step[0])

        def wide(col):
            return best[:, col, :].unsqueeze(2).broadcast_to([P, NT, E])

        ranks = rank[:].unsqueeze(1).broadcast_to([P, NT, E])
        dve.wait_ge(ld["gate_in"], 32)
        dve.wait_ge(mo["p_done"], 1)
        p_psum = bank[:, 4, 0:NT * E].rearrange("p (t e) -> p t e", e=E)
        step(dve.tensor_reduce(best[:, 0, :], p_psum, AX_X, ALU.add))
        step(dve.reciprocal(best[:, 1, :], best[:, 0, :]))
        step(dve.tensor_tensor(p_tok[:], p_psum, wide(1), ALU.mult))
        for i in range(2):
            step(dve.tensor_reduce(best[:, 2 + i, :], p_tok[:], AX_X, ALU.max))
            step(dve.tensor_tensor(scratch[:], p_tok[:], wide(2 + i), ALU.is_equal))
            step(dve.tensor_tensor(scratch[:], scratch[:], ranks, ALU.mult))
            step(dve.tensor_reduce(best[:, 4, :], scratch[:], AX_X, ALU.max))
            step(dve.tensor_tensor(chosen[:, i, :, :], scratch[:], wide(4), ALU.is_equal))
            if i == 0:
                step(dve.scalar_tensor_tensor(out=p_tok[:], in0=chosen[:, 0, :, :], scalar=-2.0, in1=p_tok[:],
                                              op0=ALU.mult, op1=ALU.add))
        step(dve.tensor_tensor(best[:, 4, :], best[:, 2, :], best[:, 3, :], ALU.add))
        step(dve.reciprocal(best[:, 5, :], best[:, 4, :]))
        for i in range(2):
            step(dve.tensor_tensor(best[:, 2 + i, :], best[:, 2 + i, :], best[:, 5, :], ALU.mult))
            step(dve.tensor_tensor(chosen[:, i, :, :], chosen[:, i, :, :], wide(2 + i), ALU.mult))
        step(dve.tensor_tensor(chosen[:, 0, :, :], chosen[:, 0, :, :], chosen[:, 1, :, :], ALU.add))
        assert n_step[0] == ROUTE_STEPS

        def expert(e, par, i, first):
            dve.wait_ge(comb_in[par], 16 * (i + 1))
            for j in range(2):
                dve.wait_ge(mo["up_done"], 2 * e + j + 1)
                dve.tensor_tensor(weighted[:, j, :], bank[:, 5 + 2 * j, :], comb_rows[:, par, 512 * j:512 * j + 512],
                                  ALU.mult).then_inc(mo["weighted"], 1)
                dve.wait_ge(mo["silu_done"], 2 * e + j + 1)
                dve.wait_ge(mo["weighted"], 2 * e + j + 1)
                dve.tensor_tensor(silu[:, j, :], silu[:, j, :], weighted[:, j, :], ALU.mult).then_inc(mo["act"], 1)
            for j in range(2):
                dve.wait_ge(mo["act_hi"], 2 * e + j + 1)
                if not first:
                    dve.wait_ge(mo["down_done"], e - 1)
                c = slice(512 * j, 512 * j + 512)
                dve.tensor_tensor(latT_lo[:, par, c], silu[:, j, :], raw(latT_hi[:, par, c]),
                                  ALU.subtract).then_inc(mo["act_lo"], 1)

        expert(0, 0, 0, True)
        expert(1, 1, 0, True)
        with dve.Fori(1, E // 2) as i:
            for par in range(2):
                expert(2 * i + par, par, i, False)

        def y_of_experts(t):
            if t == 0:
                dve.wait_ge(mo["down_done"], E)
            dve.tensor_tensor(x_tok[:, t, :], bank[:, t // 2, (t % 2) * D:(t % 2) * D + D], x_tok[:, t, :],
                              ALU.add).then_inc(ln["y_read"], 1)

        dve_layer_norm(dve, 1, y_of_experts)

        for k in range(KD):
            dve.wait_ge(kv["wk_hi"], k + 1)
            dve.tensor_tensor(perm_out(w_lo, k), perm_in(wk_raw, k, G), raw(perm_out(w_hi, k)),
                              ALU.subtract).then_inc(kv["wk_lo"], 1)
        dve_split_x(dve, 2)
        for i in range(2 * G):
            g, j = i // 2, i % 2
            dst = pair_view(keysT[:, g, 512 * j:512 * j + 512])
            dve.wait_ge(kv["swap_done"], i + 1)
            dve.tensor_tensor(dst, pair_view(bank[:, 4 + i % 4, :]), cos_rows(1), ALU.mult).then_inc(kv["cos_done"], 1)
            dve.wait_ge(kv["sin_done"], i + 1)
            dve.wait_ge(kv["cos_done"], i + 1)
            dve.tensor_tensor(dst, dst, pair_view(swapped[:, i % 2, :]), ALU.add).then_inc(kv["k_ready"], 1)
        dve.wait_ge(kv["wv_hi"], 1)
        dve.tensor_tensor(w_lo[:], wv_raw[:], raw(w_hi[:]), ALU.subtract).then_inc(kv["wv_lo"], 1)
        dve.wait_ge(kv["wq_perm"], KD)
        dve.wait_ge(kv["v_done"], NT)
        dve_attention(dve, at1)
        n_step[0] = 0

        def fstep(ins):
            n_step[0] += 1
            ins.then_inc(ff["step"], 1)
            dve.wait_ge(ff["step"], n_step[0])

        dve.wait_ge(ff["abs_done"], 2)
        fstep(dve.tensor_scalar(square_sum[:, 1, 0:2], square_sum[:, 0, 0:2], 1.0 / D, None, ALU.mult))
        fstep(dve.tensor_scalar(ffn_bw, ffn_w, 0.0, 2.0, ALU.is_ge, ALU.mult))
        for o in range(2):
            fstep(dve.tensor_scalar(ffn_bw[:, o, :], ffn_bw[:, o, :], 1.0, square_sum[:, 1, o:o + 1],
                                    ALU.subtract, ALU.mult))
        fstep(dve.tensor_tensor(ffn_bw, ffn_bw, ffn_w, ALU.subtract))
        fstep(dve.tensor_tensor(ffn_bw, ffn_bw, ffn_w, ALU.add))
        assert n_step[0] == FFN_STEPS
        dve.wait_ge(ln["rows_added"], 1)
        dve_layer_norm(dve, 2, dve_add_y(dve, 2))
        dve.wait_ge(ff["bw_hi"], 1)
        dve.tensor_tensor(w_lo[:, :, 0:D], bank[:, 4, :].rearrange("p (k o) -> p k o", k=KD),
                          raw(w_hi[:, :, 0:D]), ALU.subtract).then_inc(ff["bw_lo"], 1)
        dve_split_x(dve, 3)
        dve.wait_ge(ln["rows_added"], 2)
        dve_layer_norm(dve, 3, dve_add_y(dve, 3, 4))

    def pool_sin(pool, at, p, b):
        m = 4 * p + b
        r0 = 64 if at["layer"] == 0 else 0
        pool.wait_ge(at["swap_done"], m + 1)
        sw = pair_view(swapped[r0:P, b % 2, :])
        pool.tensor_tensor(sw, sw, sin_rows(at["layer"], r0), ALU.mult).then_inc(at["sin_done"], 1)
        if at["layer"] == 0:
            q = qT[r0:P, :, T * b:T * b + T]
            pool.wait_ge(at["cos_done"], m + 1)
            pool.wait_ge(at["sin_done"], m + 1)
            pool.tensor_tensor(q, q, sw, ALU.add).then_inc(at["q_ready"], 1)

    def pool_attention(pool, at):
        def body(p, b, n, lag, own, more):
            if own and at["layer"] == 1:
                pr = probs[:, b % 2, :, P:3 * P]
                pool.wait_ge(at["capped"], n + 1)
                pool.tensor_tensor(pr, pr, mask[:].unsqueeze(1).broadcast_to([P, 2, 2 * P]),
                                   ALU.add).then_inc(at["masked"], 1)
            if more:
                pool_sin(pool, at, p + 1, b)

        for b in range(B):
            pool_sin(pool, at, 0, b)
        steps(pool, body)

    @block.gpsimd
    def _(pool):
        pool.dma_start(ident_bf[:], a["c_ident"]).then_inc(ld["bf_in"], 16)
        pool.dma_start(mask_bf[:], a["c_mask"]).then_inc(ld["bf_in"], 16)
        pool.dma_start(alibi_queries[:], a["c_alibi_queries"]).then_inc(ld["alibi_in"], 16)
        pool.dma_start(alibi_keys[:], a["c_alibi_keys"]).then_inc(ld["alibi_in"], 16)
        pool.wait_ge(ld["wqb_in"], 32)
        for k in range(2):
            src = wqb_raw[:, k, :].rearrange("p (h f) -> p h f", h=H)[:, :, NOPE:NOPE + ROPE]
            dst = wq_full[0:KQ, k, :].rearrange("p (h f) -> p h f", h=H)[:, :, KVL:P]
            pool.tensor_copy(dst, src).then_inc(su["rope_cols"], 1)
        pool.wait_ge(ld["consts_in"], 16 * N_CONSTS)
        pool.wait_ge(su["rope_cols"], 2)
        pool_attention(pool, at0)
        pool.wait_ge(ln["y_done"], NT)
        pool.memset(raw(gate_hi[:]), 0.0).then_inc(mo["gate_zero"], 1)
        pool.memset(raw(gate_lo[:]), 0.0).then_inc(mo["gate_zero"], 1)
        pool.memset(zeros_bf[:], 0.0).then_inc(mo["zeros"], 1)

        def low(e, par):
            pool.wait_ge(mo["gu_hi"], e + 1)
            pool.tensor_tensor(w_lo[:, par, :], wgu_raw[:, par, :], raw(w_hi[:, par, :]),
                               ALU.subtract).then_inc(mo["gu_lo"], 1)
            pool.wait_ge(mo["dn_hi"], e + 1)
            pool.tensor_tensor(wdn_lo[:, par, :], wdn_raw[:, par, :], raw(wdn_hi[:, par, :]),
                               ALU.subtract).then_inc(mo["dn_lo"], 1)

        low(0, 0)
        low(1, 1)
        pool.wait_ge(ld["wq1_in"], 16)
        for k in range(KD):
            pool.tensor_copy(perm_out(wq_full, k), perm_in(wq1_raw, k, H)).then_inc(kv["wq_perm"], 1)
        with pool.Fori(1, E // 2) as i:
            for par in range(2):
                low(2 * i + par, par)
        for i in range(2 * G):
            pool.wait_ge(kv["swap_done"], i + 1)
            sw = pair_view(swapped[:, i % 2, :])
            pool.tensor_tensor(sw, sw, sin_rows(1, 0), ALU.mult).then_inc(kv["sin_done"], 1)
        pool_attention(pool, at1)

        def add_rows(rows):
            pool.tensor_tensor(x_tok[:], x_tok[:], rows[:].unsqueeze(1).broadcast_to([P, NT, D]),
                               ALU.add).then_inc(ln["rows_added"], 1)

        pool.wait_ge(ld["consts_in"], 16 * N_CONSTS)
        pool.wait_ge(ln["xT_done"], 3 * B)
        add_rows(bo_rows)
        pool.wait_ge(ln["xT_done"], 4 * B)
        pool.wait_ge(ln["x_new"], 3 * NT)
        add_rows(bias_rows)

    @block.sync
    def _(sp):
        sp.dma_start(ident[:], a["c_ident"]).then_inc(ld["ident_in"], 16)
        for b in range(B):
            sp.dma_start(x_tok[:, 2 * b:2 * b + 2, :], x_dram[:, 2 * b:2 * b + 2, :]).then_inc(x_in[b], 16)
            if b == 0:
                for name, c0, c1 in (("Wq_a", 0, QL), ("Wkv_a", QL, QL + KVL), ("Wk_rope", QL + KVL, PROJ)):
                    sp.dma_start(wa_raw[:, :, c0:c1],
                                 a[name].rearrange("(k p) n -> p k n", p=P)).then_inc(ld["wa_in"], 16)
        consts = [(mask[:], a["c_mask"]), (rope_cos[:], a["c_rope_cos"]), (rope_sin[:], a["c_rope_sin"]),
                  (key_cos[:], a["c_key_cos"]), (key_sin[:], a["c_key_sin"])]
        for dst, name in ((qn_rows, "q_norm_w"), (kvn_rows, "kv_norm_w"), (bo_rows, "bo"), (bias_rows, "ffn_bias")):
            consts.append((dst[:], a[name].partition_broadcast(P)))
        assert len(consts) == N_CONSTS
        for dst, src in consts:
            sp.dma_start(dst, src).then_inc(ld["consts_in"], 16)
        wqb = a["Wq_b"].rearrange("(k p) n -> p k n", p=KQ)
        for k in range(2):
            sp.dma_start(wqb_raw[:, k, :], wqb[:, k, :]).then_inc(ld["wqb_in"], 16)
        sp.dma_start(wkvb_raw[:], a["Wkv_b"]).then_inc(ld["wkvb_in"], 16)
        sp.dma_start(wo_raw[:], a["Wo0"].rearrange("(h p) n -> p h n", p=P)).then_inc(ld["wo0_in"], 16)
        sp.wait_ge(ln["y_done"], NT)
        sp.dma_start(gate_raw[:], a["gate_w"]).then_inc(ld["gate_in"], 16)
        sp.dma_start(rank[:], a["c_rank"]).then_inc(ld["gate_in"], 16)
        gate_up = a["gate_up"].rearrange("e (k p) f -> p e k f", p=P)
        down_w = a["down"].rearrange("e p n -> p e n")

        def load_expert(e, par):
            sp.dma_start(wgu_raw[:, par, :].rearrange("p (k f) -> p k f", k=KD),
                         gate_up[:, e, :, :]).then_inc(expert_in[par], 16)
            sp.dma_start(wdn_raw[:, par, :], down_w[:, e, :]).then_inc(expert_in[par], 16)

        def load_comb(e, par):
            sp.dma_start(comb_rows[:, par, :], comb_dram[e, :].partition_broadcast(P)).then_inc(comb_in[par], 16)

        load_expert(0, 0)
        load_expert(1, 1)
        sp.dma_start(wq1_raw[:], a["Wq1"].rearrange("(k p) n -> p k n", p=P)).then_inc(ld["wq1_in"], 16)
        sp.dma_start(wk_raw[:], a["Wk1"].rearrange("(k p) n -> p k n", p=P)).then_inc(ld["wkv1_in"], 16)
        sp.dma_start(wv_raw[:], a["Wv1"].rearrange("(k p) n -> p k n", p=P)).then_inc(ld["wkv1_in"], 16)
        sp.dma_start(wo_full[:], a["Wo1"].rearrange("(h p) n -> p h n", p=P)).then_inc(ld["wo1_in"], 16)
        sp.wait_ge(mo["combT_copied"], 1)
        sp.dma_start(comb_dram, p_rows[:]).then_inc(ld["comb_out"], 16)
        sp.wait_ge(ld["comb_out"], 16)
        load_comb(0, 0)
        load_comb(1, 1)
        with sp.Fori(1, E // 2) as i:
            for par in range(2):
                e = 2 * i + par
                sp.wait_ge(mo["gu_lo"], e - 1)
                sp.wait_ge(mo["dn_lo"], e - 1)
                sp.dma_start(wgu_raw[:, par, :].rearrange("p (k f) -> p k f", k=KD),
                             gate_up[:, bass.ds(e, 1), :, :].rearrange("p e k f -> p (e k) f"))\
                  .then_inc(expert_in[par], 16)
                sp.dma_start(wdn_raw[:, par, :],
                             down_w[:, bass.ds(e, 1), :].rearrange("p e n -> p (e n)")).then_inc(expert_in[par], 16)
                sp.wait_ge(mo["weighted"], 2 * e - 2)
                sp.dma_start(comb_rows[:, par, :],
                             comb_dram[bass.ds(e, 1), :].rearrange("e n -> (e n)").partition_broadcast(P))\
                  .then_inc(comb_in[par], 16)
        sp.wait_ge(at1["probsT_done"], 4 * PAIRS)
        sp.dma_start(ffn_w, a["ffn_w"].rearrange("(o p) n -> p o n", p=P)).then_inc(ld["ffn_in"], 16)
        for b in range(B):
            sp.wait_ge(ln["x_new"], 3 * NT + 2 * b + 2)
            sp.dma_start(out_dram[:, 2 * b:2 * b + 2, :], x_tok[:, 2 * b:2 * b + 2, :]).then_inc(ld["stored"], 16)
        sp.wait_ge(ld["stored"], 16 * B)


_NAMES = dict(
    x="L0_attn_hidden_states", Wq_a="L0_attn_Wq_a", q_norm_w="L0_attn_q_norm_w", Wq_b="L0_attn_Wq_b",
    Wk_rope="L0_attn_Wk_rope", Wkv_a="L0_attn_Wkv_a", kv_norm_w="L0_attn_kv_norm_w", Wkv_b="L0_attn_Wkv_b",
    Wo0="L0_attn_Wo", gate_w="L0_ffn_gate_w", gate_up="L0_ffn_gate_up_proj", down="L0_ffn_down_proj",
    Wq1="L1_attn_Wq", Wk1="L1_attn_Wk", Wv1="L1_attn_Wv", Wo1="L1_attn_Wo", bo="L1_attn_bo",
    ffn_w="L1_ffn_weight", ffn_bias="L1_ffn_bias")


def kernel(**inputs):
    import concourse.bacc as bacc
    from concourse.bass_utils import run_bass_kernel_spmd

    nc = bacc.Bacc("TRN2", target_bir_lowering=False, num_devices=1)
    arrays = {f"in_{k}": np.ascontiguousarray(inputs[name]) for k, name in _NAMES.items()}
    arrays.update({f"in_{k}": v for k, v in shape_constants().items()})
    aps = {k[3:]: nc.dram_tensor(k, v.shape, mybir.dt.from_np(v.dtype), kind="ExternalInput").ap()
           for k, v in arrays.items()}
    out = nc.dram_tensor("out_0", (B, T, D), F32, kind="ExternalOutput").ap()
    program(nc, aps, out)
    return run_bass_kernel_spmd(nc, [arrays], core_ids=[0]).results[0]["out_0"]
```

```python
from contextlib import ExitStack

import numpy as np

import concourse.bass as bass
from concourse import mybir

F32 = mybir.dt.float32
F32R = mybir.dt.float32r
BF16 = mybir.dt.bfloat16
ALU = mybir.AluOpType
ACT = mybir.ActivationFunctionType
AX_X = mybir.AxisListType.X

P = 128
B, T, D = 4, 256, 256
NT = B * T // P
KD = D // P
H = 16
PAIRS = H // 2
NOPE, ROPE, DV = 128, 64, 128
QL, KVL = 192, 64
KQ = QL // 2
DQ = 128
G = 4
E, FF = 16, 128
LN_EPS, RMS_EPS = 1e-5, 1e-6
NEG = -1e30
ROUTE_STEPS, FFN_STEPS, N_CONSTS = 21, 6, 9
HEAD = QL + 2 * KVL
PROJ = QL + KVL + ROPE


def shape_constants():
    pos = np.arange(T, dtype=np.float32)

    def angles(dim):
        inv = (np.float32(1.0) / np.float32(10000.0) ** (np.arange(0, dim, 2, dtype=np.float32) / np.float32(dim)))
        return (pos[:, None] * inv.astype(np.float32)[None, :]).astype(np.float32)

    a0, a1 = angles(ROPE), angles(DQ)
    c0, s0, c1, s1 = (f(a).astype(np.float32) for a in (a0, a1) for f in (np.cos, np.sin))
    one, zero = np.ones((T, KVL), np.float32), np.zeros((T, KVL), np.float32)
    rope_cos = np.stack([np.concatenate([one, c0, c0], 1).T, np.concatenate([c1, c1], 1).T], 1)
    rope_sin = np.stack([np.concatenate([zero, -s0, s0], 1).T, np.concatenate([-s1, s1], 1).T], 1)
    key_cos = np.concatenate([c0, c0], 1).reshape(T // P, P, ROPE).transpose(1, 0, 2)
    key_sin = np.concatenate([-s0, s0], 1).reshape(T // P, P, ROPE).transpose(1, 0, 2)
    later = np.where(np.arange(P)[None, :] > np.arange(P)[:, None], np.float32(NEG), np.float32(0))
    mask = np.concatenate([later, later], 1)

    def parts(x):
        out, rest = [], x.astype(np.float32)
        for _ in range(3):
            hi = ((rest.view(np.uint32) + np.uint32(0x8000)) & np.uint32(0xFFFF0000)).view(np.float32)
            out.append(hi)
            rest = (rest - hi).astype(np.float32)
        return out

    slopes = np.float32(2.0) ** (-np.arange(1, H + 1, dtype=np.float32) * np.float32(8.0) / np.float32(H))
    slopes = slopes.astype(np.float32)
    key_rows = parts((slopes[:, None] * pos[None, :]).astype(np.float32))
    key_rows += parts(np.ascontiguousarray(np.broadcast_to(-slopes[:, None], (H, T))))
    alibi_keys = np.stack(key_rows, 0)
    alibi_queries = np.stack([np.ones(T, np.float32)] * 3 + [pos] * 3, 0)
    rank = np.broadcast_to(np.float32(E) - np.arange(E, dtype=np.float32), (P, E))
    out = dict(c_ident=np.eye(P, dtype=np.float32), c_mask=mask, c_rope_cos=rope_cos, c_rope_sin=rope_sin,
               c_key_cos=key_cos, c_key_sin=key_sin, c_alibi_keys=alibi_keys, c_alibi_queries=alibi_queries,
               c_rank=rank)
    return {k: np.ascontiguousarray(v, dtype=np.float32) for k, v in out.items()}


def raw(ap):
    return ap.bitcast(F32)


def program(nc, a, out):
    with ExitStack() as ctx:
        build(nc, a, out, ctx)


def build(nc, a, out, ctx):
    def sb(name, shape, dt=F32, stack=ctx):
        return stack.enter_context(nc.sbuf_tensor(name, shape, dt))

    def sem(name):
        return ctx.enter_context(nc.semaphore(name))

    def sems(prefix, names):
        return dict(**{n: sem(f"{prefix}_{n}") for n in names.split()})

    x_tok = sb("x_tok", [P, NT, D])
    ident = sb("ident", [P, P])
    ident_bf = sb("ident_bf", [P, P], BF16)
    mask = sb("mask", [P, 2 * P])
    mask_bf = sb("mask_bf", [P, 2 * P], BF16)
    rope_cos = sb("rope_cos", [P, 2, T])
    rope_sin = sb("rope_sin", [P, 2, T])
    bo_rows = sb("bo_rows", [P, D])
    bias_rows = sb("bias_rows", [P, D])
    alibi_keys = sb("alibi_keys", [6, H, T], BF16)
    alibi_queries = sb("alibi_queries", [6, T], BF16)
    moments = sb("moments", [P, NT, 2])
    bn_out = sb("bn_out", [P, NT, 6])
    square_sum = sb("square_sum", [P, 2, NT])
    var_eps = sb("var_eps", [P, 2, NT])
    deviation = sb("deviation", [P, 2, NT])
    inv_dev = sb("inv_dev", [P, 2, NT])
    xT_hi = sb("xT_hi", [P, KD, B * T], F32R)
    xT_lo = sb("xT_lo", [P, KD, B * T], F32R)
    w_hi = sb("w_hi", [P, 2, 512], F32R)
    w_lo = sb("w_lo", [P, 2, 512], F32R)
    wq_full = sb("wq_full", [P, KD, H * P])
    wo_full = sb("wo_full", [P, H, D])
    keysT = sb("keysT", [P, G, B * T])
    v_head = sb("v_head", [P, 2, 2, DV])
    qT = sb("qT", [P, 2, B * T])
    swapped = sb("swapped", [P, 2, 2 * T])
    probs = sb("probs", [P, 2, 2, 3 * P])
    probsT = sb("probsT", [P, 2, 2, 3 * P])
    row_max = sb("row_max", [P, 2, 4])
    neg_max = sb("neg_max", [P, 2, 4])
    row_sum = sb("row_sum", [P, 2, 4])
    inv_sum = sb("inv_sum", [P, 2, 4])
    bank = ctx.enter_context(nc.psum_tensor("bank", [P, 8, 512], F32))

    with ExitStack() as early:
        latT_hi = sb("latT_hi", [P, 2, B * T], F32R, early)
        latT_lo = sb("latT_lo", [P, 2, B * T], F32R, early)
    v_tok = sb("v_tok", [P, NT, G * DV])
    with ExitStack() as setup:
        wqb_raw = sb("wqb_raw", [KQ, 2, H * (NOPE + ROPE)], F32, setup)
        wkvb_raw = sb("wkvb_raw", [KVL, H * (NOPE + DV)], F32, setup)
        wo_raw = sb("wo_raw", [P, H, D], F32, setup)
        qn_rows = sb("qn_rows", [P, QL], F32, setup)
        kvn_rows = sb("kvn_rows", [P, KVL], F32, setup)
        key_cos = sb("key_cos", [P, 2, ROPE], F32, setup)
        key_sin = sb("key_sin", [P, 2, ROPE], F32, setup)
        wa_raw = sb("wa_raw", [P, KD, PROJ], F32, setup)
    with ExitStack() as layer0:
        ctxT0 = sb("ctxT0", [P, PAIRS, B * T], F32, layer0)
    with ExitStack() as moe:
        wq1_raw = sb("wq1_raw", [P, KD, H * DQ], F32, moe)
        comb_rows = sb("comb_rows", [P, 2, B * T], F32, moe)
        silu = sb("silu", [P, 2, 512], F32, moe)
        weighted = sb("weighted", [P, 2, 512], F32, moe)
        gate_raw = sb("gate_raw", [E, D], F32, moe)
        gate_hi = sb("gate_hi", [P, KD, P], F32R, moe)
        gate_lo = sb("gate_lo", [P, KD, P], F32R, moe)
        p_rows = sb("p_rows", [E, B * T], F32, moe)
        p_tok = sb("p_tok", [P, NT, E], F32, moe)
        rank = sb("rank", [P, E], F32, moe)
        chosen = sb("chosen", [P, 2, NT, E], F32, moe)
        scratch = sb("scratch", [P, NT, E], F32, moe)
        best = sb("best", [P, 6, NT], F32, moe)
        wgu_raw = sb("wgu_raw", [P, 2, KD * 2 * FF], F32, moe)
        wdn_raw = sb("wdn_raw", [P, 2, D], F32, moe)
        wdn_hi = sb("wdn_hi", [P, 2, D], F32R, moe)
        wdn_lo = sb("wdn_lo", [P, 2, D], F32R, moe)
        zeros_bf = sb("zeros_bf", [P, 512], BF16, moe)
        wk_raw = sb("wk_raw", [P, KD, G * DQ], F32, moe)
        wv_raw = sb("wv_raw", [P, KD, G * DV], F32, moe)
    ctxT1 = sb("ctxT1", [P, H, B * T])
    qlat_tok = qT[:].rearrange("p h t -> p (h t)")[:, 0:NT * QL].rearrange("p (t f) -> p t f", f=QL)
    key_tok = keysT[:, 1, :].rearrange("p (t f) -> p t f", f=P)
    key_part = swapped[:].rearrange("p a b -> p (a b)")[:, 0:NT * ROPE].rearrange("p (t f) -> p t f", f=ROPE)
    headT = probs[:].rearrange("p a h n -> p (a h n)")[:, 0:4 * HEAD].rearrange("p (a n) -> p a n", a=4)
    squares = probsT[:].rearrange("p a h n -> p (a h n)")[:, 0:NT * QL].rearrange("p (t n) -> p t n", n=QL)
    key_sq = v_head[:].rearrange("p a t n -> p (a t n)").rearrange("p (t n) -> p t n", n=KVL)
    wv_hi = comb_rows[:, 0, :].bitcast(F32R).rearrange("p (k n) -> p k n", k=KD)
    wv_lo = comb_rows[:, 1, :].bitcast(F32R).rearrange("p (k n) -> p k n", k=KD)
    ffn_w = probs[:].rearrange("p a h n -> p (a h n)")[:, 0:2 * D].rearrange("p (a n) -> p a n", a=2)
    ffn_bw = probsT[:].rearrange("p a h n -> p (a h n)")[:, 0:2 * D].rearrange("p (a n) -> p a n", a=2)
    comb_dram = nc.dram_tensor("comb_dram", (E, B * T), F32, kind="Internal").ap()
    x_dram = a["x"].rearrange("b (j p) d -> p (b j) d", p=P)
    out_dram = out.rearrange("b (j p) d -> p (b j) d", p=P)

    x_in = [sem(f"x_in{b}") for b in range(B)]
    expert_in = [sem("expert_in0"), sem("expert_in1")]
    comb_in = [sem("comb_in0"), sem("comb_in1")]
    ld = sems("load", "ident_in consts_in bf_in alibi_in wa_in wqb_in wkvb_in wo0_in gate_in wkv1_in wq1_in wo1_in ffn_in "
              "comb_out stored")
    su = sems("setup", "wa_hi wa_lo proj_done sq_done rms_var rms_sqrt rms_inv latents key_steps latT_done latT_hi_done "
              "latT_lo_done keysT_copied headT_done headT_copied fold_done fold_q_copied fold_o_copied rope_cols")
    ln = sems("norm", "xT_done xT_hi_done xT_lo_done y_done rows_added y_read stats var_ready moments_ready sqrt_done "
              "inv_ready x_new")
    mo = sems("moe", "gateT_done gate_zero gate_hi gate_lo logits_done sigmoid_done p_done step combT_done combT_copied "
              "zeros gu_hi gu_lo dn_hi dn_lo up_done silu_done weighted act act_hi act_lo down_done")
    kv = sems("kv1", "wk_hi wk_lo k_done cos_done swap_done sin_done k_ready wv_hi wv_lo v_done v_copied wq_perm")
    ff = sems("ffn", "abs_done step bwT_done bw_hi bw_lo")

    def attention(name, layer):
        names = ("w_hi_done w_lo_done q_done cos_done swap_done sin_done q_ready scores_done max_step max_ready "
                 "capped masked exp_done inv_ready probs_ready probsT_done probsT_copied v_copied ctx_done "
                 "ctx_copied").split()
        return dict(layer=layer, **{n: sem(f"{name}_{n}") for n in names})

    at0, at1 = attention("a0", 0), attention("a1", 1)

    def scores_of(par):
        return bank[:, 2 * par:2 * par + 2, 0:3 * P]

    probsT_bank = bank[:, 4:6, 0:3 * P]
    CTX, QRY = 6, 7

    def query_bank(p, b):
        return 4 + b if isinstance(p, int) and p == 0 and b < 2 else QRY

    def xT_bank(turn, b):
        return b if turn == 0 else 4 + b

    def perm_in(x, k, heads):
        return x[:, k, :].rearrange("p (h j e) -> p h e j", h=heads, e=2)

    def perm_out(x, k):
        return x[:, k, :].rearrange("p (h e j) -> p h e j", e=2, j=DQ // 2)

    def steps(eng, body):
        def pair(p, first, more):
            for b in range(B):
                body(p, b, 4 * p + b, (lambda k, b=b: not first or b >= k), True, more)

        pair(0, True, True)
        with eng.Fori(1, PAIRS - 1) as p:
            pair(p, False, True)
        pair(PAIRS - 1, False, False)
        for b in range(3):
            body(PAIRS, b, 4 * PAIRS + b, (lambda k, b=b: k > b), False, False)

    def ahead(p, b, more):
        if b == 0:
            return p, B - 1
        return (p + 1, b - 1) if more else None

    def back(p, b, k):
        return (p, b - k) if b >= k else (p - 1, b - k + B)

    def three_pass(eng, dst, s_hi, s_lo, m_hi, m_lo, start, stop):
        eng.matmul(dst, s_hi, m_hi, start=start, stop=False, skip_group_check=True)
        eng.matmul(dst, s_hi, m_lo, start=False, stop=False, skip_group_check=True)
        return eng.matmul(dst, s_lo, m_hi, start=False, stop=stop, skip_group_check=True)

    def pe_transpose_x(eng, turn, b):
        if turn == 0:
            eng.wait_ge(x_in[b], 16)
            if b == 0:
                eng.wait_ge(ld["ident_in"], 16)
        else:
            eng.wait_ge(ln["x_new"], NT * (turn - 1) + 2 * b + 2)
        for k in range(KD):
            for j in range(2):
                mm = eng.transpose(bank[:, xT_bank(turn, b), k * T + j * P:k * T + j * P + P],
                                   x_tok[:, 2 * b + j, k * P:k * P + P], ident[:])
        mm.then_inc(ln["xT_done"], 1)

    def pe_project_out(eng, turn, ctxT, parts):
        for t in range(NT):
            if t >= 4:
                eng.wait_ge(ln["y_read"], NT * turn + t - 3)
            for i in range(parts):
                mm = eng.matmul(bank[:, t % 4, 0:D], ctxT[:, i, t * P:t * P + P], wo_full[:, i, :],
                                start=(i == 0), stop=(i == parts - 1))
            mm.then_inc(ln["y_done"], 1)
            if t >= 3 and t % 2:
                pe_transpose_x(eng, turn + 1, (t - 3) // 2)

    def pe_queries(eng, at, p, b):
        m = 4 * p + b
        rows = KQ if at["layer"] == 0 else P
        xh, xl = (latT_hi, latT_lo) if at["layer"] == 0 else (xT_hi, xT_lo)
        if b == 0:
            eng.wait_ge(at["w_hi_done"], p + 1)
            eng.wait_ge(at["w_lo_done"], p + 1)
        if not (isinstance(p, int) and m < 3):
            eng.wait_ge(at["cos_done"], m)
            eng.wait_ge(at["swap_done"], m)
        for h in range(2):
            for k in range(2):
                mm = three_pass(eng, bank[:, query_bank(p, b), h * T:h * T + T],
                                w_hi[0:rows, k, h * P:h * P + P], w_lo[0:rows, k, h * P:h * P + P],
                                xh[0:rows, k, T * b:T * b + T], xl[0:rows, k, T * b:T * b + T],
                                k == 0, k == 1)
        mm.then_inc(at["q_done"], 1)

    def pe_attention(eng, at):
        def body(p, b, n, lag, own, more):
            if own:
                eng.wait_ge(at["q_ready"], n + 1)
                if lag(2):
                    eng.wait_ge(at["exp_done"] if at["layer"] == 0 else at["capped"], n - 1)
                group = 0 if at["layer"] == 0 else p // 2
                for h in range(2):
                    dst = bank[:, 2 * (b % 2) + h, :]
                    q = qT[:, h, T * b:T * b + T]
                    eng.matmul(dst[:, 0:T], q[:, P:T], keysT[:, group, T * b:T * b + T],
                               start=True, stop=False, skip_group_check=True)
                    eng.matmul(dst[:, T:T + P], q[:, 0:P], keysT[:, group, T * b:T * b + P],
                               start=False, stop=False, skip_group_check=True)
                    if at["layer"] == 0:
                        mm = eng.matmul(dst[:, P:3 * P], ident_bf[:], mask_bf[:],
                                        start=False, stop=True, skip_group_check=True)
                    else:
                        eng.matmul(dst[:, 0:T], alibi_queries[:, P:T], alibi_keys[:, 2 * p + h, :],
                                   start=False, stop=False, skip_group_check=True)
                        mm = eng.matmul(dst[:, T:T + P], alibi_queries[:, 0:P], alibi_keys[:, 2 * p + h, 0:P],
                                        start=False, stop=True, skip_group_check=True)
                mm.then_inc(at["scores_done"], 1)
            if own and ahead(p, b, more):
                pe_queries(eng, at, *ahead(p, b, more))
            if lag(1):
                eng.wait_ge(at["probs_ready"], n)
                if lag(2):
                    eng.wait_ge(at["probsT_copied"], n - 1)
                for h in range(2):
                    pr = probs[:, (b - 1) % 2, h, :]
                    dst = probsT_bank[:, h, :]
                    eng.transpose(dst[:, 0:P], pr[:, T:T + P], ident[:])
                    eng.transpose(dst[:, P:T], pr[:, 0:P], ident[:])
                    mm = eng.transpose(dst[:, T:T + P], pr[:, P:T], ident[:])
                mm.then_inc(at["probsT_done"], 1)
            if lag(2):
                b2 = (b - 2) % B
                eng.wait_ge(at["probsT_copied"], n - 1)
                if lag(3):
                    eng.wait_ge(at["ctx_copied"], n - 2)
                if at["layer"] == 1:
                    eng.wait_ge(at["v_copied"], n - 1)
                for h in range(2):
                    pt = probsT[:, b % 2, h, :]
                    if at["layer"] == 0:
                        dst = bank[64 * h:64 * h + 64, CTX, 0:T]
                        values = [key_tok[:, (2 * b2 + j + 4) % NT, 0:KVL] for j in range(2)]
                    else:
                        dst = bank[:, CTX, T * h:T * h + T]
                        values = [v_head[:, b % 2, j, :] for j in range(2)]
                    eng.matmul(dst, values[0], pt[:, 0:T], start=True, stop=False, skip_group_check=True)
                    mm = eng.matmul(dst[:, P:T], values[1], pt[:, T:T + P],
                                    start=False, stop=True, skip_group_check=True)
                mm.then_inc(at["ctx_done"], 1)

        steps(eng, body)

    def pe_first_queries(eng, at):
        for b in range(B - 1):
            pe_queries(eng, at, 0, b)

    block = ctx.enter_context(nc.Block())

    @block.tensor
    def _(pe):
        for b in range(B):
            pe_transpose_x(pe, 0, b)
        pe.wait_ge(su["wa_hi"], 1)
        pe.wait_ge(su["wa_lo"], 1)
        for t in range(NT):
            need = max(t // 2 + 1, t - 3)
            pe.wait_ge(ln["xT_hi_done"], need)
            pe.wait_ge(ln["xT_lo_done"], need)
            for k in range(KD):
                mm = three_pass(pe, bank[:, (t + 4) % NT, 0:PROJ],
                                xT_hi[:, k, t * P:t * P + P], xT_lo[:, k, t * P:t * P + P],
                                w_hi[:, k, 0:PROJ], w_lo[:, k, 0:PROJ], k == 0, k == KD - 1)
            mm.then_inc(su["proj_done"], 1)
        pe.wait_ge(su["latents"], 2 * NT)
        pe.wait_ge(su["key_steps"], 4)
        for b in range(B):
            for k in range(2):
                for j in range(2):
                    pe.transpose(bank[0:KQ, b, k * T + j * P:k * T + j * P + P],
                                 qlat_tok[:, 2 * b + j, k * KQ:k * KQ + KQ], ident[:])
            for j in range(2):
                mm = pe.transpose(bank[:, 4 + b, j * P:j * P + P], key_tok[:, (2 * b + j + 4) % NT, :], ident[:])
            mm.then_inc(su["latT_done"], 1)
        pe.wait_ge(su["latT_hi_done"], B)
        pe.wait_ge(su["latT_lo_done"], B)
        pe.wait_ge(su["keysT_copied"], B)
        pe.wait_ge(ld["wqb_in"], 32)
        pe.wait_ge(ld["wkvb_in"], 16)
        for h in range(H + 3):
            if h < H:
                if h >= 4:
                    pe.wait_ge(su["headT_copied"], h - 3)
                dst = bank[:, 4 + h % 4, :]
                for k in range(2):
                    c = h * (NOPE + ROPE)
                    pe.transpose(dst[:, k * KQ:k * KQ + KQ], wqb_raw[:, k, c:c + NOPE], ident[0:KQ, 0:KQ])
                c = h * (NOPE + DV)
                pe.transpose(dst[:, QL:QL + KVL], wkvb_raw[:, c:c + NOPE], ident[0:KVL, 0:KVL])
                pe.transpose(dst[:, QL + KVL:QL + 2 * KVL], wkvb_raw[:, c + NOPE:c + NOPE + DV],
                             ident[0:KVL, 0:KVL]).then_inc(su["headT_done"], 1)
            if h >= 3:
                g = h - 3
                pe.wait_ge(su["headT_copied"], g + 1)
                if g == 0:
                    pe.wait_ge(ld["wo0_in"], 16)
                if g >= 2:
                    pe.wait_ge(su["fold_q_copied"], g - 1)
                if g >= 4 and g % 2 == 0:
                    pe.wait_ge(su["fold_o_copied"], g // 2 - 1)
                ht = headT[:, g % 4, :]
                for k in range(2):
                    pe.matmul(bank[0:KQ, g % 2, k * KVL:k * KVL + KVL], ht[:, k * KQ:k * KQ + KQ],
                              ht[:, QL:QL + KVL], start=True, stop=True)
                r = 64 * (g % 2)
                pe.matmul(bank[r:r + 64, 2 + (g // 2) % 2, 0:D], ht[:, QL + KVL:QL + 2 * KVL], wo_raw[:, g, :],
                          start=True, stop=True).then_inc(su["fold_done"], 1)
        pe.wait_ge(su["fold_q_copied"], H)
        pe.wait_ge(su["fold_o_copied"], PAIRS)
        pe.wait_ge(ld["bf_in"], 32)
        pe_first_queries(pe, at0)
        pe_attention(pe, at0)
        pe.wait_ge(ld["gate_in"], 32)
        for k in range(KD):
            mm = pe.transpose(bank[:, 4, k * E:k * E + E], gate_raw[:, k * P:k * P + P], ident[0:E, 0:E])
        mm.then_inc(mo["gateT_done"], 1)
        pe.wait_ge(mo["gate_hi"], 1)
        pe.wait_ge(mo["gate_lo"], 1)
        pe.wait_ge(at0["ctx_copied"], 4 * PAIRS)
        pe_project_out(pe, 0, ctxT0, PAIRS)
        for j in range(2):
            if j == 1:
                pe_transpose_x(pe, 1, 3)
            pe.wait_ge(ln["xT_hi_done"], B + 2 * j + 2)
            pe.wait_ge(ln["xT_lo_done"], B + 2 * j + 2)
            for k in range(KD):
                mm = three_pass(pe, bank[:, j, :], gate_hi[:, k, :], gate_lo[:, k, :],
                                xT_hi[:, k, 512 * j:512 * j + 512], xT_lo[:, k, 512 * j:512 * j + 512],
                                k == 0, k == KD - 1)
            mm.then_inc(mo["logits_done"], 1)

        def up(e, par, first, j):
            if j == 0:
                pe.wait_ge(mo["gu_hi"], e + 1)
                pe.wait_ge(mo["gu_lo"], e + 1)
            if not first:
                pe.wait_ge(mo["silu_done"], 2 * e + j - 1)
                pe.wait_ge(mo["weighted"], 2 * e + j - 1)
            for half in range(2):
                for k in range(KD):
                    c = k * 2 * FF + half * FF
                    mm = three_pass(pe, bank[:, 4 + 2 * j + half, :],
                                    w_hi[:, par, c:c + FF], w_lo[:, par, c:c + FF],
                                    xT_hi[:, k, 512 * j:512 * j + 512], xT_lo[:, k, 512 * j:512 * j + 512],
                                    k == 0, k == KD - 1)
            mm.then_inc(mo["up_done"], 1)

        def down(e, par, last=False):
            pe.wait_ge(mo["dn_hi"], e + 1)
            pe.wait_ge(mo["dn_lo"], e + 1)
            for j in range(2):
                pe.wait_ge(mo["act_hi"], 2 * e + j + 1)
                pe.wait_ge(mo["act_lo"], 2 * e + j + 1)
                for t in range(4 * j, 4 * j + 4):
                    mm = three_pass(pe, bank[:, t // 2, (t % 2) * D:(t % 2) * D + D],
                                    latT_hi[:, par, t * P:t * P + P], latT_lo[:, par, t * P:t * P + P],
                                    wdn_hi[:, par, :], wdn_lo[:, par, :], False, False)
                    if last and t % 2:
                        mm.then_inc(ln["y_done"], 2)
            if not last:
                mm.then_inc(mo["down_done"], 1)

        up(0, 0, True, 0)
        pe.wait_ge(mo["sigmoid_done"], 2)
        for t in range(NT):
            mm = pe.transpose(bank[:, 2, t * E:t * E + E], p_rows[:, t * P:t * P + P], ident[0:E, 0:E])
        mm.then_inc(mo["p_done"], 1)
        up(0, 0, True, 1)
        up(1, 1, False, 0)
        pe.wait_ge(mo["step"], ROUTE_STEPS)
        for t in range(NT):
            mm = pe.transpose(bank[0:E, t // 4, (t % 4) * P:(t % 4) * P + P], chosen[:, 0, t, :], ident[:])
        mm.then_inc(mo["combT_done"], 1)
        up(1, 1, False, 1)
        pe.wait_ge(mo["zeros"], 1)
        pe.wait_ge(mo["combT_copied"], 1)
        for i in range(4):
            pe.matmul(bank[:, i, :], zeros_bf[:, 0:P], zeros_bf[:], start=True, stop=False, skip_group_check=True)
        down(0, 0)
        with pe.Fori(1, E // 2) as i:
            for par in range(2):
                for j in range(2):
                    up(2 * i + par, par, False, j)
                down(2 * i + par - 1, 1 - par)
        down(E - 1, 1, True)

        pe.wait_ge(kv["wk_hi"], KD)
        pe.wait_ge(kv["wk_lo"], KD)
        for i in range(2 * G):
            j, g = i // G, i % G
            if g == 0:
                pe_transpose_x(pe, 2, 2 * j)
                pe_transpose_x(pe, 2, 2 * j + 1)
                pe.wait_ge(ln["xT_hi_done"], 2 * B + 2 * j + 2)
                pe.wait_ge(ln["xT_lo_done"], 2 * B + 2 * j + 2)
            if i < 4:
                pe.wait_ge(ln["y_read"], NT + 2 * i + 2)
            else:
                pe.wait_ge(kv["cos_done"], i - 3)
                pe.wait_ge(kv["swap_done"], i - 3)
            for k in range(KD):
                mm = three_pass(pe, bank[:, i % 4, :],
                                w_hi[:, k, g * DQ:g * DQ + DQ], w_lo[:, k, g * DQ:g * DQ + DQ],
                                xT_hi[:, k, 512 * j:512 * j + 512], xT_lo[:, k, 512 * j:512 * j + 512],
                                k == 0, k == KD - 1)
            mm.then_inc(kv["k_done"], 1)
        pe.wait_ge(kv["wv_hi"], 1)
        pe.wait_ge(kv["wv_lo"], 1)
        for t in range(NT):
            if t < 4:
                pe.wait_ge(kv["cos_done"], G + t + 1)
                pe.wait_ge(kv["swap_done"], G + t + 1)
            else:
                pe.wait_ge(kv["v_copied"], t - 3)
            if t == 4:
                pe_first_queries(pe, at1)
            for k in range(KD):
                mm = three_pass(pe, bank[:, t % 4, :],
                                xT_hi[:, k, t * P:t * P + P], xT_lo[:, k, t * P:t * P + P],
                                wv_hi[:, k, :], wv_lo[:, k, :], k == 0, k == KD - 1)
            mm.then_inc(kv["v_done"], 1)
        pe.wait_ge(kv["k_ready"], 2 * G)
        pe.wait_ge(kv["v_copied"], NT)
        pe.wait_ge(ld["alibi_in"], 32)
        pe_attention(pe, at1)
        pe.wait_ge(at1["ctx_copied"], 4 * PAIRS)
        pe.wait_ge(ld["wo1_in"], 16)
        pe.wait_ge(ff["step"], FFN_STEPS)
        for o in range(2):
            for k in range(KD):
                mm = pe.transpose(bank[:, 4, k * D + o * P:k * D + o * P + P], ffn_bw[:, o, k * P:k * P + P],
                                  ident[:])
        mm.then_inc(ff["bwT_done"], 1)
        pe.wait_ge(ff["bw_hi"], 1)
        pe.wait_ge(ff["bw_lo"], 1)
        pe_project_out(pe, 2, ctxT1, H)
        for t in range(NT):
            if t == 2:
                pe_transpose_x(pe, 3, 3)
            pe.wait_ge(ln["xT_hi_done"], 3 * B + t // 2 + 1)
            pe.wait_ge(ln["xT_lo_done"], 3 * B + t // 2 + 1)
            pe.wait_ge(ln["y_read"], 2 * NT + 4 + t + 1 if t < 4 else 3 * NT + t - 3)
            for k in range(KD):
                mm = three_pass(pe, bank[:, t % 4, 0:D],
                                xT_hi[:, k, t * P:t * P + P], xT_lo[:, k, t * P:t * P + P],
                                w_hi[:, k, 0:D], w_lo[:, k, 0:D], k == 0, k == KD - 1)
            mm.then_inc(ln["y_done"], 1)

    def act_split_x(act, turn, b):
        act.wait_ge(ln["xT_done"], B * turn + b + 1)
        act.activation(xT_hi[:, :, T * b:T * b + T],
                       bank[:, xT_bank(turn, b), :].rearrange("p (k t) -> p k t", k=KD),
                       ACT.Copy).then_inc(ln["xT_hi_done"], 1)

    def act_sqrt(act, turn, b):
        act.wait_ge(ln["var_ready"], B * turn + b + 1)
        act.activation(deviation[:, 0, 2 * b:2 * b + 2], var_eps[:, 0, 2 * b:2 * b + 2],
                       ACT.Sqrt).then_inc(ln["sqrt_done"], 1)

    def act_norm_and_split(act, turn):
        for b in range(B):
            act_sqrt(act, turn, b)
            if b >= 1:
                act_split_x(act, turn + 1, b - 1)
        act_split_x(act, turn + 1, B - 1)

    def act_split_w(act, at, p):
        rows = KQ if at["layer"] == 0 else P
        if not (isinstance(p, int) and p == 0):
            act.wait_ge(at["q_done"], 4 * p)
        act.activation(w_hi[0:rows, :, 0:2 * P], wq_full[0:rows, :, bass.ds(2 * P * p, 2 * P)],
                       ACT.Copy).then_inc(at["w_hi_done"], 1)

    def act_swap(act, at, p, b):
        m = 4 * p + b
        if at["layer"] == 0:
            act.wait_ge(at["cos_done"], m + 1)
        else:
            act.wait_ge(at["q_done"], m + 1)
        if not (isinstance(p, int) and m < 2):
            act.wait_ge(at["q_ready"], m - 1)
        r0, rn = (64, 32) if at["layer"] == 0 else (0, 64)
        act.activation(swapped[r0:r0 + rn, b % 2, :], bank[r0 + rn:r0 + 2 * rn, query_bank(p, b), :], ACT.Copy)
        act.activation(swapped[r0 + rn:r0 + 2 * rn, b % 2, :], bank[r0:r0 + rn, query_bank(p, b), :],
                       ACT.Copy).then_inc(at["swap_done"], 1)

    def act_attention(act, at):
        scale = (NOPE + ROPE) ** -0.5

        def form_queries(p, b, more):
            if at["layer"] == 0 and b == 0 and more:
                act_split_w(act, at, p + 1)
            if ahead(p, b, more):
                act_swap(act, at, *ahead(p, b, more))
            if at["layer"] == 1 and b == 0 and more:
                act_split_w(act, at, p + 1)

        def body(p, b, n, lag, own, more):
            par = b % 2
            if own and at["layer"] == 1:
                act.wait_ge(at["scores_done"], n + 1)
                if lag(2):
                    act.wait_ge(at["probsT_done"], n - 1)
                act.activation(probs[:, par, :, :], scores_of(par), ACT.Tanh,
                               scale=DQ ** -0.5 / 30.0).then_inc(at["capped"], 1)
                form_queries(p, b, more)
            if own:
                if at["layer"] == 0:
                    act.wait_ge(at["max_ready"], n + 1)
                    if lag(2):
                        act.wait_ge(at["probsT_done"], n - 1)
                else:
                    act.wait_ge(at["masked"], n + 1)
                for h in range(2):
                    for tile, c0, c1 in ((0, 0, T), (1, T, T + P)):
                        i = 2 * tile + h
                        if at["layer"] == 0:
                            ins = act.activation(probs[:, par, h, c0:c1], bank[:, 2 * par + h, c0:c1], ACT.Exp,
                                                 bias=neg_max[:, par, i:i + 1], scale=scale,
                                                 accum_out=row_sum[:, par, i:i + 1])
                        else:
                            ins = act.activation(probs[:, par, h, c0:c1], probs[:, par, h, c0:c1], ACT.Exp,
                                                 scale=30.0, accum_out=row_sum[:, par, i:i + 1])
                ins.then_inc(at["exp_done"], 1)
            if own and at["layer"] == 0:
                form_queries(p, b, more)
            if lag(1) and at["layer"] == 0:
                act.wait_ge(at["probsT_done"], n)
                if lag(3):
                    act.wait_ge(at["ctx_done"], n - 2)
                act.activation(probsT[:, (b - 1) % 2, :, :], probsT_bank, ACT.Copy).then_inc(at["probsT_copied"], 1)

        steps(act, body)

    def act_first_queries(act, at):
        for b in range(B - 1):
            act_swap(act, at, 0, b)

    @block.scalar
    def _(act):
        act.wait_ge(ld["wa_in"], 48)
        act.activation(w_hi[:, :, 0:PROJ], wa_raw[:], ACT.Copy).then_inc(su["wa_hi"], 1)
        for b in range(B):
            act_split_x(act, 0, b)
        for t in range(NT):
            act.wait_ge(su["proj_done"], t + 1)
            src = bank[:, (t + 4) % NT, :]
            act.activation(squares[:, t, :], src[:, 0:QL], ACT.Square,
                           accum_out=square_sum[:, 0, t:t + 1]).then_inc(su["sq_done"], 1)
            act.activation(key_sq[:, t, :], src[:, QL:QL + KVL], ACT.Square,
                           accum_out=square_sum[:, 1, t:t + 1]).then_inc(su["sq_done"], 1)
        act.wait_ge(su["rms_var"], 2)
        act.activation(deviation[:], var_eps[:], ACT.Sqrt).then_inc(su["rms_sqrt"], 1)
        for b in range(B):
            act.wait_ge(su["latT_done"], b + 1)
            act.activation(latT_hi[0:KQ, :, T * b:T * b + T], bank[0:KQ, b, :].rearrange("p (k t) -> p k t", k=2),
                           ACT.Copy).then_inc(su["latT_hi_done"], 1)
            act.activation(keysT[:, 0, T * b:T * b + T], bank[:, 4 + b, 0:T],
                           ACT.Copy).then_inc(su["keysT_copied"], 1)
        for h in range(H):
            if h == 8:
                act.wait_ge(su["rope_cols"], 2)
                act.wait_ge(su["fold_q_copied"], 2)
                act_split_w(act, at0, 0)
            act.wait_ge(su["headT_done"], h + 1)
            if h >= 4:
                act.wait_ge(su["fold_done"], h - 3)
            act.activation(headT[:, h % 4, :], bank[:, 4 + h % 4, 0:QL + 2 * KVL],
                           ACT.Copy).then_inc(su["headT_copied"], 1)
        act.wait_ge(su["fold_q_copied"], H)
        act_first_queries(act, at0)
        act_attention(act, at0)
        act.wait_ge(mo["gateT_done"], 1)
        act.wait_ge(mo["gate_zero"], 2)
        act.activation(gate_hi[:, :, 0:E], bank[:, 4, 0:KD * E].rearrange("p (k e) -> p k e", k=KD),
                       ACT.Copy).then_inc(mo["gate_hi"], 1)
        def gate_up_hi(e, par, i, first):
            act.wait_ge(expert_in[par], 32 * (i + 1))
            if not first:
                act.wait_ge(mo["up_done"], 2 * e - 2)
            act.activation(w_hi[:, par, :], wgu_raw[:, par, :], ACT.Copy).then_inc(mo["gu_hi"], 1)

        def down_hi(e, par, first):
            if not first:
                act.wait_ge(mo["down_done"], e - 1)
            act.activation(wdn_hi[:, par, :], wdn_raw[:, par, :], ACT.Copy).then_inc(mo["dn_hi"], 1)

        def activations(e, par, first):
            for j in range(2):
                act.wait_ge(mo["up_done"], 2 * e + j + 1)
                if not first:
                    act.wait_ge(mo["act_lo"], 2 * e + j - 1)
                act.activation(silu[:, j, :], bank[:, 4 + 2 * j, :], ACT.Silu).then_inc(mo["silu_done"], 1)
            if first:
                act.wait_ge(mo["combT_done"], 1)
                act.activation(p_rows[:].rearrange("e (a n) -> e a n", a=2), bank[0:E, 0:2, :],
                               ACT.Copy).then_inc(mo["combT_copied"], 1)
            for j in range(2):
                act.wait_ge(mo["act"], 2 * e + j + 1)
                if j == 0 and not first:
                    act.wait_ge(mo["down_done"], e - 1)
                act.activation(latT_hi[:, par, 512 * j:512 * j + 512], silu[:, j, :],
                               ACT.Copy).then_inc(mo["act_hi"], 1)

        act.wait_ge(at0["q_done"], 4 * PAIRS)
        gate_up_hi(0, 0, 0, True)
        down_hi(0, 0, True)
        gate_up_hi(1, 1, 0, True)
        down_hi(1, 1, True)
        act_norm_and_split(act, 0)
        for j in range(2):
            act.wait_ge(mo["logits_done"], j + 1)
            act.activation(p_rows[:, 512 * j:512 * j + 512], bank[0:E, j, :],
                           ACT.Sigmoid).then_inc(mo["sigmoid_done"], 1)
        activations(0, 0, True)
        with act.Fori(1, E // 2) as i:
            gate_up_hi(2 * i, 0, i, False)
            activations(2 * i - 1, 1, False)
            down_hi(2 * i, 0, False)
            gate_up_hi(2 * i + 1, 1, i, False)
            activations(2 * i, 0, False)
            down_hi(2 * i + 1, 1, False)
        activations(E - 1, 1, False)

        act.wait_ge(ld["wkv1_in"], 32)
        act.wait_ge(mo["up_done"], 2 * E)
        for k in range(KD):
            act.activation(perm_out(w_hi, k), perm_in(wk_raw, k, G), ACT.Copy).then_inc(kv["wk_hi"], 1)
        act.wait_ge(mo["act"], 2 * E)
        act.activation(wv_hi, wv_raw[:], ACT.Copy).then_inc(kv["wv_hi"], 1)
        act_norm_and_split(act, 1)
        for i in range(2 * G):
            act.wait_ge(kv["k_done"], i + 1)
            if i >= 2:
                act.wait_ge(kv["k_ready"], i - 1)
            act.activation(swapped[0:64, i % 2, :], bank[64:P, i % 4, :], ACT.Copy)
            act.activation(swapped[64:P, i % 2, :], bank[0:64, i % 4, :], ACT.Copy).then_inc(kv["swap_done"], 1)
        act.wait_ge(kv["wq_perm"], H)
        act_split_w(act, at1, 0)
        for t in range(NT):
            if t == 4:
                act.wait_ge(kv["k_ready"], 2 * G)
                act_first_queries(act, at1)
            act.wait_ge(kv["v_done"], t + 1)
            act.activation(v_tok[:, t, :], bank[:, t % 4, :], ACT.Copy).then_inc(kv["v_copied"], 1)
        act_attention(act, at1)
        act.wait_ge(ld["ffn_in"], 16)
        act.wait_ge(at1["ctx_done"], 4 * PAIRS)
        for o in range(2):
            act.activation(ffn_bw[:, o, :], ffn_w[:, o, :], ACT.Abs,
                           accum_out=square_sum[:, 0, o:o + 1]).then_inc(ff["abs_done"], 1)
        act.wait_ge(ff["bwT_done"], 1)
        act.activation(w_hi[:, :, 0:D], bank[:, 4, :].rearrange("p (k o) -> p k o", k=KD),
                       ACT.Copy).then_inc(ff["bw_hi"], 1)
        act_norm_and_split(act, 2)
        for b in range(B):
            act_sqrt(act, 3, b)

    def dve_split_x(dve, turn, b):
        dve.wait_ge(ln["xT_hi_done"], B * turn + b + 1)
        sl = (slice(None), slice(None), slice(T * b, T * b + T))
        dve.tensor_tensor(xT_lo[sl], bank[:, xT_bank(turn, b), :].rearrange("p (k t) -> p k t", k=KD),
                          raw(xT_hi[sl]), ALU.subtract).then_inc(ln["xT_lo_done"], 1)

    def dve_layer_norm(dve, turn, y_of):
        for b in range(B):
            if turn >= 2:
                dve.wait_ge(ln["rows_added"], B * (turn - 2) + b + 1)
            for t in (2 * b, 2 * b + 1):
                dve.wait_ge(ln["y_done"], NT * turn + t + 1)
                dve.tensor_tensor(x_tok[:, t, :], y_of(t), x_tok[:, t, :], ALU.add).then_inc(ln["y_read"], 1)
                dve.wait_ge(ln["y_read"], NT * turn + t + 1)
                dve.bn_stats(bn_out[:, t, :], x_tok[:, t, :]).then_inc(ln["stats"], 1)
                dve.wait_ge(ln["stats"], NT * turn + t + 1)
                dve.bn_aggr(moments[:, t, :], bn_out[:, t, :]).then_inc(ln["moments_ready"], 1)
            two = slice(2 * b, 2 * b + 2)
            dve.wait_ge(ln["moments_ready"], NT * turn + 2 * b + 2)
            dve.tensor_scalar(var_eps[:, 0, two], moments[:, two, 1], LN_EPS, None,
                              ALU.add).then_inc(ln["var_ready"], 1)
            dve.wait_ge(ln["sqrt_done"], B * turn + b + 1)
            dve.reciprocal(inv_dev[:, 0, two], deviation[:, 0, two]).then_inc(ln["inv_ready"], 1)
            dve.wait_ge(ln["inv_ready"], B * turn + b + 1)
            for t in (2 * b, 2 * b + 1):
                dve.tensor_scalar(x_tok[:, t, :], x_tok[:, t, :], moments[:, t, 0:1], inv_dev[:, 0, t:t + 1],
                                  ALU.subtract, ALU.mult).then_inc(ln["x_new"], 1)
            if turn < 3 and b >= 1:
                dve_split_x(dve, turn + 1, b - 1)
        if turn < 3:
            dve_split_x(dve, turn + 1, B - 1)

    def y_tile(t):
        return bank[:, t % 4, 0:D]

    def dve_split_w(dve, at, p):
        rows = KQ if at["layer"] == 0 else P
        dve.wait_ge(at["w_hi_done"], p + 1)
        dve.tensor_tensor(w_lo[0:rows, :, 0:2 * P], wq_full[0:rows, :, bass.ds(2 * P * p, 2 * P)],
                          raw(w_hi[0:rows, :, 0:2 * P]), ALU.subtract).then_inc(at["w_lo_done"], 1)

    def cos_rows(layer):
        return rope_cos[:, layer:layer + 1, :].broadcast_to([P, 2, T])

    def sin_rows(layer, r0):
        return rope_sin[r0:P, layer:layer + 1, :].broadcast_to([P - r0, 2, T])

    def pair_view(ap):
        return ap.rearrange("p (h t) -> p h t", h=2)

    def dve_cos(dve, at, p, b):
        m = 4 * p + b
        if at["layer"] == 0:
            dve.wait_ge(at["q_done"], m + 1)
        else:
            dve.wait_ge(at["swap_done"], m + 1)
        dve.tensor_tensor(qT[:, :, T * b:T * b + T], pair_view(bank[:, query_bank(p, b), :]), cos_rows(at["layer"]),
                          ALU.mult).then_inc(at["cos_done"], 1)

    def dve_rope_sum(dve, at, p, b):
        m = 4 * p + b
        dve.wait_ge(at["cos_done"], m + 1)
        dve.wait_ge(at["sin_done"], m + 1)
        dve.tensor_tensor(qT[:, :, T * b:T * b + T], qT[:, :, T * b:T * b + T], pair_view(swapped[:, b % 2, :]),
                          ALU.add).then_inc(at["q_ready"], 1)

    def dve_attention(dve, at):
        scale = (NOPE + ROPE) ** -0.5

        def ctx_copy(p, b, k):
            pk, bk = back(p, b, k)
            dve.wait_ge(at["ctx_done"], 4 * p + b - k + 1)
            if at["layer"] == 0:
                dst = ctxT0[:, pk, T * bk:T * bk + T]
                src = bank[:, CTX, 0:T]
            else:
                dst = ctxT1[:, bass.ds(2 * pk, 2), T * bk:T * bk + T]
                src = pair_view(bank[:, CTX, :])
            dve.tensor_copy(dst, src).then_inc(at["ctx_copied"], 1)

        def normalise(m, par):
            dve.wait_ge(at["exp_done"], m + 1)
            dve.reciprocal(inv_sum[:, par, :], row_sum[:, par, :]).then_inc(at["inv_ready"], 1)
            dve.wait_ge(at["inv_ready"], m + 1)
            for h in range(2):
                for tile, c0, c1 in ((0, 0, T), (1, T, T + P)):
                    i = 2 * tile + h
                    ins = dve.tensor_scalar(probs[:, par, h, c0:c1], probs[:, par, h, c0:c1],
                                            inv_sum[:, par, i:i + 1], None, ALU.mult)
            ins.then_inc(at["probs_ready"], 1)

        def body0(p, b, n, lag, own, more):
            par = b % 2
            if own:
                dve.wait_ge(at["scores_done"], n + 1)
                sc = scores_of(par)
                dve.tensor_reduce(row_max[:, par, 0:2], sc[:, :, 0:T], AX_X, ALU.max).then_inc(at["max_step"], 1)
                dve.tensor_reduce(row_max[:, par, 2:4], sc[:, :, T:T + P], AX_X, ALU.max).then_inc(at["max_step"], 1)
                dve.wait_ge(at["max_step"], 2 * n + 2)
                dve.tensor_scalar(neg_max[:, par, :], row_max[:, par, :], -scale, None,
                                  ALU.mult).then_inc(at["max_ready"], 1)
            if own and ahead(p, b, more):
                dve_cos(dve, at, *ahead(p, b, more))
            if b == 0 and more:
                dve_split_w(dve, at, p + 1)
            if own:
                normalise(n, par)
            if lag(2):
                ctx_copy(p, b, 2)

        def body1(p, b, n, lag, own, more):
            par = b % 2
            if lag(3):
                ctx_copy(p, b, 3)
            if lag(1):
                p1, b1 = back(p, b, 1)
                normalise(n - 1, 1 - par)
                if lag(3):
                    dve.wait_ge(at["ctx_done"], n - 2)
                dve.tensor_copy(v_head[:, 1 - par, :, :],
                                v_tok[:, 2 * b1:2 * b1 + 2, bass.ds((p1 // 2) * DV, DV)])\
                   .then_inc(at["v_copied"], 1)
            if own and ahead(p, b, more):
                dve_cos(dve, at, *ahead(p, b, more))
            if b == 0 and more:
                dve_split_w(dve, at, p + 1)
            if lag(1):
                dve.wait_ge(at["probsT_done"], n)
                dve.tensor_copy(probsT[:, 1 - par, :, :], probsT_bank).then_inc(at["probsT_copied"], 1)
            if own and ahead(p, b, more):
                dve_rope_sum(dve, at, *ahead(p, b, more))

        steps(dve, body0 if at["layer"] == 0 else body1)

    def dve_first_queries(dve, at):
        for b in range(B - 1):
            dve_cos(dve, at, 0, b)
            if at["layer"] == 1:
                dve_rope_sum(dve, at, 0, b)

    @block.vector
    def _(dve):
        dve.wait_ge(su["wa_hi"], 1)
        dve.tensor_tensor(w_lo[:, :, 0:PROJ], wa_raw[:], raw(w_hi[:, :, 0:PROJ]),
                          ALU.subtract).then_inc(su["wa_lo"], 1)
        for b in range(B):
            dve_split_x(dve, 0, b)
        dve.wait_ge(ld["consts_in"], 16 * N_CONSTS)
        dve.wait_ge(su["sq_done"], 2 * NT)
        kr = bank[:, :, QL + KVL:PROJ].rearrange("p (b j) f -> p b j f", j=2)
        kp = key_part.rearrange("p (b j) f -> p b j f", j=2)
        kt = key_tok[:, :, KVL:P].rearrange("p (b j) f -> p b j f", j=2)

        def table(x, c0, c1):
            return x[:, :, c0:c1].unsqueeze(1).broadcast_to([P, B, 2, c1 - c0])

        half = ROPE // 2
        dve.tensor_tensor(kt, kr, table(key_cos, 0, ROPE), ALU.mult).then_inc(su["key_steps"], 1)
        dve.tensor_tensor(kp[:, :, :, 0:half], kr[:, :, :, half:ROPE], table(key_sin, 0, half),
                          ALU.mult).then_inc(su["key_steps"], 1)
        dve.tensor_tensor(kp[:, :, :, half:ROPE], kr[:, :, :, 0:half], table(key_sin, half, ROPE),
                          ALU.mult).then_inc(su["key_steps"], 1)
        dve.wait_ge(su["key_steps"], 3)
        dve.tensor_tensor(kt, kt, kp, ALU.add).then_inc(su["key_steps"], 1)
        dve.tensor_scalar(var_eps[:, 0, :], square_sum[:, 0, :], 1.0 / QL, RMS_EPS, ALU.mult,
                          ALU.add).then_inc(su["rms_var"], 1)
        dve.tensor_scalar(var_eps[:, 1, :], square_sum[:, 1, :], 1.0 / KVL, RMS_EPS, ALU.mult,
                          ALU.add).then_inc(su["rms_var"], 1)
        dve.wait_ge(su["rms_sqrt"], 1)
        dve.reciprocal(inv_dev[:], deviation[:]).then_inc(su["rms_inv"], 1)
        dve.wait_ge(su["rms_inv"], 1)
        for t in range(NT):
            src = bank[:, (t + 4) % NT, :]
            dve.scalar_tensor_tensor(out=qlat_tok[:, t, :], in0=src[:, 0:QL], scalar=inv_dev[:, 0, t:t + 1],
                                     in1=qn_rows[:], op0=ALU.mult, op1=ALU.mult).then_inc(su["latents"], 1)
            dve.scalar_tensor_tensor(out=key_tok[:, (t + 4) % NT, 0:KVL], in0=src[:, QL:QL + KVL],
                                     scalar=inv_dev[:, 1, t:t + 1], in1=kvn_rows[:], op0=ALU.mult,
                                     op1=ALU.mult).then_inc(su["latents"], 1)
        for b in range(B):
            dve.wait_ge(su["latT_hi_done"], b + 1)
            sl = (slice(0, KQ), slice(None), slice(T * b, T * b + T))
            dve.tensor_tensor(latT_lo[sl], bank[0:KQ, b, :].rearrange("p (k t) -> p k t", k=2),
                              raw(latT_hi[sl]), ALU.subtract).then_inc(su["latT_lo_done"], 1)
        for h in range(H):
            if h == 6:
                dve_split_w(dve, at0, 0)
            dve.wait_ge(su["fold_done"], h + 1)
            dve.tensor_copy(wq_full[0:KQ, :, h * P:h * P + KVL],
                            bank[0:KQ, h % 2, 0:2 * KVL].rearrange("p (k f) -> p k f", k=2))\
               .then_inc(su["fold_q_copied"], 1)
            if h % 2:
                dve.tensor_copy(wo_full[:, h // 2, :], bank[:, 2 + (h // 2) % 2, 0:D])\
                   .then_inc(su["fold_o_copied"], 1)
        dve_first_queries(dve, at0)
        dve_attention(dve, at0)
        dve.wait_ge(mo["gate_hi"], 1)
        dve.tensor_tensor(gate_lo[:, :, 0:E], bank[:, 4, 0:KD * E].rearrange("p (k e) -> p k e", k=KD),
                          raw(gate_hi[:, :, 0:E]), ALU.subtract).then_inc(mo["gate_lo"], 1)
        dve_layer_norm(dve, 0, y_tile)
        n_step = [0]

        def step(ins):
            n_step[0] += 1
            ins.then_inc(mo["step"], 1)
            dve.wait_ge(mo["step"], n_step[0])

        def wide(col):
            return best[:, col, :].unsqueeze(2).broadcast_to([P, NT, E])

        ranks = rank[:].unsqueeze(1).broadcast_to([P, NT, E])
        dve.wait_ge(ld["gate_in"], 32)
        dve.wait_ge(mo["p_done"], 1)
        p_psum = bank[:, 2, 0:NT * E].rearrange("p (t e) -> p t e", e=E)
        step(dve.tensor_reduce(best[:, 0, :], p_psum, AX_X, ALU.add))
        step(dve.reciprocal(best[:, 1, :], best[:, 0, :]))
        step(dve.tensor_tensor(p_tok[:], p_psum, wide(1), ALU.mult))
        for i in range(2):
            if i == 1:
                for j in range(2):
                    dve.wait_ge(mo["silu_done"], j + 1)
                    dve.tensor_tensor(silu[:, j, :], silu[:, j, :], bank[:, 5 + 2 * j, :],
                                      ALU.mult).then_inc(mo["weighted"], 1)
            step(dve.tensor_reduce(best[:, 2 + i, :], p_tok[:], AX_X, ALU.max))
            step(dve.tensor_tensor(scratch[:], p_tok[:], wide(2 + i), ALU.is_equal))
            step(dve.tensor_tensor(scratch[:], scratch[:], ranks, ALU.mult))
            step(dve.tensor_reduce(best[:, 4, :], scratch[:], AX_X, ALU.max))
            step(dve.tensor_tensor(chosen[:, i, :, :], scratch[:], wide(4), ALU.is_equal))
            if i == 0:
                step(dve.scalar_tensor_tensor(out=p_tok[:], in0=chosen[:, 0, :, :], scalar=-2.0, in1=p_tok[:],
                                              op0=ALU.mult, op1=ALU.add))
        step(dve.tensor_tensor(best[:, 4, :], best[:, 2, :], best[:, 3, :], ALU.add))
        step(dve.reciprocal(best[:, 5, :], best[:, 4, :]))
        for i in range(2):
            step(dve.tensor_tensor(best[:, 2 + i, :], best[:, 2 + i, :], best[:, 5, :], ALU.mult))
            step(dve.tensor_tensor(chosen[:, i, :, :], chosen[:, i, :, :], wide(2 + i), ALU.mult))
        step(dve.tensor_tensor(chosen[:, 0, :, :], chosen[:, 0, :, :], chosen[:, 1, :, :], ALU.add))
        assert n_step[0] == ROUTE_STEPS

        def expert(e, par, i, first):
            dve.wait_ge(comb_in[par], 16 * (i + 1))
            for j in range(2):
                if isinstance(e, int) and e == 0:
                    dve.wait_ge(mo["weighted"], j + 1)
                    dve.tensor_tensor(silu[:, j, :], silu[:, j, :], comb_rows[:, 0, 512 * j:512 * j + 512],
                                      ALU.mult).then_inc(mo["act"], 1)
                    continue
                dve.wait_ge(mo["up_done"], 2 * e + j + 1)
                dve.tensor_tensor(weighted[:, j, :], bank[:, 5 + 2 * j, :], comb_rows[:, par, 512 * j:512 * j + 512],
                                  ALU.mult).then_inc(mo["weighted"], 1)
                dve.wait_ge(mo["silu_done"], 2 * e + j + 1)
                dve.wait_ge(mo["weighted"], 2 * e + j + 1)
                dve.tensor_tensor(silu[:, j, :], silu[:, j, :], weighted[:, j, :], ALU.mult).then_inc(mo["act"], 1)
            for j in range(2):
                dve.wait_ge(mo["act_hi"], 2 * e + j + 1)
                if not first:
                    dve.wait_ge(mo["down_done"], e - 1)
                c = slice(512 * j, 512 * j + 512)
                dve.tensor_tensor(latT_lo[:, par, c], silu[:, j, :], raw(latT_hi[:, par, c]),
                                  ALU.subtract).then_inc(mo["act_lo"], 1)

        expert(0, 0, 0, True)
        expert(1, 1, 0, True)
        with dve.Fori(1, E // 2) as i:
            for par in range(2):
                expert(2 * i + par, par, i, False)

        dve_layer_norm(dve, 1, lambda t: bank[:, t // 2, (t % 2) * D:(t % 2) * D + D])

        for i in range(2 * G):
            j, g = i // G, i % G
            dst = pair_view(keysT[:, g, 512 * j:512 * j + 512])
            dve.wait_ge(kv["swap_done"], i + 1)
            dve.tensor_tensor(dst, pair_view(bank[:, i % 4, :]), cos_rows(1), ALU.mult).then_inc(kv["cos_done"], 1)
            dve.wait_ge(kv["sin_done"], i + 1)
            dve.wait_ge(kv["cos_done"], i + 1)
            dve.tensor_tensor(dst, dst, pair_view(swapped[:, i % 2, :]), ALU.add).then_inc(kv["k_ready"], 1)
        dve_split_w(dve, at1, 0)
        dve_first_queries(dve, at1)
        dve_attention(dve, at1)
        n_step[0] = 0

        def fstep(ins):
            n_step[0] += 1
            ins.then_inc(ff["step"], 1)
            dve.wait_ge(ff["step"], n_step[0])

        dve.wait_ge(ff["abs_done"], 2)
        fstep(dve.tensor_scalar(square_sum[:, 1, 0:2], square_sum[:, 0, 0:2], 1.0 / D, None, ALU.mult))
        fstep(dve.tensor_scalar(ffn_bw, ffn_w, 0.0, 2.0, ALU.is_ge, ALU.mult))
        for o in range(2):
            fstep(dve.tensor_scalar(ffn_bw[:, o, :], ffn_bw[:, o, :], 1.0, square_sum[:, 1, o:o + 1],
                                    ALU.subtract, ALU.mult))
        fstep(dve.tensor_tensor(ffn_bw, ffn_bw, ffn_w, ALU.subtract))
        fstep(dve.tensor_tensor(ffn_bw, ffn_bw, ffn_w, ALU.add))
        assert n_step[0] == FFN_STEPS
        dve.wait_ge(ff["bw_hi"], 1)
        dve.tensor_tensor(w_lo[:, :, 0:D], bank[:, 4, :].rearrange("p (k o) -> p k o", k=KD),
                          raw(w_hi[:, :, 0:D]), ALU.subtract).then_inc(ff["bw_lo"], 1)
        dve_layer_norm(dve, 2, y_tile)
        dve_layer_norm(dve, 3, y_tile)

    def pool_sin(pool, at, p, b):
        m = 4 * p + b
        r0 = 64 if at["layer"] == 0 else 0
        pool.wait_ge(at["swap_done"], m + 1)
        sw = pair_view(swapped[r0:P, b % 2, :])
        pool.tensor_tensor(sw, sw, sin_rows(at["layer"], r0), ALU.mult).then_inc(at["sin_done"], 1)
        if at["layer"] == 0:
            q = qT[r0:P, :, T * b:T * b + T]
            pool.wait_ge(at["cos_done"], m + 1)
            pool.wait_ge(at["sin_done"], m + 1)
            pool.tensor_tensor(q, q, sw, ALU.add).then_inc(at["q_ready"], 1)

    def pool_attention(pool, at):
        def body(p, b, n, lag, own, more):
            if own and at["layer"] == 1:
                pr = probs[:, b % 2, :, P:3 * P]
                pool.wait_ge(at["capped"], n + 1)
                pool.tensor_tensor(pr, pr, mask[:].unsqueeze(1).broadcast_to([P, 2, 2 * P]),
                                   ALU.add).then_inc(at["masked"], 1)
            if own and ahead(p, b, more):
                pool_sin(pool, at, *ahead(p, b, more))

        for b in range(B - 1):
            pool_sin(pool, at, 0, b)
        steps(pool, body)

    @block.gpsimd
    def _(pool):
        pool.dma_start(ident_bf[:], a["c_ident"]).then_inc(ld["bf_in"], 16)
        pool.dma_start(mask_bf[:], a["c_mask"]).then_inc(ld["bf_in"], 16)
        pool.dma_start(alibi_queries[:], a["c_alibi_queries"]).then_inc(ld["alibi_in"], 16)
        pool.dma_start(alibi_keys[:], a["c_alibi_keys"]).then_inc(ld["alibi_in"], 16)
        pool.wait_ge(ld["wqb_in"], 32)
        for k in range(2):
            src = wqb_raw[:, k, :].rearrange("p (h f) -> p h f", h=H)[:, :, NOPE:NOPE + ROPE]
            dst = wq_full[0:KQ, k, :].rearrange("p (h f) -> p h f", h=H)[:, :, KVL:P]
            pool.tensor_copy(dst, src).then_inc(su["rope_cols"], 1)
        pool.wait_ge(ld["consts_in"], 16 * N_CONSTS)
        pool.wait_ge(su["rope_cols"], 2)
        pool.wait_ge(su["fold_done"], H)
        pool.memset(raw(gate_hi[:]), 0.0).then_inc(mo["gate_zero"], 1)
        pool.memset(raw(gate_lo[:]), 0.0).then_inc(mo["gate_zero"], 1)
        pool.memset(zeros_bf[:], 0.0).then_inc(mo["zeros"], 1)
        pool.wait_ge(mo["gate_zero"], 2)
        pool.wait_ge(mo["zeros"], 1)
        pool_attention(pool, at0)
        def low(e, par):
            pool.wait_ge(mo["gu_hi"], e + 1)
            pool.tensor_tensor(w_lo[:, par, :], wgu_raw[:, par, :], raw(w_hi[:, par, :]),
                               ALU.subtract).then_inc(mo["gu_lo"], 1)
            pool.wait_ge(mo["dn_hi"], e + 1)
            pool.tensor_tensor(wdn_lo[:, par, :], wdn_raw[:, par, :], raw(wdn_hi[:, par, :]),
                               ALU.subtract).then_inc(mo["dn_lo"], 1)

        def order_queries(h):
            src = wq1_raw[:, :, bass.ds(h * DQ, DQ)].rearrange("p k (j e) -> p k e j", e=2)
            dst = wq_full[:, :, bass.ds(h * DQ, DQ)].rearrange("p k (e j) -> p k e j", e=2)
            for k in range(KD):
                ins = pool.tensor_copy(dst[:, k], src[:, k])
            ins.then_inc(kv["wq_perm"], 1)

        low(0, 0)
        low(1, 1)
        pool.wait_ge(ld["wq1_in"], 16)
        with pool.Fori(1, E // 2) as i:
            for par in range(2):
                low(2 * i + par, par)
                order_queries(2 * i + par)
        order_queries(0)
        order_queries(1)
        for k in range(KD):
            pool.wait_ge(kv["wk_hi"], k + 1)
            pool.tensor_tensor(perm_out(w_lo, k), perm_in(wk_raw, k, G), raw(perm_out(w_hi, k)),
                               ALU.subtract).then_inc(kv["wk_lo"], 1)
        pool.wait_ge(kv["wv_hi"], 1)
        pool.tensor_tensor(wv_lo, wv_raw[:], raw(wv_hi), ALU.subtract).then_inc(kv["wv_lo"], 1)
        for i in range(2 * G):
            pool.wait_ge(kv["swap_done"], i + 1)
            sw = pair_view(swapped[:, i % 2, :])
            pool.tensor_tensor(sw, sw, sin_rows(1, 0), ALU.mult).then_inc(kv["sin_done"], 1)
        pool_attention(pool, at1)

        def add_rows(turn, rows):
            for b in range(B):
                pool.wait_ge(ln["x_new"], NT * turn + 2 * b + 2)
                pool.wait_ge(ln["xT_done"], B * (turn + 1) + b + 1)
                xb = x_tok[:, 2 * b:2 * b + 2, :]
                pool.tensor_tensor(xb, xb, rows[:].unsqueeze(1).broadcast_to([P, 2, D]),
                                   ALU.add).then_inc(ln["rows_added"], 1)

        pool.wait_ge(ld["consts_in"], 16 * N_CONSTS)
        add_rows(1, bo_rows)
        add_rows(2, bias_rows)

    @block.sync
    def _(sp):
        sp.dma_start(ident[:], a["c_ident"]).then_inc(ld["ident_in"], 16)
        for b in range(B):
            sp.dma_start(x_tok[:, 2 * b:2 * b + 2, :], x_dram[:, 2 * b:2 * b + 2, :]).then_inc(x_in[b], 16)
            if b == 0:
                for name, c0, c1 in (("Wq_a", 0, QL), ("Wkv_a", QL, QL + KVL), ("Wk_rope", QL + KVL, PROJ)):
                    sp.dma_start(wa_raw[:, :, c0:c1],
                                 a[name].rearrange("(k p) n -> p k n", p=P)).then_inc(ld["wa_in"], 16)
        consts = [(mask[:], a["c_mask"]), (rope_cos[:], a["c_rope_cos"]), (rope_sin[:], a["c_rope_sin"]),
                  (key_cos[:], a["c_key_cos"]), (key_sin[:], a["c_key_sin"])]
        for dst, name in ((qn_rows, "q_norm_w"), (kvn_rows, "kv_norm_w"), (bo_rows, "bo"), (bias_rows, "ffn_bias")):
            consts.append((dst[:], a[name].partition_broadcast(P)))
        assert len(consts) == N_CONSTS
        for dst, src in consts:
            sp.dma_start(dst, src).then_inc(ld["consts_in"], 16)
        wqb = a["Wq_b"].rearrange("(k p) n -> p k n", p=KQ)
        for k in range(2):
            sp.dma_start(wqb_raw[:, k, :], wqb[:, k, :]).then_inc(ld["wqb_in"], 16)
        sp.dma_start(wkvb_raw[:], a["Wkv_b"]).then_inc(ld["wkvb_in"], 16)
        sp.dma_start(wo_raw[:], a["Wo0"].rearrange("(h p) n -> p h n", p=P)).then_inc(ld["wo0_in"], 16)
        sp.wait_ge(su["fold_done"], H)
        sp.wait_ge(su["rope_cols"], 2)
        sp.dma_start(gate_raw[:], a["gate_w"]).then_inc(ld["gate_in"], 16)
        sp.dma_start(rank[:], a["c_rank"]).then_inc(ld["gate_in"], 16)
        gate_up = a["gate_up"].rearrange("e (k p) f -> p e k f", p=P)
        down_w = a["down"].rearrange("e p n -> p e n")

        def load_expert(e, par):
            sp.dma_start(wgu_raw[:, par, :].rearrange("p (k f) -> p k f", k=KD),
                         gate_up[:, e, :, :]).then_inc(expert_in[par], 16)
            sp.dma_start(wdn_raw[:, par, :], down_w[:, e, :]).then_inc(expert_in[par], 16)

        def load_comb(e, par):
            sp.dma_start(comb_rows[:, par, :], comb_dram[e, :].partition_broadcast(P)).then_inc(comb_in[par], 16)

        load_expert(0, 0)
        load_expert(1, 1)
        sp.dma_start(wk_raw[:], a["Wk1"].rearrange("(k p) n -> p k n", p=P)).then_inc(ld["wkv1_in"], 16)
        sp.dma_start(wv_raw[:], a["Wv1"].rearrange("(k p) n -> p k n", p=P)).then_inc(ld["wkv1_in"], 16)
        sp.wait_ge(ln["y_done"], NT)
        sp.dma_start(wq1_raw[:], a["Wq1"].rearrange("(k p) n -> p k n", p=P)).then_inc(ld["wq1_in"], 16)
        sp.dma_start(wo_full[:], a["Wo1"].rearrange("(h p) n -> p h n", p=P)).then_inc(ld["wo1_in"], 16)
        sp.wait_ge(mo["combT_copied"], 1)
        sp.dma_start(comb_dram, p_rows[:]).then_inc(ld["comb_out"], 16)
        sp.wait_ge(ld["comb_out"], 16)
        load_comb(0, 0)
        load_comb(1, 1)
        with sp.Fori(1, E // 2) as i:
            for par in range(2):
                e = 2 * i + par
                sp.wait_ge(mo["gu_lo"], e - 1)
                sp.wait_ge(mo["dn_lo"], e - 1)
                sp.dma_start(wgu_raw[:, par, :].rearrange("p (k f) -> p k f", k=KD),
                             gate_up[:, bass.ds(e, 1), :, :].rearrange("p e k f -> p (e k) f"))\
                  .then_inc(expert_in[par], 16)
                sp.dma_start(wdn_raw[:, par, :],
                             down_w[:, bass.ds(e, 1), :].rearrange("p e n -> p (e n)")).then_inc(expert_in[par], 16)
                sp.wait_ge(mo["act"], 2 * e - 2)
                sp.dma_start(comb_rows[:, par, :],
                             comb_dram[bass.ds(e, 1), :].rearrange("e n -> (e n)").partition_broadcast(P))\
                  .then_inc(comb_in[par], 16)
        sp.wait_ge(at1["probsT_done"], 4 * PAIRS)
        sp.dma_start(ffn_w, a["ffn_w"].rearrange("(o p) n -> p o n", p=P)).then_inc(ld["ffn_in"], 16)
        for b in range(B):
            sp.wait_ge(ln["x_new"], 3 * NT + 2 * b + 2)
            sp.dma_start(out_dram[:, 2 * b:2 * b + 2, :], x_tok[:, 2 * b:2 * b + 2, :]).then_inc(ld["stored"], 16)
        sp.wait_ge(ld["stored"], 16 * B)


_NAMES = dict(
    x="L0_attn_hidden_states", Wq_a="L0_attn_Wq_a", q_norm_w="L0_attn_q_norm_w", Wq_b="L0_attn_Wq_b",
    Wk_rope="L0_attn_Wk_rope", Wkv_a="L0_attn_Wkv_a", kv_norm_w="L0_attn_kv_norm_w", Wkv_b="L0_attn_Wkv_b",
    Wo0="L0_attn_Wo", gate_w="L0_ffn_gate_w", gate_up="L0_ffn_gate_up_proj", down="L0_ffn_down_proj",
    Wq1="L1_attn_Wq", Wk1="L1_attn_Wk", Wv1="L1_attn_Wv", Wo1="L1_attn_Wo", bo="L1_attn_bo",
    ffn_w="L1_ffn_weight", ffn_bias="L1_ffn_bias")


def kernel(**inputs):
    import concourse.bacc as bacc
    from concourse.bass_utils import run_bass_kernel_spmd

    nc = bacc.Bacc("TRN2", target_bir_lowering=False, num_devices=1)
    arrays = {f"in_{k}": np.ascontiguousarray(inputs[name]) for k, name in _NAMES.items()}
    arrays.update({f"in_{k}": v for k, v in shape_constants().items()})
    aps = {k[3:]: nc.dram_tensor(k, v.shape, mybir.dt.from_np(v.dtype), kind="ExternalInput").ap()
           for k, v in arrays.items()}
    out = nc.dram_tensor("out_0", (B, T, D), F32, kind="ExternalOutput").ap()
    program(nc, aps, out)
    return run_bass_kernel_spmd(nc, [arrays], core_ids=[0]).results[0]["out_0"]
```

```python
from contextlib import ExitStack

import numpy as np

import concourse.bass as bass
from concourse import mybir

F32 = mybir.dt.float32
F32R = mybir.dt.float32r
BF16 = mybir.dt.bfloat16
ALU = mybir.AluOpType
ACT = mybir.ActivationFunctionType
AX_X = mybir.AxisListType.X

P = 128
B, T, D = 4, 256, 256
NT = B * T // P
KD = D // P
H = 16
PAIRS = H // 2
NOPE, ROPE, DV = 128, 64, 128
QL, KVL = 192, 64
KQ = QL // 2
DQ = 128
G = 4
E, FF = 16, 128
LN_EPS, RMS_EPS = 1e-5, 1e-6
NEG = -1e30
ROUTE_STEPS, FFN_STEPS, N_CONSTS = 21, 6, 9
HEAD = QL + 2 * KVL
PROJ = QL + KVL + ROPE


def shape_constants():
    pos = np.arange(T, dtype=np.float32)

    def angles(dim):
        inv = (np.float32(1.0) / np.float32(10000.0) ** (np.arange(0, dim, 2, dtype=np.float32) / np.float32(dim)))
        return (pos[:, None] * inv.astype(np.float32)[None, :]).astype(np.float32)

    a0, a1 = angles(ROPE), angles(DQ)
    c0, s0, c1, s1 = (f(a).astype(np.float32) for a in (a0, a1) for f in (np.cos, np.sin))
    one, zero = np.ones((T, KVL), np.float32), np.zeros((T, KVL), np.float32)
    rope_cos = np.stack([np.concatenate([one, c0, c0], 1).T, np.concatenate([c1, c1], 1).T], 1)
    rope_sin = np.stack([np.concatenate([zero, -s0, s0], 1).T, np.concatenate([-s1, s1], 1).T], 1)
    key_cos = np.concatenate([c0, c0], 1).reshape(T // P, P, ROPE).transpose(1, 0, 2)
    key_sin = np.concatenate([-s0, s0], 1).reshape(T // P, P, ROPE).transpose(1, 0, 2)
    later = np.where(np.arange(P)[None, :] > np.arange(P)[:, None], np.float32(NEG), np.float32(0))
    mask = np.concatenate([later, later], 1)
    maskT = np.concatenate([later.T, later.T], 1)

    def parts(x):
        out, rest = [], x.astype(np.float32)
        for _ in range(3):
            hi = ((rest.view(np.uint32) + np.uint32(0x8000)) & np.uint32(0xFFFF0000)).view(np.float32)
            out.append(hi)
            rest = (rest - hi).astype(np.float32)
        return out

    slopes = np.float32(2.0) ** (-np.arange(1, H + 1, dtype=np.float32) * np.float32(8.0) / np.float32(H))
    slopes = slopes.astype(np.float32)
    query_rows = parts(np.ascontiguousarray(np.broadcast_to(slopes[:, None], (H, T))))
    query_rows += parts((-slopes[:, None] * pos[None, :]).astype(np.float32))
    alibi_queries = np.stack(query_rows, 0)
    alibi_keys = np.stack([pos] * 3 + [np.ones(T, np.float32)] * 3, 0)
    rank = np.broadcast_to(np.float32(E) - np.arange(E, dtype=np.float32), (P, E))
    out = dict(c_ident=np.eye(P, dtype=np.float32), c_mask=mask, c_maskT=maskT, c_rope_cos=rope_cos, c_rope_sin=rope_sin,
               c_key_cos=key_cos, c_key_sin=key_sin, c_alibi_keys=alibi_keys, c_alibi_queries=alibi_queries,
               c_rank=rank)
    return {k: np.ascontiguousarray(v, dtype=np.float32) for k, v in out.items()}


def raw(ap):
    return ap.bitcast(F32)


def program(nc, a, out):
    with ExitStack() as ctx:
        build(nc, a, out, ctx)


def build(nc, a, out, ctx):
    def sb(name, shape, dt=F32, stack=ctx):
        return stack.enter_context(nc.sbuf_tensor(name, shape, dt))

    def sem(name):
        return ctx.enter_context(nc.semaphore(name))

    def sems(prefix, names):
        return dict(**{n: sem(f"{prefix}_{n}") for n in names.split()})

    x_tok = sb("x_tok", [P, NT, D])
    ident = sb("ident", [P, P])
    ident_bf = sb("ident_bf", [P, P], BF16)
    maskT = sb("maskT", [P, 2 * P])
    mask_bf = sb("mask_bf", [P, 2 * P], BF16)
    rope_cos = sb("rope_cos", [P, 2, T])
    rope_sin = sb("rope_sin", [P, 2, T])
    bo_rows = sb("bo_rows", [P, D])
    bias_rows = sb("bias_rows", [P, D])
    alibi_keys = sb("alibi_keys", [6, T], BF16)
    alibi_queries = sb("alibi_queries", [6, H, T], BF16)
    moments = sb("moments", [P, NT, 2])
    bn_out = sb("bn_out", [P, NT, 6])
    square_sum = sb("square_sum", [P, 2, NT])
    var_eps = sb("var_eps", [P, 2, NT])
    deviation = sb("deviation", [P, 2, NT])
    inv_dev = sb("inv_dev", [P, 2, NT])
    with ExitStack() as before_last_layer:
        wo1_raw = sb("wo1_raw", [P, H, D], F32, before_last_layer)
    xT_hi = sb("xT_hi", [P, KD, B * T], F32R)
    xT_lo = sb("xT_lo", [P, KD, B * T], F32R)
    w_hi = sb("w_hi", [P, 2, 512], F32R)
    w_lo = sb("w_lo", [P, 2, 512], F32R)
    q_sum = sb("q_sum", [P, 2, 2 * T])
    qT = sb("qT", [P, 2, B * T])
    swapped = sb("swapped", [P, 2, 2 * T])
    row_max = sb("row_max", [P, 2, 4])
    neg_max = sb("neg_max", [P, 2, 4])
    row_sum = sb("row_sum", [P, 2, 4])
    inv_sum = sb("inv_sum", [P, 2, 4])
    bank = ctx.enter_context(nc.psum_tensor("bank", [P, 8, 512], F32))

    with ExitStack() as outputs:
        wo_hi = sb("wo_hi", [P, H, D], F32R, outputs)
        wo_lo = sb("wo_lo", [P, H, D], F32R, outputs)
        ctx_hi0 = sb("ctx_hi0", [P, H, P], F32R, outputs)
        ctx_lo0 = sb("ctx_lo0", [P, H, P], F32R, outputs)
        ctx_hi1 = sb("ctx_hi1", [P, 12, P], F32R, outputs)
        ctx_lo1 = sb("ctx_lo1", [P, 12, P], F32R, outputs)
    with ExitStack() as heads:
        sb("under_wq_full", [P, KD, H * P], F32, heads)
        q_hi = sb("q_hi", [P, 2, B * T], F32R, heads)
        q_lo = sb("q_lo", [P, 2, B * T], F32R, heads)
        sb("under_keysT_and_probs", [P, G * B * T + 4 * 3 * P], F32, heads)
        k_hi = sb("k_hi", [P, 2, T], F32R, heads)
        k_lo = sb("k_lo", [P, 2, T], F32R, heads)
        ctx_tok = sb("ctx_tok", [P, 2, 2, DV], F32, heads)
    wq_full = sb("wq_full", [P, KD, H * P])
    wo_full = sb("wo_full", [P, H, D])
    keysT = sb("keysT", [P, G, B * T])
    probs = sb("probs", [P, 2, 2, 3 * P])
    probsT = sb("probsT", [P, 2, 2, 3 * P])
    with ExitStack() as early:
        latT_hi = sb("latT_hi", [P, 2, B * T], F32R, early)
        latT_lo = sb("latT_lo", [P, 2, B * T], F32R, early)
    v_tok = sb("v_tok", [P, NT, G, DV + 1])
    with ExitStack() as setup:
        wqb_raw = sb("wqb_raw", [KQ, 2, H * (NOPE + ROPE)], F32, setup)
        wkvb_raw = sb("wkvb_raw", [KVL, H * (NOPE + DV)], F32, setup)
        wo_raw = sb("wo_raw", [P, H, D], F32, setup)
        qn_rows = sb("qn_rows", [P, QL], F32, setup)
        kvn_rows = sb("kvn_rows", [P, KVL], F32, setup)
        key_cos = sb("key_cos", [P, 2, ROPE], F32, setup)
        key_sin = sb("key_sin", [P, 2, ROPE], F32, setup)
        wa_raw = sb("wa_raw", [P, KD, PROJ], F32, setup)
    with ExitStack() as layer0:
        ctxT0 = sb("ctxT0", [P, PAIRS, B * T], F32, layer0)
    with ExitStack() as moe:
        wq1_raw = sb("wq1_raw", [P, KD, H * DQ], F32, moe)
        comb_rows = sb("comb_rows", [P, 2, B * T], F32, moe)
        silu = sb("silu", [P, 2, 512], F32, moe)
        weighted = sb("weighted", [P, 2, 512], F32, moe)
        gate_raw = sb("gate_raw", [E, D], F32, moe)
        gate_hi = sb("gate_hi", [P, KD, P], F32R, moe)
        gate_lo = sb("gate_lo", [P, KD, P], F32R, moe)
        p_rows = sb("p_rows", [E, B * T], F32, moe)
        p_tok = sb("p_tok", [P, NT, E], F32, moe)
        rank = sb("rank", [P, E], F32, moe)
        chosen = sb("chosen", [P, 2, NT, E], F32, moe)
        scratch = sb("scratch", [P, NT, E], F32, moe)
        best = sb("best", [P, 6, NT], F32, moe)
        wgu_raw = sb("wgu_raw", [P, 2, KD * 2 * FF], F32, moe)
        wdn_raw = sb("wdn_raw", [P, 2, D], F32, moe)
        wdn_hi = sb("wdn_hi", [P, 2, D], F32R, moe)
        wdn_lo = sb("wdn_lo", [P, 2, D], F32R, moe)
        zeros_bf = sb("zeros_bf", [P, 512], BF16, moe)
        wk_raw = sb("wk_raw", [P, KD, G * DQ], F32, moe)
        wv_raw = sb("wv_raw", [P, KD, G * DV], F32, moe)
    ctxT1 = sb("ctxT1", [P, H, B * T])
    qlat_tok = qT[:].rearrange("p h t -> p (h t)")[:, 0:NT * QL].rearrange("p (t f) -> p t f", f=QL)
    key_tok = keysT[:, 1, :].rearrange("p (t f) -> p t f", f=P)
    key_part = swapped[:].rearrange("p a b -> p (a b)")[:, 0:NT * ROPE].rearrange("p (t f) -> p t f", f=ROPE)
    headT = probs[:].rearrange("p a h n -> p (a h n)")[:, 0:4 * HEAD].rearrange("p (a n) -> p a n", a=4)
    squares = probsT[:].rearrange("p a h n -> p (a h n)")[:, 0:NT * QL].rearrange("p (t n) -> p t n", n=QL)
    key_sq = q_sum[:].rearrange("p a n -> p (a n)")[:, 0:NT * KVL].rearrange("p (t n) -> p t n", n=KVL)
    wv_hi = comb_rows[:, 0, :].bitcast(F32R).rearrange("p (k n) -> p k n", k=KD)
    wv_lo = comb_rows[:, 1, :].bitcast(F32R).rearrange("p (k n) -> p k n", k=KD)
    def wo_raw_of(at):
        return wo_full if at["layer"] == 0 else wo1_raw

    def ctx_parts(layer, t):
        if layer == 0:
            return (ctx_hi1[:, 0:PAIRS], ctx_lo1[:, 0:PAIRS]) if t % 2 else (ctx_lo0[:, 0:PAIRS], ctx_lo0[:, PAIRS:H])
        if t % 2:
            return [x[:].rearrange("p k (h n) -> p (k h) n", n=P) for x in (latT_hi, latT_lo)]
        return ctx_hi0[:], ctx_lo0[:]

    ffn_w = probs[:].rearrange("p a h n -> p (a h n)")[:, 0:2 * D].rearrange("p (a n) -> p a n", a=2)
    ffn_bw = probsT[:].rearrange("p a h n -> p (a h n)")[:, 0:2 * D].rearrange("p (a n) -> p a n", a=2)
    comb_dram = nc.dram_tensor("comb_dram", (E, B * T), F32, kind="Internal").ap()
    x_dram = a["x"].rearrange("b (j p) d -> p (b j) d", p=P)
    out_dram = out.rearrange("b (j p) d -> p (b j) d", p=P)

    x_in = [sem(f"x_in{b}") for b in range(B)]
    expert_in = [sem("expert_in0"), sem("expert_in1")]
    comb_in = [sem("comb_in0"), sem("comb_in1")]
    ld = sems("load", "ident_in consts_in bf_in alibi_in wa_in wqb_in wkvb_in wo0_in gate_in wkv1_in wq1_in wo1_in ffn_in "
              "comb_out stored")
    su = sems("setup", "wa_hi wa_lo proj_done sq_done rms_var rms_sqrt rms_inv latents key_steps latT_done latT_hi_done "
              "latT_lo_done keysT_copied headT_done headT_copied fold_done fold_q_copied fold_o_copied rope_cols")
    ln = sems("norm", "xT_done xT_hi_done xT_lo_done y_done rows_added y_read stats var_ready moments_ready sqrt_done "
              "inv_ready x_new")
    mo = sems("moe", "gateT_done gate_zero gate_hi gate_lo logits_done sigmoid_done p_done step combT_done combT_copied comb_ready "
              "zeros gu_hi gu_lo dn_hi dn_lo up_done silu_done weighted act act_hi act_lo down_done")
    kv = sems("kv1", "wk_hi wk_lo k_done cos_done swap_done sin_done k_ready wv_hi wv_lo v_done v_copied ones wq_perm")
    ff = sems("ffn", "abs_done step bwT_done bw_hi bw_lo")

    def attention(name, layer):
        names = ("w_hi_done w_lo_done q_done cos_done swap_done sin_done q_ready scores_done max_step max_ready "
                 "q_summed q_hi_done k_hi_done k_copied capped masked exp_done inv_ready probs_ready probsT_done "
                 "probsT_copied ctx_done ctx_norm ctxT_done "
                 "ctx_copied wo_hi_done wo_lo_done wo_lo_rest ctx_hi_done ctx_lo_done").split()
        return dict(layer=layer, **{n: sem(f"{name}_{n}") for n in names})

    at0, at1 = attention("a0", 0), attention("a1", 1)

    def scores_of(par):
        return bank[:, 2 * par:2 * par + 2, 0:3 * P]

    probsT_bank = bank[:, 4:6, 0:3 * P]
    CTX, QRY = 6, 7

    def pair_view(ap):
        return ap.rearrange("p (h t) -> p h t", h=2)

    def all_of(x, par):
        return x[:, 2 * par:2 * par + 2, :].rearrange("p a n -> p (a n)")[:, 0:6 * P]

    def keys_first(par):
        return probs[:, par, :, :].rearrange("p h n -> p (h n)")

    ctx_banks = bank[:, 4:6, 0:2 * (DV + 1)].rearrange("p h (t n) -> p h t n", t=2)

    def query_bank(p, b):
        return 4 + b if isinstance(p, int) and p == 0 and b < 2 else QRY

    def comb_bank(e, j):
        return 2 * e + j

    def lat_bank(b):
        return (2 * b + 4) % NT

    def xT_bank(turn, b):
        return b if turn == 0 else 4 + b

    def perm_in(x, k, heads):
        return x[:, k, :].rearrange("p (h j e) -> p h e j", h=heads, e=2)

    def perm_out(x, k):
        return x[:, k, :].rearrange("p (h e j) -> p h e j", e=2, j=DQ // 2)

    def steps(eng, body):
        def pair(p, first, more):
            for b in range(B):
                body(p, b, 4 * p + b, (lambda k, b=b: not first or b >= k), True, more)

        pair(0, True, True)
        with eng.Fori(1, PAIRS - 1) as p:
            pair(p, False, True)
        pair(PAIRS - 1, False, False)
        for b in range(3):
            body(PAIRS, b, 4 * PAIRS + b, (lambda k, b=b: k > b), False, False)

    def ahead(p, b, more):
        if b == 0:
            return p, B - 1
        return (p + 1, b - 1) if more else None

    def forward(p, b, k):
        return (p, b + k) if b + k < B else (p + 1, b + k - B)

    def back(p, b, k):
        return (p, b - k) if b >= k else (p - 1, b - k + B)

    def three_pass(eng, dst, s_hi, s_lo, m_hi, m_lo, start, stop):
        eng.matmul(dst, s_hi, m_hi, start=start, stop=False, skip_group_check=True)
        eng.matmul(dst, s_hi, m_lo, start=False, stop=False, skip_group_check=True)
        return eng.matmul(dst, s_lo, m_hi, start=False, stop=stop, skip_group_check=True)

    def pe_transpose_x(eng, turn, b):
        if turn == 0:
            eng.wait_ge(x_in[b], 16)
            if b == 0:
                eng.wait_ge(ld["ident_in"], 16)
        else:
            eng.wait_ge(ln["x_new"], NT * (turn - 1) + 2 * b + 2)
        for k in range(KD):
            for j in range(2):
                mm = eng.transpose(bank[:, xT_bank(turn, b), k * T + j * P:k * T + j * P + P],
                                   x_tok[:, 2 * b + j, k * P:k * P + P], ident[:])
        mm.then_inc(ln["xT_done"], 1)

    def pe_project_out(eng, at):
        turn, parts = (0, PAIRS) if at["layer"] == 0 else (2, H)
        for t in range(NT):
            c_hi, c_lo = ctx_parts(at["layer"], t)
            eng.wait_ge(at["ctx_hi_done"], t + 1)
            eng.wait_ge(at["ctx_lo_done"], t + 1)
            if t >= 4:
                eng.wait_ge(ln["y_read"], NT * turn + t - 3)
            for i in range(parts):
                if t == 0 and i % (parts // 4) == 0:
                    quarter = i // (parts // 4)
                    eng.wait_ge(at["wo_hi_done"], quarter + 1)
                    if quarter < 2:
                        eng.wait_ge(at["wo_lo_done"], quarter + 1)
                    else:
                        eng.wait_ge(at["wo_lo_rest"], quarter - 1)
                mm = three_pass(eng, bank[:, t % 4, 0:D], c_hi[:, i, :], c_lo[:, i, :],
                                wo_hi[:, i, :], wo_lo[:, i, :], i == 0, i == parts - 1)
            mm.then_inc(ln["y_done"], 1)
            if t == 3 and at["layer"] == 0:
                eng.wait_ge(mo["gate_hi"], 1)
                eng.wait_ge(mo["gate_lo"], 1)
            if t >= 3 and t % 2:
                pe_transpose_x(eng, turn + 1, (t - 3) // 2)
            if t == 5 and at["layer"] == 1:
                eng.wait_ge(ff["step"], FFN_STEPS)
                for o in range(2):
                    for k in range(KD):
                        mm = eng.transpose(bank[:, 7, k * D + o * P:k * D + o * P + P],
                                           ffn_bw[:, o, k * P:k * P + P], ident[:])
                mm.then_inc(ff["bwT_done"], 1)

    def pe_queries(eng, at, p, b):
        m = 4 * p + b
        rows = KQ if at["layer"] == 0 else P
        xh, xl = (latT_hi, latT_lo) if at["layer"] == 0 else (xT_hi, xT_lo)
        if b == 0:
            eng.wait_ge(at["w_hi_done"], p + 1)
            eng.wait_ge(at["w_lo_done"], p + 1)
        if not (isinstance(p, int) and m < 3):
            eng.wait_ge(at["cos_done"], m)
            eng.wait_ge(at["swap_done"], m)
        for h in range(2):
            for k in range(2):
                mm = three_pass(eng, bank[:, query_bank(p, b), h * T:h * T + T],
                                w_hi[0:rows, k, h * P:h * P + P], w_lo[0:rows, k, h * P:h * P + P],
                                xh[0:rows, k, T * b:T * b + T], xl[0:rows, k, T * b:T * b + T],
                                k == 0, k == 1)
        mm.then_inc(at["q_done"], 1)

    def pe_attention0(eng, at):
        def body(p, b, n, lag, own, more):
            if own:
                eng.wait_ge(at["q_ready"], n + 1)
                if lag(2):
                    eng.wait_ge(at["exp_done"], n - 1)
                for h in range(2):
                    dst = bank[:, 2 * (b % 2) + h, :]
                    q = qT[:, h, T * b:T * b + T]
                    eng.matmul(dst[:, 0:T], q[:, P:T], keysT[:, 0, T * b:T * b + T],
                               start=True, stop=False, skip_group_check=True)
                    eng.matmul(dst[:, T:T + P], q[:, 0:P], keysT[:, 0, T * b:T * b + P],
                               start=False, stop=False, skip_group_check=True)
                    mm = eng.matmul(dst[:, P:3 * P], ident_bf[:], mask_bf[:],
                                    start=False, stop=True, skip_group_check=True)
                mm.then_inc(at["scores_done"], 1)
            if own and ahead(p, b, more):
                pe_queries(eng, at, *ahead(p, b, more))
            if lag(1):
                eng.wait_ge(at["probs_ready"], n)
                if lag(2):
                    eng.wait_ge(at["probsT_copied"], n - 1)
                for h in range(2):
                    pr = probs[:, (b - 1) % 2, h, :]
                    dst = probsT_bank[:, h, :]
                    eng.transpose(dst[:, 0:P], pr[:, T:T + P], ident[:])
                    eng.transpose(dst[:, P:T], pr[:, 0:P], ident[:])
                    mm = eng.transpose(dst[:, T:T + P], pr[:, P:T], ident[:])
                mm.then_inc(at["probsT_done"], 1)
            if lag(2):
                b2 = (b - 2) % B
                eng.wait_ge(at["probsT_copied"], n - 1)
                if lag(3):
                    eng.wait_ge(at["ctx_copied"], n - 2)
                values = [key_tok[:, (2 * b2 + j + 4) % NT, 0:KVL] for j in range(2)]
                for h in range(2):
                    pt = probsT[:, b % 2, h, :]
                    dst = bank[64 * h:64 * h + 64, CTX, 0:T]
                    eng.matmul(dst, values[0], pt[:, 0:T], start=True, stop=False, skip_group_check=True)
                    mm = eng.matmul(dst[:, P:T], values[1], pt[:, T:T + P],
                                    start=False, stop=True, skip_group_check=True)
                mm.then_inc(at["ctx_done"], 1)

        steps(eng, body)

    def pe_attention1(eng, at):
        def body(p, b, n, lag, own, more):
            par = b % 2
            if own:
                eng.wait_ge(at["q_ready"], n + 1)
                eng.wait_ge(at["k_copied"], n + 1)
                if lag(2):
                    eng.wait_ge(at["capped"], n - 1)
                for tile in range(2):
                    dst = bank[:, 2 * par + tile, 0:(2 - tile) * T]
                    keys = slice(tile * P, tile * P + P)
                    queries = slice(T * b + tile * P, T * b + T)
                    three_pass(eng, dst, k_hi[:, par, keys], k_lo[:, par, keys], q_hi[:, :, queries],
                               q_lo[:, :, queries], True, False)
                    mm = eng.matmul(dst, alibi_keys[:, keys], alibi_queries[:, bass.ds(2 * p, 2), tile * P:T],
                                    start=False, stop=True, skip_group_check=True)
                mm.then_inc(at["scores_done"], 1)
            if own and ahead(p, b, more):
                pe_queries(eng, at, *ahead(p, b, more))
            if lag(1):
                if lag(2):
                    eng.wait_ge(at["ctx_norm"], n - 1)
            if lag(2):
                if lag(3):
                    eng.wait_ge(at["ctx_copied"], n - 2)
                if not lag(1):
                    eng.wait_ge(at["ctx_norm"], n - 1)
                for h in range(2):
                    for tile in range(2):
                        mm = eng.transpose(bank[:, CTX, h * T + tile * P:h * T + tile * P + P],
                                           ctx_tok[:, h, tile, :], ident[:])
                mm.then_inc(at["ctxT_done"], 1)
            if lag(1):
                eng.wait_ge(at["exp_done"], n)
                p1, b1 = back(p, b, 1)
                e = keys_first(1 - par)
                values = [v_tok[:, 2 * b1 + j, bass.ds(p1 // 2, 1), :].rearrange("p g n -> p (g n)")
                          for j in range(2)]
                for h in range(2):
                    dst = [bank[:, 4 + h, tile * (DV + 1):(tile + 1) * (DV + 1)] for tile in range(2)]
                    eng.matmul(dst[0], e[:, h * T:h * T + P], values[0], start=True, stop=True,
                               skip_group_check=True)
                    eng.matmul(dst[1], e[:, h * T + P:h * T + T], values[0], start=True, stop=False,
                               skip_group_check=True)
                    mm = eng.matmul(dst[1], e[:, 2 * T + h * P:2 * T + h * P + P], values[1], start=False,
                                    stop=True, skip_group_check=True)
                mm.then_inc(at["ctx_done"], 1)

        steps(eng, body)

    def pe_first_queries(eng, at):
        for b in range(B - 1):
            pe_queries(eng, at, 0, b)

    block = ctx.enter_context(nc.Block())

    @block.tensor
    def _(pe):
        for b in range(B):
            pe_transpose_x(pe, 0, b)
        pe.wait_ge(su["wa_hi"], 1)
        pe.wait_ge(su["wa_lo"], 1)
        for t in range(NT):
            need = max(t // 2 + 1, t - 3)
            pe.wait_ge(ln["xT_hi_done"], need)
            pe.wait_ge(ln["xT_lo_done"], need)
            for k in range(KD):
                mm = three_pass(pe, bank[:, (t + 4) % NT, 0:PROJ],
                                xT_hi[:, k, t * P:t * P + P], xT_lo[:, k, t * P:t * P + P],
                                w_hi[:, k, 0:PROJ], w_lo[:, k, 0:PROJ], k == 0, k == KD - 1)
            mm.then_inc(su["proj_done"], 1)
        pe.wait_ge(su["key_steps"], 4)
        for b in range(B):
            pe.wait_ge(su["latents"], 4 * b + 4)
            for k in range(2):
                for j in range(2):
                    pe.transpose(bank[0:KQ, lat_bank(b), k * T + j * P:k * T + j * P + P],
                                 qlat_tok[:, 2 * b + j, k * KQ:k * KQ + KQ], ident[:])
            for j in range(2):
                mm = pe.transpose(bank[:, lat_bank(b) + 1, j * P:j * P + P], key_tok[:, (2 * b + j + 4) % NT, :], ident[:])
            mm.then_inc(su["latT_done"], 1)
        pe.wait_ge(su["latT_hi_done"], B)
        pe.wait_ge(su["latT_lo_done"], B)
        pe.wait_ge(su["keysT_copied"], B)
        pe.wait_ge(ld["wqb_in"], 32)
        pe.wait_ge(ld["wkvb_in"], 16)
        for h in range(H + 3):
            if h < H:
                if h >= 4:
                    pe.wait_ge(su["headT_copied"], h - 3)
                dst = bank[:, 4 + h % 4, :]
                for k in range(2):
                    c = h * (NOPE + ROPE)
                    pe.transpose(dst[:, k * KQ:k * KQ + KQ], wqb_raw[:, k, c:c + NOPE], ident[0:KQ, 0:KQ])
                c = h * (NOPE + DV)
                pe.transpose(dst[:, QL:QL + KVL], wkvb_raw[:, c:c + NOPE], ident[0:KVL, 0:KVL])
                pe.transpose(dst[:, QL + KVL:QL + 2 * KVL], wkvb_raw[:, c + NOPE:c + NOPE + DV],
                             ident[0:KVL, 0:KVL]).then_inc(su["headT_done"], 1)
            if h >= 3:
                g = h - 3
                pe.wait_ge(su["headT_copied"], g + 1)
                if g == 0:
                    pe.wait_ge(ld["wo0_in"], 16)
                if g >= 2:
                    pe.wait_ge(su["fold_q_copied"], g - 1)
                if g >= 4 and g % 2 == 0:
                    pe.wait_ge(su["fold_o_copied"], g // 2 - 1)
                ht = headT[:, g % 4, :]
                for k in range(2):
                    pe.matmul(bank[0:KQ, g % 2, k * KVL:k * KVL + KVL], ht[:, k * KQ:k * KQ + KQ],
                              ht[:, QL:QL + KVL], start=True, stop=True)
                r = 64 * (g % 2)
                pe.matmul(bank[r:r + 64, 2 + (g // 2) % 2, 0:D], ht[:, QL + KVL:QL + 2 * KVL], wo_raw[:, g, :],
                          start=True, stop=True).then_inc(su["fold_done"], 1)
        pe.wait_ge(su["fold_q_copied"], H)
        pe.wait_ge(su["fold_o_copied"], PAIRS)
        pe.wait_ge(ld["bf_in"], 32)
        pe_first_queries(pe, at0)
        pe_attention0(pe, at0)
        pe.wait_ge(ld["gate_in"], 32)
        for k in range(KD):
            mm = pe.transpose(bank[:, 4, k * E:k * E + E], gate_raw[:, k * P:k * P + P], ident[0:E, 0:E])
        mm.then_inc(mo["gateT_done"], 1)
        pe_project_out(pe, at0)
        for j in range(2):
            if j == 1:
                pe_transpose_x(pe, 1, 3)
            pe.wait_ge(ln["xT_hi_done"], B + 2 * j + 2)
            pe.wait_ge(ln["xT_lo_done"], B + 2 * j + 2)
            for k in range(KD):
                mm = three_pass(pe, bank[:, j, :], gate_hi[:, k, :], gate_lo[:, k, :],
                                xT_hi[:, k, 512 * j:512 * j + 512], xT_lo[:, k, 512 * j:512 * j + 512],
                                k == 0, k == KD - 1)
            mm.then_inc(mo["logits_done"], 1)

        def up(e, par, first, j, between=None):
            if j == 0:
                pe.wait_ge(mo["gu_hi"], e + 1)
                pe.wait_ge(mo["gu_lo"], e + 1)
            if not first:
                pe.wait_ge(mo["silu_done"], 2 * e + j - 1)
                pe.wait_ge(mo["weighted"], 2 * e + j - 1)
            for half in range(2):
                if half and between:
                    between()
                for k in range(KD):
                    c = k * 2 * FF + half * FF
                    mm = three_pass(pe, bank[:, 4 + 2 * j + half, :],
                                    w_hi[:, par, c:c + FF], w_lo[:, par, c:c + FF],
                                    xT_hi[:, k, 512 * j:512 * j + 512], xT_lo[:, k, 512 * j:512 * j + 512],
                                    k == 0, k == KD - 1)
            mm.then_inc(mo["up_done"], 1)

        def down(e, par, last=False):
            pe.wait_ge(mo["dn_hi"], e + 1)
            pe.wait_ge(mo["dn_lo"], e + 1)
            for j in range(2):
                if isinstance(e, int) and e == 0:
                    pe.wait_ge(mo["zeros"], 1)
                    pe.wait_ge(mo["act"], 2 * j + 2)
                    for i in (2 * j, 2 * j + 1):
                        pe.matmul(bank[:, i, :], zeros_bf[:, 0:P], zeros_bf[:], start=True, stop=False,
                                  skip_group_check=True)
                pe.wait_ge(mo["act_hi"], 2 * e + j + 1)
                pe.wait_ge(mo["act_lo"], 2 * e + j + 1)
                for t in range(4 * j, 4 * j + 4):
                    mm = three_pass(pe, bank[:, t // 2, (t % 2) * D:(t % 2) * D + D],
                                    latT_hi[:, par, t * P:t * P + P], latT_lo[:, par, t * P:t * P + P],
                                    wdn_hi[:, par, :], wdn_lo[:, par, :], False, False)
                    if last and t % 2:
                        mm.then_inc(ln["y_done"], 2)
            if not last:
                mm.then_inc(mo["down_done"], 1)

        def p_transposed():
            pe.wait_ge(mo["sigmoid_done"], 2)
            for t in range(NT):
                mm = pe.transpose(bank[:, 2, t * E:t * E + E], p_rows[:, t * P:t * P + P], ident[0:E, 0:E])
            mm.then_inc(mo["p_done"], 1)

        def comb_on_all(e):
            pe.wait_ge(mo["combT_copied"], 1)
            for j in range(2):
                mm = pe.matmul(bank[:, comb_bank(e, j), :], ident[0:E, e:e + 1].broadcast_to([E, P]),
                               p_rows[:, 512 * j:512 * j + 512], start=True, stop=True)
            mm.then_inc(mo["comb_ready"], 1)

        up(0, 0, True, 0, p_transposed)
        up(0, 0, True, 1)
        up(1, 1, False, 0)
        pe.wait_ge(mo["step"], ROUTE_STEPS)
        for t in range(NT):
            mm = pe.transpose(bank[0:E, 2 + t // 4, (t % 4) * P:(t % 4) * P + P], chosen[:, 0, t, :], ident[:])
        mm.then_inc(mo["combT_done"], 1)
        up(1, 1, False, 1, lambda: comb_on_all(0))
        comb_on_all(1)
        down(0, 0)
        with pe.Fori(1, E // 2) as i:
            for par in range(2):
                for j in range(2):
                    up(2 * i + par, par, False, j)
                down(2 * i + par - 1, 1 - par)
        down(E - 1, 1, True)

        pe.wait_ge(kv["wk_hi"], KD)
        pe.wait_ge(kv["wk_lo"], KD)
        for i in range(2 * G):
            j, g = i // G, i % G
            if i == 0:
                pe_transpose_x(pe, 2, 0)
                pe_transpose_x(pe, 2, 1)
            if i in (2, 3):
                pe_transpose_x(pe, 2, i)
            if g == 0:
                pe.wait_ge(ln["xT_hi_done"], 2 * B + 2 * j + 2)
                pe.wait_ge(ln["xT_lo_done"], 2 * B + 2 * j + 2)
            if i < 4:
                pe.wait_ge(ln["y_read"], NT + 2 * i + 2)
            else:
                pe.wait_ge(kv["cos_done"], i - 3)
                pe.wait_ge(kv["swap_done"], i - 3)
            for k in range(KD):
                mm = three_pass(pe, bank[:, i % 4, :],
                                w_hi[:, k, g * DQ:g * DQ + DQ], w_lo[:, k, g * DQ:g * DQ + DQ],
                                xT_hi[:, k, 512 * j:512 * j + 512], xT_lo[:, k, 512 * j:512 * j + 512],
                                k == 0, k == KD - 1)
            mm.then_inc(kv["k_done"], 1)
        pe.wait_ge(kv["wv_hi"], 1)
        pe.wait_ge(kv["wv_lo"], 1)
        for t in range(NT):
            if t < 4:
                pe.wait_ge(kv["cos_done"], G + t + 1)
                pe.wait_ge(kv["swap_done"], G + t + 1)
            else:
                pe.wait_ge(kv["v_copied"], t - 3)
            if t == 4:
                pe_first_queries(pe, at1)
            for k in range(KD):
                mm = three_pass(pe, bank[:, t % 4, :],
                                xT_hi[:, k, t * P:t * P + P], xT_lo[:, k, t * P:t * P + P],
                                wv_hi[:, k, :], wv_lo[:, k, :], k == 0, k == KD - 1)
            mm.then_inc(kv["v_done"], 1)
        pe.wait_ge(kv["k_ready"], 2 * G)
        pe.wait_ge(kv["v_copied"], NT)
        pe.wait_ge(kv["ones"], 1)
        pe.wait_ge(ld["alibi_in"], 32)
        pe_attention1(pe, at1)
        pe.wait_ge(at1["ctx_copied"], 4 * PAIRS)
        pe.wait_ge(ld["wo1_in"], 16)
        pe_project_out(pe, at1)
        for t in range(NT):
            if t == 0:
                pe.wait_ge(ff["bw_hi"], 1)
                pe.wait_ge(ff["bw_lo"], 1)
            if t == 2:
                pe_transpose_x(pe, 3, 3)
            pe.wait_ge(ln["xT_hi_done"], 3 * B + t // 2 + 1)
            pe.wait_ge(ln["xT_lo_done"], 3 * B + t // 2 + 1)
            pe.wait_ge(ln["y_read"], 2 * NT + 4 + t + 1 if t < 4 else 3 * NT + t - 3)
            for k in range(KD):
                mm = three_pass(pe, bank[:, t % 4, 0:D],
                                xT_hi[:, k, t * P:t * P + P], xT_lo[:, k, t * P:t * P + P],
                                w_hi[:, k, 0:D], w_lo[:, k, 0:D], k == 0, k == KD - 1)
            mm.then_inc(ln["y_done"], 1)

    def act_split_x(act, turn, b):
        act.wait_ge(ln["xT_done"], B * turn + b + 1)
        act.activation(xT_hi[:, :, T * b:T * b + T],
                       bank[:, xT_bank(turn, b), :].rearrange("p (k t) -> p k t", k=KD),
                       ACT.Copy).then_inc(ln["xT_hi_done"], 1)

    def tiles_before(b):
        return ((0, 1, 2, 3), (4, 5), (6, 7), ())[b]

    def act_split_ctx(act, at, tiles):
        turn = 2 * at["layer"]
        ctxT = ctxT0 if at["layer"] == 0 else ctxT1
        for t in tiles:
            act.wait_ge(at["ctx_copied"], 4 * (PAIRS - 1) + t // 2 + 1)
            if t == 0 and at["layer"] == 1:
                act.wait_ge(at["k_copied"], 4 * PAIRS)
            if t == 1:
                act.wait_ge(at["ctx_done"], 4 * PAIRS)
            if t >= 2:
                act.wait_ge(ln["y_done"], NT * turn + t - 1)
            act.activation(ctx_parts(at["layer"], t)[0], ctxT[:, :, t * P:t * P + P],
                           ACT.Copy).then_inc(at["ctx_hi_done"], 1)

    def act_split_wo(act, at, b):
        n = (PAIRS if at["layer"] == 0 else H) // 4
        if b == 0:
            act.wait_ge(at["w_lo_done"], PAIRS)
            if at["layer"] == 1:
                act.wait_ge(ld["wo1_in"], 16)
        act.activation(wo_hi[:, n * b:n * b + n, :], wo_raw_of(at)[:, n * b:n * b + n, :],
                       ACT.Copy).then_inc(at["wo_hi_done"], 1)

    def act_layer_norm(act, turn, at=None):
        for b in range(B):
            if at:
                act_split_ctx(act, at, [t for t in tiles_before(b) if t >= 2])
            if turn == 2 and b == 0:
                act.wait_ge(ld["ffn_in"], 16)
                for o in range(2):
                    act.activation(ffn_bw[:, o, :], ffn_w[:, o, :], ACT.Abs,
                                   accum_out=square_sum[:, 0, o:o + 1]).then_inc(ff["abs_done"], 1)
            if turn == 2 and b == 3:
                act.wait_ge(ff["bwT_done"], 1)
                act.activation(w_hi[:, :, 0:D], bank[:, 7, :].rearrange("p (k o) -> p k o", k=KD),
                               ACT.Copy).then_inc(ff["bw_hi"], 1)
            if turn < 3 and b >= 1:
                act_split_x(act, turn + 1, b - 1)
            act.wait_ge(ln["var_ready"], B * turn + b + 1)
            act.activation(deviation[:, 0, 2 * b:2 * b + 2], var_eps[:, 0, 2 * b:2 * b + 2],
                           ACT.Sqrt).then_inc(ln["sqrt_done"], 1)
        if turn < 3:
            act_split_x(act, turn + 1, B - 1)

    def act_split_w(act, at, p):
        rows = KQ if at["layer"] == 0 else P
        if not (isinstance(p, int) and p == 0):
            act.wait_ge(at["q_done"], 4 * p)
        act.activation(w_hi[0:rows, :, 0:2 * P], wq_full[0:rows, :, bass.ds(2 * P * p, 2 * P)],
                       ACT.Copy).then_inc(at["w_hi_done"], 1)

    def act_swap(act, at, p, b):
        m = 4 * p + b
        if at["layer"] == 0:
            act.wait_ge(at["cos_done"], m + 1)
        else:
            act.wait_ge(at["q_done"], m + 1)
        if not (isinstance(p, int) and m < 2):
            act.wait_ge(at["q_ready"] if at["layer"] == 0 else at["q_summed"], m - 1)
        r0, rn = (64, 32) if at["layer"] == 0 else (0, 64)
        act.activation(swapped[r0:r0 + rn, b % 2, :], bank[r0 + rn:r0 + 2 * rn, query_bank(p, b), :], ACT.Copy)
        act.activation(swapped[r0 + rn:r0 + 2 * rn, b % 2, :], bank[r0:r0 + rn, query_bank(p, b), :],
                       ACT.Copy).then_inc(at["swap_done"], 1)

    def act_attention0(act, at):
        scale = (NOPE + ROPE) ** -0.5

        def body(p, b, n, lag, own, more):
            par = b % 2
            if own:
                if not more and b >= 1:
                    act_split_wo(act, at, b - 1)
                act.wait_ge(at["max_ready"], n + 1)
                if lag(2):
                    act.wait_ge(at["probsT_done"], n - 1)
                for h in range(2):
                    for tile, c0, c1 in ((0, 0, T), (1, T, T + P)):
                        i = 2 * tile + h
                        ins = act.activation(probs[:, par, h, c0:c1], bank[:, 2 * par + h, c0:c1], ACT.Exp,
                                             bias=neg_max[:, par, i:i + 1], scale=scale,
                                             accum_out=row_sum[:, par, i:i + 1])
                ins.then_inc(at["exp_done"], 1)
                if b == 0 and more:
                    act_split_w(act, at, p + 1)
                if ahead(p, b, more):
                    act_swap(act, at, *ahead(p, b, more))
            if lag(1):
                act.wait_ge(at["probsT_done"], n)
                if lag(3):
                    act.wait_ge(at["ctx_done"], n - 2)
                act.activation(probsT[:, (b - 1) % 2, :, :], probsT_bank, ACT.Copy).then_inc(at["probsT_copied"], 1)
            if not own and b == 0:
                act_split_wo(act, at, 3)
                act_split_ctx(act, at, (0,))

        steps(act, body)

    def act_query_hi(act, at, p, b):
        m = 4 * p + b
        act.wait_ge(at["q_summed"], m + 1)
        if not (isinstance(p, int) and p == 0):
            act.wait_ge(at["scores_done"], m - 3)
        act.activation(q_hi[:, :, T * b:T * b + T], pair_view(q_sum[:, b % 2, :]), ACT.Copy).then_inc(at["q_hi_done"], 1)

    def act_attention1(act, at):
        def body(p, b, n, lag, own, more):
            par = b % 2
            if own:
                act.wait_ge(at["scores_done"], n + 1)
                if lag(2):
                    act.wait_ge(at["ctx_done"], n - 1)
                act.activation(keys_first(par), all_of(bank, par), ACT.Tanh,
                               scale=DQ ** -0.5 / 30.0).then_inc(at["capped"], 1)
                if b < 2 or more:
                    act_query_hi(act, at, *forward(p, b, 2))
                if ahead(p, b, more):
                    act_swap(act, at, *ahead(p, b, more))
                if b == 0 and more:
                    act_split_w(act, at, p + 1)
                if not more and b == 3:
                    act_split_wo(act, at, 0)
                act.wait_ge(at["masked"], n + 1)
                act.activation(keys_first(par), keys_first(par), ACT.Exp, scale=30.0).then_inc(at["exp_done"], 1)
            if lag(2):
                p2, b2 = back(p, b, 2)
                act.wait_ge(at["ctxT_done"], n - 1)
                act.activation(ctxT1[:, bass.ds(2 * p2, 2), T * b2:T * b2 + T], pair_view(bank[:, CTX, :]),
                               ACT.Copy).then_inc(at["ctx_copied"], 1)
            if own and not more and b == 3:
                for quarter in (1, 2, 3):
                    act_split_wo(act, at, quarter)
            if not own and b == 0:
                act_split_ctx(act, at, (0,))

        steps(act, body)

    def act_first_queries(act, at):
        for b in range(B - 1):
            act_swap(act, at, 0, b)
            if at["layer"] == 1 and b >= 1:
                act_query_hi(act, at, 0, b - 1)

    @block.scalar
    def _(act):
        act.wait_ge(ld["wa_in"], 48)
        act.activation(w_hi[:, :, 0:PROJ], wa_raw[:], ACT.Copy).then_inc(su["wa_hi"], 1)
        for b in range(B):
            act_split_x(act, 0, b)
        for t in range(NT):
            act.wait_ge(su["proj_done"], t + 1)
            src = bank[:, (t + 4) % NT, :]
            act.activation(squares[:, t, :], src[:, 0:QL], ACT.Square,
                           accum_out=square_sum[:, 0, t:t + 1]).then_inc(su["sq_done"], 1)
            act.activation(key_sq[:, t, :], src[:, QL:QL + KVL], ACT.Square,
                           accum_out=square_sum[:, 1, t:t + 1]).then_inc(su["sq_done"], 1)
        act.wait_ge(su["rms_var"], 2)
        act.activation(deviation[:], var_eps[:], ACT.Sqrt).then_inc(su["rms_sqrt"], 1)
        for b in range(B):
            act.wait_ge(su["latT_done"], b + 1)
            act.activation(latT_hi[0:KQ, :, T * b:T * b + T], bank[0:KQ, lat_bank(b), :].rearrange("p (k t) -> p k t", k=2),
                           ACT.Copy).then_inc(su["latT_hi_done"], 1)
            act.activation(keysT[:, 0, T * b:T * b + T], bank[:, lat_bank(b) + 1, 0:T],
                           ACT.Copy).then_inc(su["keysT_copied"], 1)
        for h in range(H):
            if h == 8:
                act.wait_ge(su["rope_cols"], 2)
                act.wait_ge(su["fold_q_copied"], 2)
                act_split_w(act, at0, 0)
            act.wait_ge(su["headT_done"], h + 1)
            if h >= 4:
                act.wait_ge(su["fold_done"], h - 3)
            act.activation(headT[:, h % 4, :], bank[:, 4 + h % 4, 0:QL + 2 * KVL],
                           ACT.Copy).then_inc(su["headT_copied"], 1)
        act.wait_ge(su["fold_q_copied"], H)
        act_first_queries(act, at0)
        act_attention0(act, at0)
        act.wait_ge(mo["gateT_done"], 1)
        act.wait_ge(mo["gate_zero"], 2)
        act.activation(gate_hi[:, :, 0:E], bank[:, 4, 0:KD * E].rearrange("p (k e) -> p k e", k=KD),
                       ACT.Copy).then_inc(mo["gate_hi"], 1)
        def gate_up_hi(e, par, i, first):
            act.wait_ge(expert_in[par], 32 * (i + 1))
            if not first:
                act.wait_ge(mo["up_done"], 2 * e - 2)
            act.activation(w_hi[:, par, :], wgu_raw[:, par, :], ACT.Copy).then_inc(mo["gu_hi"], 1)

        def down_hi(e, par, first):
            if not first:
                act.wait_ge(mo["down_done"], e - 1)
            act.activation(wdn_hi[:, par, :], wdn_raw[:, par, :], ACT.Copy).then_inc(mo["dn_hi"], 1)

        def silus(e, j):
            act.wait_ge(mo["up_done"], 2 * e + j + 1)
            dst = weighted if isinstance(e, int) and e == 1 else silu
            if not isinstance(e, int) or e >= 2:
                act.wait_ge(mo["act_lo"], 2 * e + j - 1)
            act.activation(dst[:, j, :], bank[:, 4 + 2 * j, :], ACT.Silu).then_inc(mo["silu_done"], 1)

        def high(e, par, j):
            act.wait_ge(mo["act"], 2 * e + j + 1)
            src = weighted if isinstance(e, int) and e == 1 else silu
            if j == 0 and (not isinstance(e, int) or e >= 2):
                act.wait_ge(mo["down_done"], e - 1)
            act.activation(latT_hi[:, par, 512 * j:512 * j + 512], src[:, j, :],
                           ACT.Copy).then_inc(mo["act_hi"], 1)

        def activations(e, par):
            for j in range(2):
                silus(e, j)
            for j in range(2):
                high(e, par, j)

        act_split_ctx(act, at0, (1,))
        act.wait_ge(at0["q_done"], 4 * PAIRS)
        gate_up_hi(0, 0, 0, True)
        down_hi(0, 0, True)
        gate_up_hi(1, 1, 0, True)
        down_hi(1, 1, True)
        act_layer_norm(act, 0, at0)
        for j in range(2):
            act.wait_ge(mo["logits_done"], j + 1)
            act.activation(p_rows[:, 512 * j:512 * j + 512], bank[0:E, j, :],
                           ACT.Sigmoid).then_inc(mo["sigmoid_done"], 1)
        silus(0, 0)
        silus(0, 1)
        silus(1, 0)
        act.wait_ge(mo["combT_done"], 1)
        act.activation(p_rows[:].rearrange("e (a n) -> e a n", a=2), bank[0:E, 2:4, :],
                       ACT.Copy).then_inc(mo["combT_copied"], 1)
        high(0, 0, 0)
        high(0, 0, 1)
        silus(1, 1)
        gate_up_hi(2, 0, 1, False)
        high(1, 1, 0)
        high(1, 1, 1)
        down_hi(2, 0, False)
        gate_up_hi(3, 1, 1, False)
        activations(2, 0)
        down_hi(3, 1, False)
        with act.Fori(2, E // 2) as i:
            gate_up_hi(2 * i, 0, i, False)
            activations(2 * i - 1, 1)
            down_hi(2 * i, 0, False)
            gate_up_hi(2 * i + 1, 1, i, False)
            activations(2 * i, 0)
            down_hi(2 * i + 1, 1, False)
        activations(E - 1, 1)

        act.wait_ge(ld["wkv1_in"], 32)
        act.wait_ge(mo["up_done"], 2 * E)
        for k in range(KD):
            act.activation(perm_out(w_hi, k), perm_in(wk_raw, k, G), ACT.Copy).then_inc(kv["wk_hi"], 1)
        act.wait_ge(mo["act"], 2 * E)
        act.activation(wv_hi, wv_raw[:], ACT.Copy).then_inc(kv["wv_hi"], 1)
        act_layer_norm(act, 1)
        for i in range(2 * G):
            act.wait_ge(kv["k_done"], i + 1)
            if i >= 2:
                act.wait_ge(kv["k_ready"], i - 1)
            act.activation(swapped[0:64, i % 2, :], bank[64:P, i % 4, :], ACT.Copy)
            act.activation(swapped[64:P, i % 2, :], bank[0:64, i % 4, :], ACT.Copy).then_inc(kv["swap_done"], 1)
        act.wait_ge(kv["wq_perm"], H)
        act_split_w(act, at1, 0)
        for t in range(NT):
            if t == 4:
                act.wait_ge(kv["k_ready"], 2 * G)
                act_first_queries(act, at1)
            act.wait_ge(kv["v_done"], t + 1)
            act.activation(v_tok[:, t, :, 0:DV], bank[:, t % 4, :].rearrange("p (g n) -> p g n", g=G),
                           ACT.Copy).then_inc(kv["v_copied"], 1)
        act_attention1(act, at1)
        act_split_ctx(act, at1, (1,))
        act_layer_norm(act, 2, at1)
        act_layer_norm(act, 3)

    def dve_split_x(dve, turn, b):
        dve.wait_ge(ln["xT_hi_done"], B * turn + b + 1)
        sl = (slice(None), slice(None), slice(T * b, T * b + T))
        dve.tensor_tensor(xT_lo[sl], bank[:, xT_bank(turn, b), :].rearrange("p (k t) -> p k t", k=KD),
                          raw(xT_hi[sl]), ALU.subtract).then_inc(ln["xT_lo_done"], 1)

    def dve_binarise(dve):
        n_step = [0]

        def step(ins):
            n_step[0] += 1
            ins.then_inc(ff["step"], 1)
            dve.wait_ge(ff["step"], n_step[0])

        dve.wait_ge(ff["abs_done"], 2)
        step(dve.tensor_scalar(square_sum[:, 1, 0:2], square_sum[:, 0, 0:2], 1.0 / D, None, ALU.mult))
        step(dve.tensor_scalar(ffn_bw, ffn_w, 0.0, 2.0, ALU.is_ge, ALU.mult))
        for o in range(2):
            step(dve.tensor_scalar(ffn_bw[:, o, :], ffn_bw[:, o, :], 1.0, square_sum[:, 1, o:o + 1],
                                   ALU.subtract, ALU.mult))
        step(dve.tensor_tensor(ffn_bw, ffn_bw, ffn_w, ALU.subtract))
        step(dve.tensor_tensor(ffn_bw, ffn_bw, ffn_w, ALU.add))
        assert n_step[0] == FFN_STEPS

    def dve_split_ctx(dve, at, tiles):
        ctxT = ctxT0 if at["layer"] == 0 else ctxT1
        for t in tiles:
            c_hi, c_lo = ctx_parts(at["layer"], t)
            dve.wait_ge(at["ctx_hi_done"], t + 1)
            dve.tensor_tensor(c_lo, ctxT[:, :, t * P:t * P + P], raw(c_hi),
                              ALU.subtract).then_inc(at["ctx_lo_done"], 1)

    def split_wo_low(eng, at, quarter):
        n = (PAIRS if at["layer"] == 0 else H) // 4
        some = slice(n * quarter, n * quarter + n)
        eng.wait_ge(at["wo_hi_done"], quarter + 1)
        if at["layer"] == 1:
            eng.wait_ge(at["scores_done"], 4 * PAIRS)
        eng.tensor_tensor(wo_lo[:, some, :], wo_raw_of(at)[:, some, :], raw(wo_hi[:, some, :]),
                          ALU.subtract).then_inc(at["wo_lo_done"] if quarter < 2 else at["wo_lo_rest"], 1)

    def dve_layer_norm(dve, turn, y_of, at=None):
        for b in range(B):
            if at:
                dve_split_ctx(dve, at, [t for t in tiles_before(b) if t > 0])
            if turn == 2 and b == 1:
                dve_binarise(dve)
            if turn == 2 and b == 3:
                dve.wait_ge(ff["bw_hi"], 1)
                dve.tensor_tensor(w_lo[:, :, 0:D], bank[:, 7, :].rearrange("p (k o) -> p k o", k=KD),
                                  raw(w_hi[:, :, 0:D]), ALU.subtract).then_inc(ff["bw_lo"], 1)
            if turn >= 2:
                dve.wait_ge(ln["rows_added"], B * (turn - 2) + b + 1)
            two, done = slice(2 * b, 2 * b + 2), NT * turn + 2 * b + 2
            dve.wait_ge(ln["y_done"], done)
            dve.tensor_tensor(x_tok[:, two, :], y_of(b), x_tok[:, two, :], ALU.add).then_inc(ln["y_read"], 2)
            dve.wait_ge(ln["y_read"], done)
            for t in (2 * b, 2 * b + 1):
                dve.bn_stats(bn_out[:, t, :], x_tok[:, t, :]).then_inc(ln["stats"], 1)
            for t in (2 * b, 2 * b + 1):
                dve.wait_ge(ln["stats"], NT * turn + t + 1)
                dve.bn_aggr(moments[:, t, :], bn_out[:, t, :]).then_inc(ln["moments_ready"], 1)
            dve.wait_ge(ln["moments_ready"], done)
            dve.tensor_scalar(var_eps[:, 0, two], moments[:, two, 1], LN_EPS, None,
                              ALU.add).then_inc(ln["var_ready"], 1)

            if turn < 3 and b >= 1:
                dve_split_x(dve, turn + 1, b - 1)
            dve.wait_ge(ln["sqrt_done"], B * turn + b + 1)
            dve.reciprocal(inv_dev[:, 0, two], deviation[:, 0, two]).then_inc(ln["inv_ready"], 1)
            dve.wait_ge(ln["inv_ready"], B * turn + b + 1)
            for t in (2 * b, 2 * b + 1):
                dve.tensor_scalar(x_tok[:, t, :], x_tok[:, t, :], moments[:, t, 0:1], inv_dev[:, 0, t:t + 1],
                                  ALU.subtract, ALU.mult).then_inc(ln["x_new"], 1)
        if turn < 3:
            dve_split_x(dve, turn + 1, B - 1)

    def y_tiles(b):
        return bank[:, 2 * (b % 2):2 * (b % 2) + 2, 0:D]

    def split_w_low(eng, at, p):
        rows = KQ if at["layer"] == 0 else P
        eng.wait_ge(at["w_hi_done"], p + 1)
        eng.tensor_tensor(w_lo[0:rows, :, 0:2 * P], wq_full[0:rows, :, bass.ds(2 * P * p, 2 * P)],
                          raw(w_hi[0:rows, :, 0:2 * P]), ALU.subtract).then_inc(at["w_lo_done"], 1)

    def cos_rows(layer):
        return rope_cos[:, layer:layer + 1, :].broadcast_to([P, 2, T])

    def sin_rows(layer, r0):
        return rope_sin[r0:P, layer:layer + 1, :].broadcast_to([P - r0, 2, T])

    def dve_cos(dve, at, p, b):
        m = 4 * p + b
        if at["layer"] == 0:
            dve.wait_ge(at["q_done"], m + 1)
        else:
            dve.wait_ge(at["swap_done"], m + 1)
            if not (isinstance(p, int) and m < 2):
                dve.wait_ge(at["q_ready"], m - 1)
        dst = qT[:, :, T * b:T * b + T] if at["layer"] == 0 else pair_view(q_sum[:, b % 2, :])
        dve.tensor_tensor(dst, pair_view(bank[:, query_bank(p, b), :]), cos_rows(at["layer"]),
                          ALU.mult).then_inc(at["cos_done"], 1)

    def dve_rope_sum(dve, at, p, b):
        m = 4 * p + b
        dve.wait_ge(at["cos_done"], m + 1)
        dve.wait_ge(at["sin_done"], m + 1)
        dve.tensor_tensor(q_sum[:, b % 2, :], q_sum[:, b % 2, :], swapped[:, b % 2, :],
                          ALU.add).then_inc(at["q_summed"], 1)

    def dve_query_lo(dve, at, p, b):
        dve.wait_ge(at["q_hi_done"], 4 * p + b + 1)
        dve.tensor_tensor(q_lo[:, :, T * b:T * b + T], pair_view(q_sum[:, b % 2, :]),
                          raw(q_hi[:, :, T * b:T * b + T]), ALU.subtract).then_inc(at["q_ready"], 1)

    def dve_keys(dve, at, p, b):
        m = 4 * p + b
        keys = keysT[:, bass.ds(p // 2, 1), T * b:T * b + T].rearrange("p g n -> p (g n)")
        if not (isinstance(p, int) and m < 2):
            dve.wait_ge(at["scores_done"], m - 1)
        dve.tensor_copy(k_hi[:, b % 2, :], keys).then_inc(at["k_hi_done"], 1)
        dve.wait_ge(at["k_hi_done"], m + 1)
        dve.tensor_tensor(k_lo[:, b % 2, :], keys, raw(k_hi[:, b % 2, :]), ALU.subtract).then_inc(at["k_copied"], 1)

    def dve_attention0(dve, at):
        scale = (NOPE + ROPE) ** -0.5

        def normalise(m, par):
            dve.wait_ge(at["exp_done"], m + 1)
            dve.reciprocal(inv_sum[:, par, :], row_sum[:, par, :]).then_inc(at["inv_ready"], 1)
            dve.wait_ge(at["inv_ready"], m + 1)
            for h in range(2):
                for tile, c0, c1 in ((0, 0, T), (1, T, T + P)):
                    i = 2 * tile + h
                    ins = dve.tensor_scalar(probs[:, par, h, c0:c1], probs[:, par, h, c0:c1],
                                            inv_sum[:, par, i:i + 1], None, ALU.mult)
            ins.then_inc(at["probs_ready"], 1)

        def body(p, b, n, lag, own, more):
            par = b % 2
            if own:
                dve.wait_ge(at["scores_done"], n + 1)
                sc = scores_of(par)
                dve.tensor_reduce(row_max[:, par, 0:2], sc[:, :, 0:T], AX_X, ALU.max).then_inc(at["max_step"], 1)
                dve.tensor_reduce(row_max[:, par, 2:4], sc[:, :, T:T + P], AX_X, ALU.max).then_inc(at["max_step"], 1)
                dve.wait_ge(at["max_step"], 2 * n + 2)
                dve.tensor_scalar(neg_max[:, par, :], row_max[:, par, :], -scale, None,
                                  ALU.mult).then_inc(at["max_ready"], 1)
            if own and ahead(p, b, more):
                dve_cos(dve, at, *ahead(p, b, more))
            if own:
                normalise(n, par)
            if lag(2):
                p2, b2 = back(p, b, 2)
                dve.wait_ge(at["ctx_done"], n - 1)
                dve.tensor_copy(ctxT0[:, p2, T * b2:T * b2 + T], bank[:, CTX, 0:T]).then_inc(at["ctx_copied"], 1)
            if not own and b < 2:
                split_wo_low(dve, at, b)
            if not own and b == 2:
                dve_split_ctx(dve, at, (0,))

        steps(dve, body)

    def dve_attention1(dve, at):
        def body(p, b, n, lag, own, more):
            if own and (b < 3 or more):
                dve_keys(dve, at, *forward(p, b, 1))
            if own and (b < 2 or more):
                dve_query_lo(dve, at, *forward(p, b, 2))
            if own and ahead(p, b, more):
                dve_cos(dve, at, *ahead(p, b, more))
            if b == 0 and more:
                split_w_low(dve, at, p + 1)
            if lag(1):
                dve.wait_ge(at["ctx_done"], n)
                if lag(2):
                    dve.wait_ge(at["ctxT_done"], n - 1)
                inv = inv_sum[:, b % 2, :].rearrange("p (h t) -> p h t", h=2)
                dve.reciprocal(inv, ctx_banks[:, :, :, DV]).then_inc(at["inv_ready"], 1)
                dve.wait_ge(at["inv_ready"], n)
                dve.tensor_tensor(ctx_tok[:], ctx_banks[:, :, :, 0:DV],
                                  inv.unsqueeze(3).broadcast_to([P, 2, 2, DV]), ALU.mult).then_inc(at["ctx_norm"], 1)
            if own and ahead(p, b, more):
                dve_rope_sum(dve, at, *ahead(p, b, more))
            if own and not more and b == 3:
                split_wo_low(dve, at, 0)
                split_wo_low(dve, at, 1)
            if not own and b == 0:
                dve_split_ctx(dve, at, (0,))

        steps(dve, body)

    def dve_first_queries(dve, at):
        for b in range(B - 1):
            dve_cos(dve, at, 0, b)
            if at["layer"] == 1:
                dve_rope_sum(dve, at, 0, b)
                if b == 0:
                    dve_keys(dve, at, 0, 0)
                if b >= 1:
                    dve_query_lo(dve, at, 0, b - 1)

    @block.vector
    def _(dve):
        dve.wait_ge(su["wa_hi"], 1)
        dve.tensor_tensor(w_lo[:, :, 0:PROJ], wa_raw[:], raw(w_hi[:, :, 0:PROJ]),
                          ALU.subtract).then_inc(su["wa_lo"], 1)
        for b in range(B):
            dve_split_x(dve, 0, b)
        dve.wait_ge(ld["consts_in"], 16 * N_CONSTS)
        dve.wait_ge(su["sq_done"], 2 * NT)
        kr = bank[:, :, QL + KVL:PROJ].rearrange("p (b j) f -> p b j f", j=2)
        kp = key_part.rearrange("p (b j) f -> p b j f", j=2)
        kt = key_tok[:, :, KVL:P].rearrange("p (b j) f -> p b j f", j=2)

        def table(x, c0, c1):
            return x[:, :, c0:c1].unsqueeze(1).broadcast_to([P, B, 2, c1 - c0])

        half = ROPE // 2
        dve.tensor_tensor(kt, kr, table(key_cos, 0, ROPE), ALU.mult).then_inc(su["key_steps"], 1)
        dve.tensor_tensor(kp[:, :, :, 0:half], kr[:, :, :, half:ROPE], table(key_sin, 0, half),
                          ALU.mult).then_inc(su["key_steps"], 1)
        dve.tensor_tensor(kp[:, :, :, half:ROPE], kr[:, :, :, 0:half], table(key_sin, half, ROPE),
                          ALU.mult).then_inc(su["key_steps"], 1)
        dve.wait_ge(su["key_steps"], 3)
        dve.tensor_tensor(kt, kt, kp, ALU.add).then_inc(su["key_steps"], 1)
        dve.tensor_scalar(var_eps[:, 0, :], square_sum[:, 0, :], 1.0 / QL, RMS_EPS, ALU.mult,
                          ALU.add).then_inc(su["rms_var"], 1)
        dve.tensor_scalar(var_eps[:, 1, :], square_sum[:, 1, :], 1.0 / KVL, RMS_EPS, ALU.mult,
                          ALU.add).then_inc(su["rms_var"], 1)
        dve.wait_ge(su["rms_sqrt"], 1)
        dve.reciprocal(inv_dev[:], deviation[:]).then_inc(su["rms_inv"], 1)
        dve.wait_ge(su["rms_inv"], 1)
        for t in range(NT):
            src = bank[:, (t + 4) % NT, :]
            dve.scalar_tensor_tensor(out=qlat_tok[:, t, :], in0=src[:, 0:QL], scalar=inv_dev[:, 0, t:t + 1],
                                     in1=qn_rows[:], op0=ALU.mult, op1=ALU.mult).then_inc(su["latents"], 1)
            dve.scalar_tensor_tensor(out=key_tok[:, (t + 4) % NT, 0:KVL], in0=src[:, QL:QL + KVL],
                                     scalar=inv_dev[:, 1, t:t + 1], in1=kvn_rows[:], op0=ALU.mult,
                                     op1=ALU.mult).then_inc(su["latents"], 1)
        for b in range(B):
            dve.wait_ge(su["latT_hi_done"], b + 1)
            sl = (slice(0, KQ), slice(None), slice(T * b, T * b + T))
            dve.tensor_tensor(latT_lo[sl], bank[0:KQ, lat_bank(b), :].rearrange("p (k t) -> p k t", k=2),
                              raw(latT_hi[sl]), ALU.subtract).then_inc(su["latT_lo_done"], 1)
        for h in range(H):
            if h == 6:
                split_w_low(dve, at0, 0)
            dve.wait_ge(su["fold_done"], h + 1)
            dve.tensor_copy(wq_full[0:KQ, :, h * P:h * P + KVL],
                            bank[0:KQ, h % 2, 0:2 * KVL].rearrange("p (k f) -> p k f", k=2))\
               .then_inc(su["fold_q_copied"], 1)
            if h % 2:
                dve.tensor_copy(wo_full[:, h // 2, :], bank[:, 2 + (h // 2) % 2, 0:D])\
                   .then_inc(su["fold_o_copied"], 1)
        dve_first_queries(dve, at0)
        dve_attention0(dve, at0)
        dve.wait_ge(mo["gate_hi"], 1)
        dve.tensor_tensor(gate_lo[:, :, 0:E], bank[:, 4, 0:KD * E].rearrange("p (k e) -> p k e", k=KD),
                          raw(gate_hi[:, :, 0:E]), ALU.subtract).then_inc(mo["gate_lo"], 1)
        dve_layer_norm(dve, 0, y_tiles, at0)
        n_step = [0]

        def step(ins):
            n_step[0] += 1
            ins.then_inc(mo["step"], 1)
            dve.wait_ge(mo["step"], n_step[0])

        def wide(col):
            return best[:, col, :].unsqueeze(2).broadcast_to([P, NT, E])

        def gated(e, j):
            buf = (silu, weighted)[e]
            dve.wait_ge(mo["silu_done"], 2 * e + j + 1)
            dve.tensor_tensor(buf[:, j, :], buf[:, j, :], bank[:, 5 + 2 * j, :], ALU.mult).then_inc(mo["weighted"], 1)

        ranks = rank[:].unsqueeze(1).broadcast_to([P, NT, E])
        dve.wait_ge(ld["gate_in"], 32)
        dve.wait_ge(mo["p_done"], 1)
        p_psum = bank[:, 2, 0:NT * E].rearrange("p (t e) -> p t e", e=E)
        step(dve.tensor_reduce(best[:, 0, :], p_psum, AX_X, ALU.add))
        step(dve.reciprocal(best[:, 1, :], best[:, 0, :]))
        step(dve.tensor_tensor(p_tok[:], p_psum, wide(1), ALU.mult))
        for i in range(2):
            if i == 1:
                gated(0, 0)
            step(dve.tensor_reduce(best[:, 2 + i, :], p_tok[:], AX_X, ALU.max))
            step(dve.tensor_tensor(scratch[:], p_tok[:], wide(2 + i), ALU.is_equal))
            step(dve.tensor_tensor(scratch[:], scratch[:], ranks, ALU.mult))
            step(dve.tensor_reduce(best[:, 4, :], scratch[:], AX_X, ALU.max))
            step(dve.tensor_tensor(chosen[:, i, :, :], scratch[:], wide(4), ALU.is_equal))
            if i == 0:
                step(dve.scalar_tensor_tensor(out=p_tok[:], in0=chosen[:, 0, :, :], scalar=-2.0, in1=p_tok[:],
                                              op0=ALU.mult, op1=ALU.add))
        step(dve.tensor_tensor(best[:, 4, :], best[:, 2, :], best[:, 3, :], ALU.add))
        step(dve.reciprocal(best[:, 5, :], best[:, 4, :]))
        for i in range(2):
            step(dve.tensor_tensor(best[:, 2 + i, :], best[:, 2 + i, :], best[:, 5, :], ALU.mult))
            step(dve.tensor_tensor(chosen[:, i, :, :], chosen[:, i, :, :], wide(2 + i), ALU.mult))
        step(dve.tensor_tensor(chosen[:, 0, :, :], chosen[:, 0, :, :], chosen[:, 1, :, :], ALU.add))
        assert n_step[0] == ROUTE_STEPS

        def expert(e, par, i):
            dve.wait_ge(comb_in[par], 16 * i)
            for j in range(2):
                dve.wait_ge(mo["up_done"], 2 * e + j + 1)
                dve.tensor_tensor(weighted[:, j, :], bank[:, 5 + 2 * j, :], comb_rows[:, par, 512 * j:512 * j + 512],
                                  ALU.mult).then_inc(mo["weighted"], 1)
                dve.wait_ge(mo["silu_done"], 2 * e + j + 1)
                dve.wait_ge(mo["weighted"], 2 * e + j + 1)
                dve.tensor_tensor(silu[:, j, :], silu[:, j, :], weighted[:, j, :], ALU.mult).then_inc(mo["act"], 1)
            for j in range(2):
                low(e, par, j)

        def low(e, par, j):
            src = weighted if isinstance(e, int) and e == 1 else silu
            dve.wait_ge(mo["act_hi"], 2 * e + j + 1)
            if not isinstance(e, int):
                dve.wait_ge(mo["down_done"], e - 1)
            c = slice(512 * j, 512 * j + 512)
            dve.tensor_tensor(latT_lo[:, par, c], src[:, j, :], raw(latT_hi[:, par, c]),
                              ALU.subtract).then_inc(mo["act_lo"], 1)

        gated(0, 1)
        gated(1, 0)
        for e in range(2):
            if e == 1:
                gated(1, 1)
            dve.wait_ge(mo["comb_ready"], e + 1)
            for j in range(2):
                buf = (silu, weighted)[e]
                dve.wait_ge(mo["weighted"], 2 * e + j + 1)
                dve.tensor_tensor(buf[:, j, :], buf[:, j, :], bank[:, comb_bank(e, j), :],
                                  ALU.mult).then_inc(mo["act"], 1)
            for j in range(2):
                low(e, e, j)
        dve.wait_ge(mo["act_lo"], 4)
        with dve.Fori(1, E // 2) as i:
            for par in range(2):
                expert(2 * i + par, par, i)

        dve_layer_norm(dve, 1, lambda b: bank[:, b, :].rearrange("p (t n) -> p t n", t=2))

        for i in range(2 * G):
            j, g = i // G, i % G
            dst = pair_view(keysT[:, g, 512 * j:512 * j + 512])
            dve.wait_ge(kv["swap_done"], i + 1)
            dve.tensor_tensor(dst, pair_view(bank[:, i % 4, :]), cos_rows(1), ALU.mult).then_inc(kv["cos_done"], 1)
            dve.wait_ge(kv["sin_done"], i + 1)
            dve.wait_ge(kv["cos_done"], i + 1)
            dve.tensor_tensor(dst, dst, pair_view(swapped[:, i % 2, :]), ALU.add).then_inc(kv["k_ready"], 1)
        split_w_low(dve, at1, 0)
        dve_first_queries(dve, at1)
        dve_attention1(dve, at1)
        dve_layer_norm(dve, 2, y_tiles, at1)
        dve_layer_norm(dve, 3, y_tiles)

    def pool_sin(pool, at, p, b):
        m = 4 * p + b
        r0 = 64 if at["layer"] == 0 else 0
        pool.wait_ge(at["swap_done"], m + 1)
        sw = pair_view(swapped[r0:P, b % 2, :])
        pool.tensor_tensor(sw, sw, sin_rows(at["layer"], r0), ALU.mult).then_inc(at["sin_done"], 1)
        if at["layer"] == 0:
            q = qT[r0:P, :, T * b:T * b + T]
            pool.wait_ge(at["cos_done"], m + 1)
            pool.wait_ge(at["sin_done"], m + 1)
            pool.tensor_tensor(q, q, sw, ALU.add).then_inc(at["q_ready"], 1)

    def pool_attention(pool, at):
        def body(p, b, n, lag, own, more):
            if own and at["layer"] == 1:
                pr = keys_first(b % 2)
                first = pair_view(pr[:, 0:2 * T])[:, :, 0:P]
                pool.wait_ge(at["capped"], n + 1)
                pool.tensor_tensor(first, first, maskT[:].rearrange("p (h n) -> p h n", h=2), ALU.add)
                pool.tensor_tensor(pr[:, 2 * T:3 * T], pr[:, 2 * T:3 * T], maskT[:], ALU.add).then_inc(at["masked"], 1)
            if at["layer"] == 0 and b == 0 and more:
                pool.wait_ge(at["q_ready"], n + 3)
                split_w_low(pool, at, p + 1)
                pool.wait_ge(at["w_lo_done"], p + 2)
            if own and ahead(p, b, more):
                pool_sin(pool, at, *ahead(p, b, more))

        for b in range(B - 1):
            pool_sin(pool, at, 0, b)
        steps(pool, body)
        pool.wait_ge(at["q_ready"], 4 * PAIRS)
        for quarter in (2, 3):
            split_wo_low(pool, at, quarter)

    @block.gpsimd
    def _(pool):
        pool.dma_start(ident_bf[:], a["c_ident"]).then_inc(ld["bf_in"], 16)
        pool.dma_start(mask_bf[:], a["c_mask"]).then_inc(ld["bf_in"], 16)
        pool.dma_start(alibi_queries[:], a["c_alibi_queries"]).then_inc(ld["alibi_in"], 16)
        pool.dma_start(alibi_keys[:], a["c_alibi_keys"]).then_inc(ld["alibi_in"], 16)
        pool.wait_ge(ld["wqb_in"], 32)
        for k in range(2):
            src = wqb_raw[:, k, :].rearrange("p (h f) -> p h f", h=H)[:, :, NOPE:NOPE + ROPE]
            dst = wq_full[0:KQ, k, :].rearrange("p (h f) -> p h f", h=H)[:, :, KVL:P]
            pool.tensor_copy(dst, src).then_inc(su["rope_cols"], 1)
        pool.wait_ge(ld["consts_in"], 16 * N_CONSTS)
        pool.wait_ge(su["rope_cols"], 2)
        pool.wait_ge(su["fold_done"], H)
        pool.memset(raw(gate_hi[:]), 0.0).then_inc(mo["gate_zero"], 1)
        pool.memset(raw(gate_lo[:]), 0.0).then_inc(mo["gate_zero"], 1)
        pool.memset(zeros_bf[:], 0.0).then_inc(mo["zeros"], 1)
        pool.wait_ge(mo["gate_zero"], 2)
        pool.wait_ge(mo["zeros"], 1)
        pool_attention(pool, at0)
        def low(e, par):
            pool.wait_ge(mo["gu_hi"], e + 1)
            pool.tensor_tensor(w_lo[:, par, :], wgu_raw[:, par, :], raw(w_hi[:, par, :]),
                               ALU.subtract).then_inc(mo["gu_lo"], 1)
            pool.wait_ge(mo["dn_hi"], e + 1)
            pool.tensor_tensor(wdn_lo[:, par, :], wdn_raw[:, par, :], raw(wdn_hi[:, par, :]),
                               ALU.subtract).then_inc(mo["dn_lo"], 1)

        def order_queries(h):
            src = wq1_raw[:, :, bass.ds(h * DQ, DQ)].rearrange("p k (j e) -> p k e j", e=2)
            dst = wq_full[:, :, bass.ds(h * DQ, DQ)].rearrange("p k (e j) -> p k e j", e=2)
            for k in range(KD):
                ins = pool.tensor_copy(dst[:, k], src[:, k])
            ins.then_inc(kv["wq_perm"], 1)

        low(0, 0)
        low(1, 1)
        pool.wait_ge(ld["wq1_in"], 16)
        with pool.Fori(1, E // 2) as i:
            for par in range(2):
                low(2 * i + par, par)
                order_queries(2 * i + par)
        order_queries(0)
        order_queries(1)
        for k in range(KD):
            pool.wait_ge(kv["wk_hi"], k + 1)
            pool.tensor_tensor(perm_out(w_lo, k), perm_in(wk_raw, k, G), raw(perm_out(w_hi, k)),
                               ALU.subtract).then_inc(kv["wk_lo"], 1)
        pool.wait_ge(kv["wv_hi"], 1)
        pool.tensor_tensor(wv_lo, wv_raw[:], raw(wv_hi), ALU.subtract).then_inc(kv["wv_lo"], 1)
        pool.wait_ge(ln["y_done"], 2 * NT)
        pool.memset(v_tok[:, :, :, DV:DV + 1], 1.0).then_inc(kv["ones"], 1)
        for i in range(2 * G):
            pool.wait_ge(kv["swap_done"], i + 1)
            sw = pair_view(swapped[:, i % 2, :])
            pool.tensor_tensor(sw, sw, sin_rows(1, 0), ALU.mult).then_inc(kv["sin_done"], 1)
        pool_attention(pool, at1)

        def add_rows(turn, rows):
            for b in range(B):
                pool.wait_ge(ln["x_new"], NT * turn + 2 * b + 2)
                pool.wait_ge(ln["xT_done"], B * (turn + 1) + b + 1)
                xb = x_tok[:, 2 * b:2 * b + 2, :]
                pool.tensor_tensor(xb, xb, rows[:].unsqueeze(1).broadcast_to([P, 2, D]),
                                   ALU.add).then_inc(ln["rows_added"], 1)

        pool.wait_ge(ld["consts_in"], 16 * N_CONSTS)
        add_rows(1, bo_rows)
        add_rows(2, bias_rows)

    @block.sync
    def _(sp):
        sp.dma_start(ident[:], a["c_ident"]).then_inc(ld["ident_in"], 16)
        for b in range(B):
            sp.dma_start(x_tok[:, 2 * b:2 * b + 2, :], x_dram[:, 2 * b:2 * b + 2, :]).then_inc(x_in[b], 16)
            if b == 0:
                for name, c0, c1 in (("Wq_a", 0, QL), ("Wkv_a", QL, QL + KVL), ("Wk_rope", QL + KVL, PROJ)):
                    sp.dma_start(wa_raw[:, :, c0:c1],
                                 a[name].rearrange("(k p) n -> p k n", p=P)).then_inc(ld["wa_in"], 16)
        consts = [(maskT[:], a["c_maskT"]), (rope_cos[:], a["c_rope_cos"]), (rope_sin[:], a["c_rope_sin"]),
                  (key_cos[:], a["c_key_cos"]), (key_sin[:], a["c_key_sin"])]
        for dst, name in ((qn_rows, "q_norm_w"), (kvn_rows, "kv_norm_w"), (bo_rows, "bo"), (bias_rows, "ffn_bias")):
            consts.append((dst[:], a[name].partition_broadcast(P)))
        assert len(consts) == N_CONSTS
        for dst, src in consts:
            sp.dma_start(dst, src).then_inc(ld["consts_in"], 16)
        wqb = a["Wq_b"].rearrange("(k p) n -> p k n", p=KQ)
        for k in range(2):
            sp.dma_start(wqb_raw[:, k, :], wqb[:, k, :]).then_inc(ld["wqb_in"], 16)
        sp.dma_start(wkvb_raw[:], a["Wkv_b"]).then_inc(ld["wkvb_in"], 16)
        sp.dma_start(wo_raw[:], a["Wo0"].rearrange("(h p) n -> p h n", p=P)).then_inc(ld["wo0_in"], 16)
        sp.wait_ge(su["fold_done"], H)
        sp.wait_ge(su["rope_cols"], 2)
        sp.dma_start(gate_raw[:], a["gate_w"]).then_inc(ld["gate_in"], 16)
        sp.dma_start(rank[:], a["c_rank"]).then_inc(ld["gate_in"], 16)
        gate_up = a["gate_up"].rearrange("e (k p) f -> p e k f", p=P)
        down_w = a["down"].rearrange("e p n -> p e n")

        def load_expert(e, par):
            sp.dma_start(wgu_raw[:, par, :].rearrange("p (k f) -> p k f", k=KD),
                         gate_up[:, e, :, :]).then_inc(expert_in[par], 16)
            sp.dma_start(wdn_raw[:, par, :], down_w[:, e, :]).then_inc(expert_in[par], 16)

        load_expert(0, 0)
        load_expert(1, 1)
        sp.dma_start(wk_raw[:], a["Wk1"].rearrange("(k p) n -> p k n", p=P)).then_inc(ld["wkv1_in"], 16)
        sp.dma_start(wv_raw[:], a["Wv1"].rearrange("(k p) n -> p k n", p=P)).then_inc(ld["wkv1_in"], 16)
        sp.wait_ge(ln["y_done"], NT)
        sp.dma_start(wq1_raw[:], a["Wq1"].rearrange("(k p) n -> p k n", p=P)).then_inc(ld["wq1_in"], 16)
        sp.wait_ge(mo["combT_copied"], 1)
        sp.dma_start(comb_dram, p_rows[:]).then_inc(ld["comb_out"], 16)
        sp.wait_ge(ld["comb_out"], 16)
        with sp.Fori(1, E // 2) as i:
            for par in range(2):
                e = 2 * i + par
                sp.wait_ge(mo["gu_lo"], e - 1)
                sp.wait_ge(mo["dn_lo"], e - 1)
                sp.dma_start(wgu_raw[:, par, :].rearrange("p (k f) -> p k f", k=KD),
                             gate_up[:, bass.ds(e, 1), :, :].rearrange("p e k f -> p (e k) f"))\
                  .then_inc(expert_in[par], 16)
                sp.dma_start(wdn_raw[:, par, :],
                             down_w[:, bass.ds(e, 1), :].rearrange("p e n -> p (e n)")).then_inc(expert_in[par], 16)
                sp.wait_ge(mo["act"], 2 * e - 2)
                sp.dma_start(comb_rows[:, par, :],
                             comb_dram[bass.ds(e, 1), :].rearrange("e n -> (e n)").partition_broadcast(P))\
                  .then_inc(comb_in[par], 16)
        sp.wait_ge(at1["q_done"], 4 * PAIRS)
        sp.dma_start(wo1_raw[:], a["Wo1"].rearrange("(h p) n -> p h n", p=P)).then_inc(ld["wo1_in"], 16)
        sp.wait_ge(at1["ctx_done"], 4 * PAIRS)
        sp.dma_start(ffn_w, a["ffn_w"].rearrange("(o p) n -> p o n", p=P)).then_inc(ld["ffn_in"], 16)
        for b in range(B):
            sp.wait_ge(ln["x_new"], 3 * NT + 2 * b + 2)
            sp.dma_start(out_dram[:, 2 * b:2 * b + 2, :], x_tok[:, 2 * b:2 * b + 2, :]).then_inc(ld["stored"], 16)
        sp.wait_ge(ld["stored"], 16 * B)


_NAMES = dict(
    x="L0_attn_hidden_states", Wq_a="L0_attn_Wq_a", q_norm_w="L0_attn_q_norm_w", Wq_b="L0_attn_Wq_b",
    Wk_rope="L0_attn_Wk_rope", Wkv_a="L0_attn_Wkv_a", kv_norm_w="L0_attn_kv_norm_w", Wkv_b="L0_attn_Wkv_b",
    Wo0="L0_attn_Wo", gate_w="L0_ffn_gate_w", gate_up="L0_ffn_gate_up_proj", down="L0_ffn_down_proj",
    Wq1="L1_attn_Wq", Wk1="L1_attn_Wk", Wv1="L1_attn_Wv", Wo1="L1_attn_Wo", bo="L1_attn_bo",
    ffn_w="L1_ffn_weight", ffn_bias="L1_ffn_bias")


def kernel(**inputs):
    import concourse.bacc as bacc
    from concourse.bass_utils import run_bass_kernel_spmd

    nc = bacc.Bacc("TRN2", target_bir_lowering=False, num_devices=1)
    arrays = {f"in_{k}": np.ascontiguousarray(inputs[name]) for k, name in _NAMES.items()}
    arrays.update({f"in_{k}": v for k, v in shape_constants().items()})
    aps = {k[3:]: nc.dram_tensor(k, v.shape, mybir.dt.from_np(v.dtype), kind="ExternalInput").ap()
           for k, v in arrays.items()}
    out = nc.dram_tensor("out_0", (B, T, D), F32, kind="ExternalOutput").ap()
    program(nc, aps, out)
    return run_bass_kernel_spmd(nc, [arrays], core_ids=[0]).results[0]["out_0"]
```
